# Optimizing a Trainium2 kernel written in Bass

```python
import numpy as np
import jax
import jax.numpy as jnp

def _softmax(x, axis=-1):
    return jax.nn.softmax(x, axis=axis)

def _gelu(x):
    return jax.nn.gelu(x, approximate=True)

def _silu(x):
    return jax.nn.silu(x)

def _sigmoid(x):
    return jax.nn.sigmoid(x)

def _layernorm(x, axis=-1, eps=1e-05):
    m = jnp.mean(x, axis=axis, keepdims=True)
    v = jnp.var(x, axis=axis, keepdims=True)
    return (x - m) / jnp.sqrt(v + eps)

def _scatter_add(tgt, idx, src, axis=0):
    return tgt.at[idx].add(src)

def _segment_sum(src, seg, n):
    return jax.ops.segment_sum(src, seg, n)
kernel_name = 'mk_lm_tower_d1_tok_ids512_r4_fb1180'

def setup_inputs(seed: int=0):
    np.random.seed(seed)
    _w = jnp.asarray

    def _rec_inputs():
        import jax
        import jax.numpy as jnp
        _rk = jax.random.key(seed)
        x = jax.random.randint(jax.random.fold_in(_rk, 1), (64, 256), 0, 31993, jnp.int32)
        return x
    x = _rec_inputs()

    def _L0_tok_setup():
        import jax, jax.numpy as jnp
        import numpy as np
        V, D, L, F, H, NL = (8000, 128, 1024, 512, 8, 2)
        NB, NHASH, CS = (64, 4, 64)
        DH = D // H
        B, S = (2, 1024)

        def layer_norm(x, scale, bias):
            mu = jnp.mean(x, axis=-1, keepdims=True)
            var = jnp.var(x, axis=-1, keepdims=True)
            return (x - mu) * jax.lax.rsqrt(var + 1e-05) * scale + bias

        def lsh_attention(x, Wqk, Wv, Wo, rots):
            b, s, d = x.shape
            qk = (x @ Wqk).reshape(b, s, H, DH).transpose(0, 2, 1, 3)
            v = (x @ Wv).reshape(b, s, H, DH).transpose(0, 2, 1, 3)
            rot = jnp.einsum('bhsd,hrdk->bhrsk', qk, rots)
            buckets = jnp.argmax(jnp.concatenate([rot, -rot], -1), -1)
            order = jnp.argsort(buckets, axis=-1)
            inv = jnp.argsort(order, axis=-1)
            gather = lambda t: jnp.take_along_axis(jnp.broadcast_to(t[:, :, None], (b, H, NHASH, s, DH)), order[..., None], axis=3)
            sqk = gather(qk).reshape(b, H, NHASH, s // CS, CS, DH)
            sv = gather(v).reshape(b, H, NHASH, s // CS, CS, DH)
            k = sqk / (jnp.linalg.norm(sqk, axis=-1, keepdims=True) + 1e-06)
            kk = jnp.concatenate([k, jnp.roll(k, 1, axis=3)], axis=4)
            vv = jnp.concatenate([sv, jnp.roll(sv, 1, axis=3)], axis=4)
            scores = jnp.einsum('bhrcwd,bhrcud->bhrcwu', sqk, kk) / jnp.sqrt(jnp.float32(DH))
            attn = jax.nn.softmax(scores, axis=-1)
            out = jnp.einsum('bhrcwu,bhrcud->bhrcwd', attn, vv).reshape(b, H, NHASH, s, DH)
            out = jnp.take_along_axis(out, inv[..., None], axis=3).mean(axis=2)
            out = out.transpose(0, 2, 1, 3).reshape(b, s, d)
            return out @ Wo

        def ffn(x, W1, b1, W2, b2):
            return jax.nn.gelu(x @ W1 + b1) @ W2 + b2
        key = jax.random.key(seed)
        ks = jax.random.split(key, 16)
        sd = 0.02
        inp = {'x': jax.random.randint(ks[0], (B, S), 0, V), 'emb': jax.random.normal(ks[1], (V, D), jnp.float32) * sd, 'pos': jax.random.normal(ks[2], (1, L, D), jnp.float32) * sd, 'ln1_s': jnp.ones((NL, D), jnp.float32), 'ln1_b': jnp.zeros((NL, D), jnp.float32), 'Wqk': jax.random.normal(ks[3], (NL, D, D), jnp.float32) * sd, 'Wv': jax.random.normal(ks[4], (NL, D, D), jnp.float32) * sd, 'Wo': jax.random.normal(ks[5], (NL, D, D), jnp.float32) * sd, 'rots': jax.random.normal(ks[6], (NL, H, NHASH, DH, NB // 2), jnp.float32), 'ln2_s': jnp.ones((NL, D), jnp.float32), 'ln2_b': jnp.zeros((NL, D), jnp.float32), 'W1': jax.random.normal(ks[7], (NL, D, F), jnp.float32) * sd, 'b1': jnp.zeros((NL, F), jnp.float32), 'W2': jax.random.normal(ks[8], (NL, F, D), jnp.float32) * sd, 'b2': jnp.zeros((NL, D), jnp.float32)}
        return inp
    _L0_tok_all = _L0_tok_setup()
    _L0_tok_in = {k: v for k, v in _L0_tok_all.items() if k in ('emb', 'pos', 'ln1_s', 'ln1_b', 'Wqk', 'Wv', 'Wo', 'rots', 'ln2_s', 'ln2_b', 'W1', 'b1', 'W2', 'b2')}
    del _L0_tok_all

    def _L0_attn_setup():
        import jax, jax.numpy as jnp
        import numpy as np
        EPS = 1e-05
        NUM_HEADS = 8
        SCALE = 0.125

        def _lin_bn_relu(x, w, b, g, beta, mu, var):
            y = jnp.einsum('bnc,dc->bnd', x, w) + b
            y = (y - mu) * (g / jnp.sqrt(var + EPS)) + beta
            return jax.nn.relu(y)
        key = jax.random.key(seed)
        B, N, C = (8, 256, 128)
        keys = jax.random.split(key, 16)
        d = {'x': jax.random.normal(keys[0], (B, N, C), dtype=jnp.float32)}
        for i, p in enumerate(['q', 'k', 'v', 'p']):
            kw, kb, kmu = (keys[1 + 3 * i], keys[2 + 3 * i], keys[3 + 3 * i])
            d[f'{p}_w'] = jax.random.normal(kw, (C, C), dtype=jnp.float32) * 0.02
            d[f'{p}_b'] = jnp.zeros((C,), dtype=jnp.float32)
            d[f'{p}_g'] = jnp.ones((C,), dtype=jnp.float32)
            d[f'{p}_beta'] = jnp.zeros((C,), dtype=jnp.float32)
            d[f'{p}_mu'] = jax.random.normal(kmu, (C,), dtype=jnp.float32) * 0.02
            d[f'{p}_var'] = jax.random.uniform(kb, (C,), dtype=jnp.float32, minval=0.5, maxval=1.5)
        return d
    _L0_attn_all = _L0_attn_setup()
    _L0_attn_in = {k: v for k, v in _L0_attn_all.items() if k in ('q_w', 'q_b', 'q_g', 'q_beta', 'q_mu', 'q_var', 'k_w', 'k_b', 'k_g', 'k_beta', 'k_mu', 'k_var', 'v_w', 'v_b', 'v_g', 'v_beta', 'v_mu', 'v_var', 'p_w', 'p_b', 'p_g', 'p_beta', 'p_mu', 'p_var')}
    del _L0_attn_all

    def _L0_ffn_setup():
        import jax, jax.numpy as jnp
        import numpy as np
        import math
        D_MODEL = 128
        N_EXPERTS = 128
        TOP_K = 8
        N_HEADS = 8
        D_KEYS = 128
        HALF = D_KEYS // 2
        N_BATCH, T_SEQ = (2, 512)
        key = jax.random.key(seed)
        k1, k2, k3, k4, k5, k6 = jax.random.split(key, 6)
        queries = jax.random.normal(k1, (N_BATCH, T_SEQ, D_MODEL), dtype=jnp.float32)
        bound_q = 1.0 / math.sqrt(D_MODEL)
        Wq = jax.random.uniform(k2, (N_HEADS * D_KEYS, D_MODEL), minval=-bound_q, maxval=bound_q, dtype=jnp.float32)
        bq = jax.random.uniform(k3, (N_HEADS * D_KEYS,), minval=-bound_q, maxval=bound_q, dtype=jnp.float32)
        bound_k = 1.0 / math.sqrt(HALF)
        keys = jax.random.uniform(k4, (N_HEADS, 2, N_EXPERTS, HALF), minval=-bound_k, maxval=bound_k, dtype=jnp.float32)
        std = D_MODEL ** (-0.5)
        w_down_embed = std * jax.random.normal(k5, (N_EXPERTS * N_EXPERTS, D_MODEL), dtype=jnp.float32)
        w_up_embed = std * jax.random.normal(k6, (N_EXPERTS * N_EXPERTS, D_MODEL), dtype=jnp.float32)
        return {'queries': queries, 'Wq': Wq, 'bq': bq, 'keys': keys, 'w_down_embed': w_down_embed, 'w_up_embed': w_up_embed}
    _L0_ffn_all = _L0_ffn_setup()
    _L0_ffn_in = {k: v for k, v in _L0_ffn_all.items() if k in ('Wq', 'bq', 'keys', 'w_down_embed', 'w_up_embed')}
    del _L0_ffn_all
    return {'x': x, 'L0_tok_emb': _L0_tok_in['emb'], 'L0_tok_pos': _L0_tok_in['pos'], 'L0_tok_ln1_s': _L0_tok_in['ln1_s'], 'L0_tok_ln1_b': _L0_tok_in['ln1_b'], 'L0_tok_Wqk': _L0_tok_in['Wqk'], 'L0_tok_Wv': _L0_tok_in['Wv'], 'L0_tok_Wo': _L0_tok_in['Wo'], 'L0_tok_rots': _L0_tok_in['rots'], 'L0_tok_ln2_s': _L0_tok_in['ln2_s'], 'L0_tok_ln2_b': _L0_tok_in['ln2_b'], 'L0_tok_W1': _L0_tok_in['W1'], 'L0_tok_b1': _L0_tok_in['b1'], 'L0_tok_W2': _L0_tok_in['W2'], 'L0_tok_b2': _L0_tok_in['b2'], 'L0_attn_q_w': _L0_attn_in['q_w'], 'L0_attn_q_b': _L0_attn_in['q_b'], 'L0_attn_q_g': _L0_attn_in['q_g'], 'L0_attn_q_beta': _L0_attn_in['q_beta'], 'L0_attn_q_mu': _L0_attn_in['q_mu'], 'L0_attn_q_var': _L0_attn_in['q_var'], 'L0_attn_k_w': _L0_attn_in['k_w'], 'L0_attn_k_b': _L0_attn_in['k_b'], 'L0_attn_k_g': _L0_attn_in['k_g'], 'L0_attn_k_beta': _L0_attn_in['k_beta'], 'L0_attn_k_mu': _L0_attn_in['k_mu'], 'L0_attn_k_var': _L0_attn_in['k_var'], 'L0_attn_v_w': _L0_attn_in['v_w'], 'L0_attn_v_b': _L0_attn_in['v_b'], 'L0_attn_v_g': _L0_attn_in['v_g'], 'L0_attn_v_beta': _L0_attn_in['v_beta'], 'L0_attn_v_mu': _L0_attn_in['v_mu'], 'L0_attn_v_var': _L0_attn_in['v_var'], 'L0_attn_p_w': _L0_attn_in['p_w'], 'L0_attn_p_b': _L0_attn_in['p_b'], 'L0_attn_p_g': _L0_attn_in['p_g'], 'L0_attn_p_beta': _L0_attn_in['p_beta'], 'L0_attn_p_mu': _L0_attn_in['p_mu'], 'L0_attn_p_var': _L0_attn_in['p_var'], 'L0_ffn_Wq': _L0_ffn_in['Wq'], 'L0_ffn_bq': _L0_ffn_in['bq'], 'L0_ffn_keys': _L0_ffn_in['keys'], 'L0_ffn_w_down_embed': _L0_ffn_in['w_down_embed'], 'L0_ffn_w_up_embed': _L0_ffn_in['w_up_embed']}

def reference(x, L0_tok_emb, L0_tok_pos, L0_tok_ln1_s, L0_tok_ln1_b, L0_tok_Wqk, L0_tok_Wv, L0_tok_Wo, L0_tok_rots, L0_tok_ln2_s, L0_tok_ln2_b, L0_tok_W1, L0_tok_b1, L0_tok_W2, L0_tok_b2, L0_attn_q_w, L0_attn_q_b, L0_attn_q_g, L0_attn_q_beta, L0_attn_q_mu, L0_attn_q_var, L0_attn_k_w, L0_attn_k_b, L0_attn_k_g, L0_attn_k_beta, L0_attn_k_mu, L0_attn_k_var, L0_attn_v_w, L0_attn_v_b, L0_attn_v_g, L0_attn_v_beta, L0_attn_v_mu, L0_attn_v_var, L0_attn_p_w, L0_attn_p_b, L0_attn_p_g, L0_attn_p_beta, L0_attn_p_mu, L0_attn_p_var, L0_ffn_Wq, L0_ffn_bq, L0_ffn_keys, L0_ffn_w_down_embed, L0_ffn_w_up_embed):
    import jax
    import jax.numpy as jnp

    def _L0_tok_ref(x, emb, pos, ln1_s, ln1_b, Wqk, Wv, Wo, rots, ln2_s, ln2_b, W1, b1, W2, b2):
        import jax, jax.numpy as jnp
        import numpy as np
        V, D, L, F, H, NL = (8000, 128, 1024, 512, 8, 2)
        NB, NHASH, CS = (64, 4, 64)
        DH = D // H
        B, S = (2, 1024)

        def layer_norm(x, scale, bias):
            mu = jnp.mean(x, axis=-1, keepdims=True)
            var = jnp.var(x, axis=-1, keepdims=True)
            return (x - mu) * jax.lax.rsqrt(var + 1e-05) * scale + bias

        def lsh_attention(x, Wqk, Wv, Wo, rots):
            b, s, d = x.shape
            qk = (x @ Wqk).reshape(b, s, H, DH).transpose(0, 2, 1, 3)
            v = (x @ Wv).reshape(b, s, H, DH).transpose(0, 2, 1, 3)
            rot = jnp.einsum('bhsd,hrdk->bhrsk', qk, rots)
            buckets = jnp.argmax(jnp.concatenate([rot, -rot], -1), -1)
            order = jnp.argsort(buckets, axis=-1)
            inv = jnp.argsort(order, axis=-1)
            gather = lambda t: jnp.take_along_axis(jnp.broadcast_to(t[:, :, None], (b, H, NHASH, s, DH)), order[..., None], axis=3)
            sqk = gather(qk).reshape(b, H, NHASH, s // CS, CS, DH)
            sv = gather(v).reshape(b, H, NHASH, s // CS, CS, DH)
            k = sqk / (jnp.linalg.norm(sqk, axis=-1, keepdims=True) + 1e-06)
            kk = jnp.concatenate([k, jnp.roll(k, 1, axis=3)], axis=4)
            vv = jnp.concatenate([sv, jnp.roll(sv, 1, axis=3)], axis=4)
            scores = jnp.einsum('bhrcwd,bhrcud->bhrcwu', sqk, kk) / jnp.sqrt(jnp.float32(DH))
            attn = jax.nn.softmax(scores, axis=-1)
            out = jnp.einsum('bhrcwu,bhrcud->bhrcwd', attn, vv).reshape(b, H, NHASH, s, DH)
            out = jnp.take_along_axis(out, inv[..., None], axis=3).mean(axis=2)
            out = out.transpose(0, 2, 1, 3).reshape(b, s, d)
            return out @ Wo

        def ffn(x, W1, b1, W2, b2):
            return jax.nn.gelu(x @ W1 + b1) @ W2 + b2
        h = emb[x] + pos[:, :x.shape[1], :]
        x1, x2 = (h, jnp.zeros_like(h))
        for l in range(NL):
            y1 = x1 + lsh_attention(layer_norm(x2, ln1_s[l], ln1_b[l]), Wqk[l], Wv[l], Wo[l], rots[l])
            y2 = x2 + ffn(layer_norm(y1, ln2_s[l], ln2_b[l]), W1[l], b1[l], W2[l], b2[l])
            x1, x2 = (y1, y2)
        return (x1 + x2) / 2

    def _L0_attn_ref(x, q_w, q_b, q_g, q_beta, q_mu, q_var, k_w, k_b, k_g, k_beta, k_mu, k_var, v_w, v_b, v_g, v_beta, v_mu, v_var, p_w, p_b, p_g, p_beta, p_mu, p_var):
        import jax, jax.numpy as jnp
        import numpy as np
        EPS = 1e-05
        NUM_HEADS = 8
        SCALE = 0.125

        def _lin_bn_relu(x, w, b, g, beta, mu, var):
            y = jnp.einsum('bnc,dc->bnd', x, w) + b
            y = (y - mu) * (g / jnp.sqrt(var + EPS)) + beta
            return jax.nn.relu(y)
        B, N, C = x.shape
        H = NUM_HEADS
        dh = C // H

        def heads(t):
            return t.reshape(B, N, H, dh).transpose(0, 2, 1, 3)
        q = heads(_lin_bn_relu(x, q_w, q_b, q_g, q_beta, q_mu, q_var))
        k = heads(_lin_bn_relu(x, k_w, k_b, k_g, k_beta, k_mu, k_var))
        v = heads(_lin_bn_relu(x, v_w, v_b, v_g, v_beta, v_mu, v_var))
        attn = jnp.einsum('bhnd,bhmd->bhnm', q, k) * SCALE
        out = jnp.einsum('bhnm,bhmd->bhnd', attn, v)
        out = out.transpose(0, 2, 1, 3).reshape(B, N, C)
        out = jax.nn.relu(out)
        return _lin_bn_relu(out, p_w, p_b, p_g, p_beta, p_mu, p_var)

    def _L0_ffn_ref(queries, Wq, bq, keys, w_down_embed, w_up_embed):
        import jax, jax.numpy as jnp
        import numpy as np
        import math
        D_MODEL = 128
        N_EXPERTS = 128
        TOP_K = 8
        N_HEADS = 8
        D_KEYS = 128
        HALF = D_KEYS // 2
        N_BATCH, T_SEQ = (2, 512)
        N, T, D = queries.shape
        H, E, K = (N_HEADS, N_EXPERTS, TOP_K)
        q_tok = queries.reshape(-1, D)
        qh = q_tok @ Wq.T + bq
        qh = qh.reshape(-1, H, 2, HALF)
        sub_scores = jnp.einsum('nhcf,hcef->nhce', qh, keys)
        s, idx = jax.lax.top_k(sub_scores, K)
        all_scores = (s[:, :, 0, :, None] + s[:, :, 1, None, :]).reshape(-1, H, K * K)
        all_idx = (idx[:, :, 0, :, None] * E + idx[:, :, 1, None, :]).reshape(-1, H, K * K)
        best_s, best_pos = jax.lax.top_k(all_scores, K)
        indices = jnp.take_along_axis(all_idx, best_pos, axis=-1)
        w_down = w_down_embed[indices]
        w_up = w_up_embed[indices]
        x = jnp.einsum('nd,nhkd->nhk', q_tok, w_down)
        x = jax.nn.gelu(x)
        vals = x * jax.nn.softmax(best_s, axis=-1)
        out = jnp.einsum('nhk,nhkd->nd', vals, w_up)
        return out.reshape(N, T, D)
    h = _L0_tok_ref(x, L0_tok_emb, L0_tok_pos, L0_tok_ln1_s, L0_tok_ln1_b, L0_tok_Wqk, L0_tok_Wv, L0_tok_Wo, L0_tok_rots, L0_tok_ln2_s, L0_tok_ln2_b, L0_tok_W1, L0_tok_b1, L0_tok_W2, L0_tok_b2)
    h = h + _L0_attn_ref(_layernorm(h, axis=-1), L0_attn_q_w, L0_attn_q_b, L0_attn_q_g, L0_attn_q_beta, L0_attn_q_mu, L0_attn_q_var, L0_attn_k_w, L0_attn_k_b, L0_attn_k_g, L0_attn_k_beta, L0_attn_k_mu, L0_attn_k_var, L0_attn_v_w, L0_attn_v_b, L0_attn_v_g, L0_attn_v_beta, L0_attn_v_mu, L0_attn_v_var, L0_attn_p_w, L0_attn_p_b, L0_attn_p_g, L0_attn_p_beta, L0_attn_p_mu, L0_attn_p_var)
    h = h + _L0_ffn_ref(_layernorm(h, axis=-1), L0_ffn_Wq, L0_ffn_bq, L0_ffn_keys, L0_ffn_w_down_embed, L0_ffn_w_up_embed)
    return h

_drawn_inputs = setup_inputs


def setup_inputs(seed=0):
    import zlib

    import numpy as np

    out = dict(_drawn_inputs(seed))
    spreads = {'L0_tok_ln1_s': (1.0, 0.2),
     'L0_tok_ln1_b': (0.0, 0.1),
     'L0_tok_ln2_s': (1.0, 0.2),
     'L0_tok_ln2_b': (0.0, 0.1),
     'L0_tok_b1': (0.0, 0.1),
     'L0_tok_b2': (0.0, 0.1),
     'L0_attn_q_b': (0.0, 0.1),
     'L0_attn_q_g': (1.0, 0.2),
     'L0_attn_q_beta': (0.0, 0.1),
     'L0_attn_k_b': (0.0, 0.1),
     'L0_attn_k_g': (1.0, 0.2),
     'L0_attn_k_beta': (0.0, 0.1),
     'L0_attn_v_b': (0.0, 0.1),
     'L0_attn_v_g': (1.0, 0.2),
     'L0_attn_v_beta': (0.0, 0.1),
     'L0_attn_p_b': (0.0, 0.1),
     'L0_attn_p_g': (1.0, 0.2),
     'L0_attn_p_beta': (0.0, 0.1)}
    factors = {'L0_tok_Wqk': 37.11, 'L0_tok_rots': 43.308}
    for name, (base, spread) in spreads.items():
        noise = np.random.default_rng([zlib.crc32(name.encode()), seed]).standard_normal(out[name].shape)
        drawn = base * np.exp(spread * noise) if base else spread * noise
        out[name] = jnp.asarray(drawn.astype(out[name].dtype))
    for name, factor in factors.items():
        out[name] = (out[name] * factor).astype(out[name].dtype)
    return out
```

```python
from contextlib import ExitStack

import concourse.bass as bass
from concourse import mybir

ALU = mybir.AluOpType
ACT = mybir.ActivationFunctionType
AX_X = mybir.AxisListType.X
F32 = mybir.dt.float32
BF16 = mybir.dt.bfloat16
I32 = mybir.dt.int32
U32 = mybir.dt.uint32

P = 128
TILES = 2
SEQ = P * TILES
HEADS = 8
DH = P // HEADS
AUG = 32
HASHES = 4
ORDERS = HEADS * HASHES
ROTS = 32
CHUNKS = SEQ // 64
HID = 4
VC = DH + 1
MASKED = HASHES * CHUNKS * VC
TOPK = 8
CAND = 20
ROWS = HEADS * TOPK
EXPERTS = 128
GROUP = 16
GROUPS = TILES * ROWS // GROUP
RING = 4
KEY_BITS = 14
LN_EPS = 1e-5
ROOT_GUESS = float(0x5F3759DF)
GELU_CUBE = 0.044715
GELU_SCALE = 0.7978845608028654

LN1_S, LN1_B, LN2A_S, LN2A_B, LN2B_S, LN2B_B, LN1A_B = range(7)
B1 = 7
BN = B1 + 2 * HID
BQ = BN + 5 * 4
NVEC = BQ + HEADS
C_ID = 0
C_DIAG = C_ID + P
C_SUM = C_DIAG + P
C_CHUNK = C_SUM + ORDERS
C_CAND = C_CHUNK + CHUNKS
C_PRIO = C_CAND + CAND
C_POS = C_PRIO + ROTS
C_RANK = C_POS + TILES
NCONST = C_RANK + 1


class Signal:

    def __init__(self, nc, ctx, name, per):
        self.sem = ctx.enter_context(nc.semaphore(name))
        self.per = per

    def at(self, it, n):
        return it * self.per + n


def build(nc, ids, emb, pos, vecs, consts, b2, wqk, wv, wo, rots, w1, w2, wblk, wqT, keysT, table, out):
    batches = ids.shape[0] // TILES
    vocabulary = emb.shape[0]
    with ExitStack() as ctx:
        def sb(name, shape, dt=F32):
            return ctx.enter_context(nc.sbuf_tensor(name, shape, dt))

        def sem(name):
            return ctx.enter_context(nc.semaphore(name))

        def sig(name, per):
            return Signal(nc, ctx, name, per)

        cst = sb("cst", [P, NCONST])
        vec = sb("vec", [P, NVEC])
        ident = cst[:, C_ID:C_ID + P]
        ids_rows = sb("ids_rows", [P, P], I32)
        ids_col = sb("ids_col", [P, P], I32)
        pos_sb = sb("pos_sb", [P, TILES, P])
        b2_row = sb("b2_row", [1, 2 * P])
        b2_all = sb("b2_all", [P, 2, P])
        ones_row = sb("ones_row", [1, P])
        w_qkv = sb("w_qkv", [P, 2 * P])
        w_o1 = sb("w_o1", [P, P])
        w1_sb = sb("w1_sb", [P, 2, HID, P])
        w2_sb = sb("w2_sb", [P, 2, HID, P])
        rot_sb = sb("rot_sb", [P, 2, 4 * HASHES * ROTS])
        wblk_T = sb("wblk_T", [P, 4, P])
        bn_scale = sb("bn_scale", [P, 4])
        bn_tmp = sb("bn_tmp", [P, 4])
        bn_bias = sb("bn_bias", [P, 4])
        bias_row = sb("bias_row", [1, 3 * P])
        wq_sb = sb("wq_sb", [P, HEADS, P])
        key_sb = sb("key_sb", [P, HEADS, EXPERTS])
        prio = sb("prio", [P, ROTS], BF16)

        ids_now = sb("ids_now", [P, TILES], I32)
        emb_rows = sb("emb_rows", [P, TILES, P])
        y1 = sb("y1", [P, TILES, P])
        y2 = sb("y2", [P, TILES, P])
        half_sum = sb("half_sum", [P, TILES, P])
        stats = sb("stats", [P, TILES, 6])
        moments = sb("moments", [P, TILES, 2])
        variance = sb("variance", [P, TILES])
        rstd = sb("rstd", [P, TILES])
        root_tmp = sb("root_tmp", [P, TILES * HEADS])
        xhat = sb("xhat", [P, TILES, P])
        xT = sb("xT", [P, SEQ])
        hidT = sb("hidT", [P, HID, SEQ])
        q_aug = sb("q_aug", [P, TILES, HEADS, AUG])
        k_aug = sb("k_aug", [P, TILES, HEADS, AUG])
        v_one = sb("v_one", [P, TILES, HEADS, VC])
        q_sq = sb("q_sq", [P, TILES * HEADS, DH])
        norm2 = sb("norm2", [P, TILES * HEADS])
        norm = sb("norm", [P, TILES * HEADS])
        inv_norm = sb("inv_norm", [P, TILES * HEADS])
        qT = sb("qT", [P, 2, SEQ])
        kT = sb("kT", [P, 2, SEQ])
        rot_side = sb("rot_side", [P, TILES, ORDERS, ROTS], BF16)
        rot_abs = sb("rot_abs", [P, TILES, ORDERS, ROTS])
        rot_max = sb("rot_max", [P, ORDERS])
        rot_hit = sb("rot_hit", [P, ORDERS, ROTS], BF16)
        rot_won = sb("rot_won", [P, ORDERS, ROTS], BF16)
        bucket = sb("bucket", [P, ORDERS])
        sort_key = sb("sort_key", [P, TILES, 3, ORDERS])
        keys_rows = sb("keys_rows", [3 * ORDERS, SEQ])
        below = sb("below", [3 * ORDERS, SEQ])
        count = sb("count", [3 * ORDERS, 1])
        step_up = sb("step_up", [3 * ORDERS, 1])
        probe = sb("probe", [3 * ORDERS, 1])
        reached = sb("reached", [3 * ORDERS, SEQ])
        own = sb("own", [P, TILES, ORDERS, CHUNKS])
        seen = sb("seen", [P, TILES, ORDERS, CHUNKS])
        masked_v = sb("masked_v", [P, TILES, HEADS, HASHES * CHUNKS, VC])
        weights = sb("weights", [P, HEADS, TILES, SEQ])
        picked = sb("picked", [P, 2, HASHES * CHUNKS, VC])
        hashed = sb("hashed", [P, TILES, HEADS, HASHES, VC])
        inv_sum = sb("inv_sum", [P, TILES * ORDERS])
        hashed_n = sb("hashed_n", [P, TILES * ORDERS, DH])
        attended = sb("attended", [P, TILES, P])
        h = sb("h", [P, TILES, P])
        h2 = sb("h2", [P, TILES, P])
        bqT = sb("bqT", [P, SEQ])
        bkv = sb("bkv", [P, TILES, 2 * P])
        kv_diag = sb("kv_diag", [P, P])
        boT = sb("boT", [P, SEQ])
        z = sb("z", [P, TILES, P])
        query_T = sb("query_T", [P, 2, SEQ])
        half_s = sb("half_s", [P, TILES, HEADS, 2, TOPK])
        half_i = sb("half_i", [P, TILES, HEADS, 2, TOPK], U32)
        half_f = sb("half_f", [P, TILES * HEADS, 2, TOPK])
        pair_s = sb("pair_s", [P, TILES * HEADS, CAND])
        pair_i = sb("pair_i", [P, TILES * HEADS, CAND])
        best_s = sb("best_s", [P, TILES * HEADS, TOPK])
        best_p = sb("best_p", [P, TILES * HEADS, TOPK], U32)
        best_f = sb("best_f", [P, TILES * HEADS, TOPK])
        expert = sb("expert", [P, TILES, ROWS])
        shifted = sb("shifted", [P, TILES * HEADS, TOPK])
        exps = sb("exps", [P, TILES * HEADS, TOPK])
        exp_sum = sb("exp_sum", [P, TILES * HEADS])
        gate = sb("gate", [P, TILES * HEADS, TOPK])

        x_expert = sb("x_expert", [P, TILES, P])
        x_resid = sb("x_resid", [P, TILES, P])
        x_gate = sb("x_gate", [P, GROUPS, GROUP])
        x_index = sb("x_index", [P, TILES, ROWS], I32)
        ring = sb("ring", [P, RING, GROUP, 2, P])
        ids_f, ids_wrap, first_bias, first_value, w_v0, w_o0 = (ring[:, 0, n, 0, :] for n in range(6))
        wblk_rows, wblk_scaled = (ring[:, n, 0:2, :, :].rearrange("p a b d -> p (a b) d") for n in (1, 2))
        choice = masked_v[:, :, :, :, :].rearrange("p t h c v -> p (t h c v)")[:, 0:TILES * ROWS * CAND].rearrange("p (n c) -> p n c", c=CAND)
        product = rot_abs[:, :, :, :].rearrange("p t o k -> p (t o k)").rearrange("p (s d) -> p s d", s=GROUP)
        dot = sb("dot", [P, GROUP])
        dot2 = sb("dot2", [P, GROUP])
        cubed = sb("cubed", [P, GROUP])
        inner = sb("inner", [P, GROUP])
        bent = sb("bent", [P, GROUP])
        gelu2 = sb("gelu2", [P, GROUP])
        value = sb("value", [P, RING, GROUP])
        mix = sb("mix", [P, P])
        out_rows = sb("out_rows", [P, TILES, P])

        ps_mix = ctx.enter_context(nc.psum_tensor("ps_mix", [P, 4, P], F32))
        ps_tr = ctx.enter_context(nc.psum_tensor("ps_tr", [P, 512], F32))
        ps_wide = [ctx.enter_context(nc.psum_tensor(f"ps_wide{n}", [P, 1024], F32)) for n in range(2)]
        ps_pair = [ctx.enter_context(nc.psum_tensor(f"ps_pair{n}", [P, 512], F32)) for n in range(2)]

        def wide_bank(n):
            return ps_wide[n // 2 % 2][:, 512 * (n % 2):512 * (n % 2) + 512]

        def halves_bank(n, half):
            return ps_pair[half] if n % 2 else ps_wide[0][:, 512 * half:512 * half + 512]

        loaded = sem("loaded")
        zeroed = sem("zeroed")
        rots_loaded = sem("rots_loaded")
        ids_wrapped = sem("ids_wrapped")
        setup_scaled = sem("setup_scaled")
        setup_psum = sem("setup_psum")
        setup_read = sem("setup_read")

        ids_ready = sig("ids_ready", 1)
        emb_here = sig("emb_here", 16 * TILES)
        y1_made = sig("y1_made", 1)
        xhat_ready = sig("xhat_ready", 5)
        xT_in_psum = sig("xT_in_psum", 5)
        xT_ready = sig("xT_ready", 5)
        hid_in_psum = sig("hid_in_psum", 4)
        hid_ready = sig("hid_ready", 4)
        ffn_in_psum = sig("ffn_in_psum", 2)
        qkv_in_psum = sig("qkv_in_psum", 1)
        aug_ready = sig("aug_ready", 1)
        augT_in_psum = sig("augT_in_psum", 2)
        qT_ready = sig("qT_ready", 1)
        kT_ready = sig("kT_ready", 1)
        rot_in_psum = sig("rot_in_psum", TILES)
        side_taken = sig("side_taken", TILES)
        abs_taken = sig("abs_taken", TILES)
        sort_key_ready = sig("sort_key_ready", 1)
        sort_keyT_in_psum = sig("sort_keyT_in_psum", 1)
        reached_ready = sig("reached_ready", 1)
        chunk_in_psum = sig("chunk_in_psum", 1)
        scores_in_psum = sig("scores_in_psum", HEADS)
        weights_ready = sig("weights_ready", HEADS)
        masked_ready = sig("masked_ready", TILES)
        pv_in_psum = sig("pv_in_psum", HEADS * TILES)
        pv_taken = sig("pv_taken", HEADS * TILES)
        attended_ready = sig("attended_ready", 1)
        attendedT_in_psum = sig("attendedT_in_psum", 1)
        attendedT_ready = sig("attendedT_ready", 1)
        wo_in_psum = sig("wo_in_psum", 1)
        blk_q_in_psum = sig("blk_q_in_psum", 1)
        blk_kv_in_psum = sig("blk_kv_in_psum", TILES)
        blk_q_ready = sig("blk_q_ready", 1)
        blk_kv_ready = sig("blk_kv_ready", TILES)
        kv_in_psum = sig("kv_in_psum", 1)
        kv_diag_ready = sig("kv_diag_ready", 1)
        blk_o_in_psum = sig("blk_o_in_psum", 1)
        blk_o_ready = sig("blk_o_ready", 1)
        blk_p_in_psum = sig("blk_p_in_psum", 1)
        query_in_psum = sig("query_in_psum", HEADS)
        query_ready = sig("query_ready", HEADS)
        halves_in_psum = sig("halves_in_psum", HEADS)
        halves_taken = sig("halves_taken", HEADS)
        shifted_ready = sig("shifted_ready", 1)
        exps_ready = sig("exps_ready", 1)

        index_ready = [sig(f"index_ready{t}", 1) for t in range(TILES)]
        gathered = [sig(f"gathered{g}", 16 * GROUP) for g in range(GROUPS)]
        slots_free = sig("slots_free", GROUPS)
        inner_ready = sig("inner_ready", GROUPS)
        bent_ready = sig("bent_ready", GROUPS)
        value_ready = sig("value_ready", GROUPS)
        scaled = sig("scaled", GROUPS)
        mix_in_psum = sig("mix_in_psum", TILES)
        out_ready = sig("out_ready", TILES)
        stored = [sig(f"stored{t}", 16) for t in range(TILES)]
        pool_passed = sem("pool_passed")
        vector_passed = sem("vector_passed")

        block = ctx.enter_context(nc.Block())

        LOADS = 0

        @block.sync
        def _(sp):
            nonlocal LOADS

            def load(to, of):
                nonlocal LOADS
                sp.dma_start(to, of).then_inc(loaded, 16)
                LOADS += 1

            load(ids_rows[0:ids.shape[0], :], ids)
            load(cst[:, :], consts)
            load(vec[:, :], vecs)
            load(pos_sb[:, :, :], pos[0, 0:SEQ, :].rearrange("(t p) d -> p t d", p=P))
            load(b2_row[:, :], b2.rearrange("(a l) d -> a (l d)", a=1))
            load(w_qkv[:, 0:P], wqk[1])
            load(w_qkv[:, P:2 * P], wv[1])
            load(w_v0[:, :], wv[0])
            load(w_o0[:, :], wo[0])
            load(w_o1[:, :], wo[1])
            load(w1_sb[:, :, :, :], w1.rearrange("l d (c f) -> d l c f", f=P))
            load(w2_sb[:, :, :, :], w2.rearrange("l (c f) d -> f l c d", f=P))
            load(wblk_rows[:, :, :], wblk.rearrange("w o i -> o w i"))
            load(wq_sb[:, :, :], wqT.rearrange("d (h n) -> d h n", h=HEADS))
            load(key_sb[:, :, :], keysT.rearrange("f (h e) -> f h e", h=HEADS))
            sp.wait_ge(zeroed, 1)
            for n in range(HEADS):
                g = n % 4
                sp.dma_start(rot_sb[AUG * g:AUG * g + DH, n // 4, P * g:P * g + P].rearrange("d (r k) -> d r k", r=HASHES),
                             rots[1, n].rearrange("r d k -> d r k")).then_inc(rots_loaded, 16)
            for t in range(TILES):
                sp.sem_inc(stored[t].sem, 1)

            def store(it):
                for t in range(TILES):
                    sp.wait_ge(out_ready.sem, out_ready.at(it, t + 1))
                    sp.dma_start(out[bass.ds(it * SEQ + t * P, P), :], out_rows[:, t, :]).then_inc(stored[t].sem, 16)

            with sp.Fori(0, batches - 1) as i:
                store(i)
            store(batches - 1)
            for t in range(TILES):
                sp.wait_ge(stored[t].sem, 16 * batches + 1)

        @block.gpsimd
        def _(pool):
            pool.memset(rot_sb[:, :, :], 0.0).then_inc(zeroed, 1)
            pool.sem_inc(slots_free.sem, RING)

            def gather_embeddings(it):
                pool.wait_ge(ids_ready.sem, ids_ready.at(it, 1))
                pool.sem_inc(pool_passed, 1)
                for t in range(TILES):
                    pool.indirect_dma_start(
                        out=emb_rows[:, t, :], out_offset=None, in_=emb,
                        in_offset=bass.IndirectOffsetOnAxis(ap=ids_now[:, t:t + 1], axis=0)).then_inc(emb_here.sem, 16)

            def gather_experts(it):
                for g in range(GROUPS):
                    t, first = g // (GROUPS // TILES), g % (GROUPS // TILES) * GROUP
                    pool.wait_ge(index_ready[t].sem, index_ready[t].at(it, 1))
                    pool.sem_inc(pool_passed, 1)
                    pool.wait_ge(slots_free.sem, slots_free.at(it, g + 1))
                    pool.sem_inc(pool_passed, 1)
                    for s in range(GROUP):
                        pool.indirect_dma_start(
                            out=ring[:, g % RING, s, :, :].rearrange("p a d -> p (a d)"), out_offset=None, in_=table,
                            in_offset=bass.IndirectOffsetOnAxis(ap=x_index[:, t, first + s:first + s + 1], axis=0)
                        ).then_inc(gathered[g].sem, 16)

            gather_embeddings(0)
            with pool.Fori(0, batches - 1) as i:
                gather_embeddings(i + 1)
                gather_experts(i)
            gather_experts(batches - 1)

        @block.tensor
        def _(pe):
            pe.wait_ge(loaded, 16 * LOADS)
            pe.wait_ge(ids_wrapped, 1)
            pe.transpose(ps_tr[:, 0:P], ids_f[:, :], ident).then_inc(setup_psum, 1)
            pe.wait_ge(setup_scaled, 1)
            pe.matmul(ps_wide[0][:, 0:P], w_v0[:, :], first_bias[:, :], start=True, stop=True).then_inc(setup_psum, 1)
            pe.matmul(ps_wide[1][:, 0:2 * P], ones_row[:, :], b2_row[:, :], start=True, stop=True).then_inc(setup_psum, 1)
            for n in range(4):
                last = pe.transpose(ps_pair[0][:, n * P:(n + 1) * P], wblk_scaled[:, n, :], ident)
            last.then_inc(setup_psum, 1)
            for n in range(3):
                last = pe.transpose(ps_pair[1][0:1, n * P:(n + 1) * P], bn_bias[:, n + 1:n + 2], ident)
            last.then_inc(setup_psum, 1)
            pe.wait_ge(setup_read, 1)
            pe.matmul(ps_wide[0][:, 512:512 + P], first_value[:, :], w_o0[:, :], start=True, stop=True).then_inc(setup_psum, 1)

            def turn(it, n, source):
                pe.wait_ge(xhat_ready.sem, xhat_ready.at(it, n + 1))
                for t in range(TILES):
                    last = pe.transpose(ps_tr[:, t * P:(t + 1) * P], source[:, t, :], ident)
                last.then_inc(xT_in_psum.sem, 1)

            def feed_forward(it, layer, n):
                pe.wait_ge(xT_ready.sem, xT_ready.at(it, n + 1))
                for c in range(HID):
                    mm = pe.matmul(ps_wide[0][:, c * SEQ:(c + 1) * SEQ], w1_sb[:, layer, c, :], xT[:, :], start=True, stop=True)
                    if c % 2:
                        mm.then_inc(hid_in_psum.sem, 1)
                pe.wait_ge(hid_ready.sem, hid_ready.at(it, 2 * layer + 2))
                for t in range(TILES):
                    for c in range(HID):
                        mm = pe.matmul(ps_wide[1][:, t * P:(t + 1) * P], hidT[:, c, t * P:(t + 1) * P], w2_sb[:, layer, c, :],
                                       start=(c == 0), stop=(c == HID - 1))
                mm.then_inc(ffn_in_psum.sem, 1)

            def tower(stage, it):
                if stage == 0:
                    turn(it, 0, xhat)
                    feed_forward(it, 0, 0)
                elif stage == 1:
                    turn(it, 1, xhat)
                    pe.wait_ge(xT_ready.sem, xT_ready.at(it, 2))
                    for t in range(TILES):
                        mm = pe.matmul(ps_wide[1][:, t * 2 * P:(t + 1) * 2 * P], xT[:, t * P:(t + 1) * P], w_qkv[:, :],
                                       start=True, stop=True)
                    mm.then_inc(qkv_in_psum.sem, 1)
                    pe.wait_ge(aug_ready.sem, aug_ready.at(it, 1))
                    for bank, source in ((ps_pair[0], q_aug), (ps_pair[1], k_aug)):
                        for half in range(2):
                            for t in range(TILES):
                                last = pe.transpose(bank[:, half * SEQ + t * P:half * SEQ + (t + 1) * P],
                                                    source[:, t, 4 * half:4 * half + 4, :].rearrange("p h a -> p (h a)"), ident)
                        last.then_inc(augT_in_psum.sem, 1)
                    pe.wait_ge(qT_ready.sem, qT_ready.at(it, 1))
                    for t in range(TILES):
                        for half in range(2):
                            mm = pe.matmul(ps_wide[t][:, half * 512:half * 512 + 512], qT[:, half, t * P:(t + 1) * P],
                                           rot_sb[:, half, :], start=True, stop=True)
                        mm.then_inc(rot_in_psum.sem, 1)
                elif stage == 2:
                    pe.wait_ge(kT_ready.sem, kT_ready.at(it, 1))
                    for n in range(HEADS):
                        if n >= 2:
                            pe.wait_ge(weights_ready.sem, weights_ready.at(it, n - 1))
                        rows = slice(AUG * (n % 4), AUG * (n % 4) + AUG)
                        for t in range(TILES):
                            mm = pe.matmul(ps_pair[n % 2][:, t * SEQ:(t + 1) * SEQ], kT[rows, n // 4, t * P:(t + 1) * P],
                                           qT[rows, n // 4, :], start=True, stop=True)
                        mm.then_inc(scores_in_psum.sem, 1)
                    pe.wait_ge(sort_key_ready.sem, sort_key_ready.at(it, 1))
                    for t in range(TILES):
                        last = pe.transpose(ps_tr[0:3 * ORDERS, t * P:(t + 1) * P],
                                            sort_key[:, t, :, :].rearrange("p c o -> p (c o)"), ident)
                    last.then_inc(sort_keyT_in_psum.sem, 1)
                elif stage == 3:
                    pe.wait_ge(reached_ready.sem, reached_ready.at(it, 1))
                    for t in range(TILES):
                        mm = pe.matmul(ps_tr[:, t * ORDERS:(t + 1) * ORDERS], reached[:, t * P:(t + 1) * P],
                                       cst[0:3 * ORDERS, C_SUM:C_SUM + ORDERS], start=True, stop=True)
                    mm.then_inc(chunk_in_psum.sem, 1)
                elif stage == 4:
                    pe.wait_ge(masked_ready.sem, masked_ready.at(it, TILES))
                    pe.wait_ge(weights_ready.sem, weights_ready.at(it, HEADS))
                    for n in range(HEADS * TILES):
                        head, t = n // TILES, n % TILES
                        if n >= 4:
                            pe.wait_ge(pv_taken.sem, pv_taken.at(it, n - 3))
                        for kt in range(TILES):
                            mm = pe.matmul(wide_bank(n)[:, 0:MASKED], weights[:, head, kt, t * P:(t + 1) * P],
                                           masked_v[:, kt, head, :, :].rearrange("p c v -> p (c v)"),
                                           start=(kt == 0), stop=(kt == TILES - 1))
                        mm.then_inc(pv_in_psum.sem, 1)
                elif stage == 5:
                    pe.wait_ge(attended_ready.sem, attended_ready.at(it, 1))
                    for t in range(TILES):
                        last = pe.transpose(ps_tr[:, t * P:(t + 1) * P], attended[:, t, :], ident)
                    last.then_inc(attendedT_in_psum.sem, 1)
                    pe.wait_ge(attendedT_ready.sem, attendedT_ready.at(it, 1))
                    for t in range(TILES):
                        mm = pe.matmul(ps_wide[1][:, t * P:(t + 1) * P], xT[:, t * P:(t + 1) * P], w_o1[:, :], start=True, stop=True)
                    mm.then_inc(wo_in_psum.sem, 1)
                    turn(it, 2, xhat)
                    feed_forward(it, 1, 2)
                elif stage == 6:
                    turn(it, 3, xhat)
                    pe.wait_ge(xT_ready.sem, xT_ready.at(it, 4))
                    pe.matmul(ps_wide[1][:, 0:SEQ], wblk_T[:, 0, :], xT[:, :], start=True, stop=True).then_inc(blk_q_in_psum.sem, 1)
                    for t in range(TILES):
                        bank = ps_wide[0][:, t * 512:t * 512 + 2 * P]
                        pe.matmul(bank, xT[:, t * P:(t + 1) * P], wblk_T[:, 1:3, :].rearrange("p w c -> p (w c)"), start=True, stop=False)
                        pe.matmul(bank, ones_row[:, :], bias_row[:, 0:2 * P], start=False, stop=True).then_inc(blk_kv_in_psum.sem, 1)
                    pe.wait_ge(blk_kv_ready.sem, blk_kv_ready.at(it, TILES))
                    for t in range(TILES):
                        mm = pe.matmul(ps_wide[1][:, 512:512 + P], bkv[:, t, 0:P], bkv[:, t, P:2 * P], start=(t == 0), stop=(t == TILES - 1))
                    mm.then_inc(kv_in_psum.sem, 1)
                    pe.wait_ge(kv_diag_ready.sem, kv_diag_ready.at(it, 1))
                    pe.wait_ge(blk_q_ready.sem, blk_q_ready.at(it, 1))
                    pe.matmul(ps_pair[0][:, 0:SEQ], kv_diag[:, :], bqT[:, :], start=True, stop=True).then_inc(blk_o_in_psum.sem, 1)
                    pe.wait_ge(blk_o_ready.sem, blk_o_ready.at(it, 1))
                    for t in range(TILES):
                        pe.matmul(ps_pair[1][:, t * P:(t + 1) * P], boT[:, t * P:(t + 1) * P], wblk_T[:, 3, :], start=True, stop=False)
                        mm = pe.matmul(ps_pair[1][:, t * P:(t + 1) * P], ones_row[:, :], bias_row[:, 2 * P:3 * P], start=False, stop=True)
                    mm.then_inc(blk_p_in_psum.sem, 1)
                    turn(it, 4, z)
                elif stage == 7:
                    pe.wait_ge(xT_ready.sem, xT_ready.at(it, 5))

                    def query(n):
                        if n >= 2:
                            pe.wait_ge(query_ready.sem, query_ready.at(it, n - 1))
                        pe.matmul(ps_wide[1][:, n % 2 * 512:n % 2 * 512 + SEQ], wq_sb[:, n, :], xT[:, :],
                                  start=True, stop=True).then_inc(query_in_psum.sem, 1)

                    query(0)
                    for n in range(HEADS):
                        if n + 1 < HEADS:
                            query(n + 1)
                        pe.wait_ge(query_ready.sem, query_ready.at(it, n + 1))
                        if n >= 2:
                            pe.wait_ge(halves_taken.sem, halves_taken.at(it, n - 1))
                        for t in range(TILES):
                            for half in range(2):
                                rows = slice(64 * half, 64 * half + 64)
                                mm = pe.matmul(halves_bank(n, half)[:, t * EXPERTS:(t + 1) * EXPERTS], query_T[rows, n % 2, t * P:(t + 1) * P],
                                               key_sb[rows, n, :], start=True, stop=True)
                        mm.then_inc(halves_in_psum.sem, 1)

            def experts(g, it):
                t, first = g // (GROUPS // TILES), g % (GROUPS // TILES) == 0
                pe.wait_ge(scaled.sem, scaled.at(it, g + 1))
                for n in range(GROUP // 4):
                    mm = pe.matmul(ps_mix[:, :, :], ident, ring[:, g % RING, 4 * n:4 * n + 4, 1, :],
                                   start=(first and n == 0), stop=(g % (GROUPS // TILES) == GROUPS // TILES - 1 and n == GROUP // 4 - 1))
                mm.then_inc(slots_free.sem, 1)
                if g % (GROUPS // TILES) == GROUPS // TILES - 1:
                    pe.wait_ge(slots_free.sem, slots_free.at(it, g + 1) + RING)
                    pe.sem_inc(mix_in_psum.sem, 1)

            pe.wait_ge(setup_read, 5)
            pe.wait_ge(rots_loaded, 16 * HEADS)
            for stage in range(8):
                tower(stage, 0)
            with pe.Fori(0, batches - 1) as i:
                for g in range(GROUPS):
                    tower(g, i + 1)
                    if g:
                        experts(g - 1, i)
                experts(GROUPS - 1, i)
            for g in range(GROUPS):
                experts(g, batches - 1)

        @block.scalar
        def _(act):
            act.wait_ge(setup_psum, 2)
            act.activation(first_value[:, :], ps_wide[0][:, 0:P], ACT.Copy).then_inc(setup_read, 1)
            act.wait_ge(setup_psum, 3)
            act.activation(b2_all[:, :, :].rearrange("p l d -> p (l d)"), ps_wide[1][:, 0:2 * P], ACT.Copy).then_inc(setup_read, 1)
            act.wait_ge(setup_psum, 4)
            act.activation(wblk_T[:, :, :].rearrange("p w c -> p (w c)"), ps_pair[0][:, :], ACT.Copy).then_inc(setup_read, 1)
            act.wait_ge(setup_psum, 5)
            act.activation(bias_row[:, :], ps_pair[1][0:1, 0:3 * P], ACT.Copy).then_inc(setup_read, 1)

            def turned(it, n, scale=None, bias=None):
                act.wait_ge(xT_in_psum.sem, xT_in_psum.at(it, n + 1))
                if scale is None:
                    ins = act.activation(xT[:, :], ps_tr[:, 0:SEQ], ACT.Copy)
                else:
                    ins = act.activation(xT[:, :], ps_tr[:, 0:SEQ], ACT.Identity, bias=vec[:, bias:bias + 1], scale=vec[:, scale:scale + 1])
                ins.then_inc(xT_ready.sem, 1)

            def feed_forward(it, layer):
                for c in range(HID):
                    if c % 2 == 0:
                        act.wait_ge(hid_in_psum.sem, hid_in_psum.at(it, 2 * layer + c // 2 + 1))
                    ins = act.activation(hidT[:, c, :], ps_wide[0][:, c * SEQ:(c + 1) * SEQ], ACT.Gelu_apprx_tanh,
                                         bias=vec[:, B1 + HID * layer + c:B1 + HID * layer + c + 1])
                    if c % 2:
                        ins.then_inc(hid_ready.sem, 1)

            def tower(stage, it):
                if stage == 0:
                    turned(it, 0, LN2A_S, LN2A_B)
                    feed_forward(it, 0)
                elif stage == 1:
                    turned(it, 1, LN1_S, LN1_B)
                    act.wait_ge(augT_in_psum.sem, augT_in_psum.at(it, 1))
                    act.activation(qT[:, :, :].rearrange("p a s -> p (a s)"), ps_pair[0][:, :], ACT.Copy).then_inc(qT_ready.sem, 1)
                    act.wait_ge(augT_in_psum.sem, augT_in_psum.at(it, 2))
                    act.activation(kT[:, :, :].rearrange("p a s -> p (a s)"), ps_pair[1][:, :], ACT.Copy).then_inc(kT_ready.sem, 1)
                elif stage == 2:
                    for t in range(TILES):
                        act.wait_ge(side_taken.sem, side_taken.at(it, t + 1))
                        act.activation(rot_abs[:, t, :, :].rearrange("p o k -> p (o k)"), ps_wide[t][:, :], ACT.Abs).then_inc(abs_taken.sem, 1)
                    for n in range(HEADS):
                        act.wait_ge(scores_in_psum.sem, scores_in_psum.at(it, n + 1))
                        act.activation(weights[:, n, :, :].rearrange("p t s -> p (t s)"), ps_pair[n % 2][:, :], ACT.Exp).then_inc(weights_ready.sem, 1)
                elif stage == 5:
                    act.wait_ge(attendedT_in_psum.sem, attendedT_in_psum.at(it, 1))
                    act.activation(xT[:, :], ps_tr[:, 0:SEQ], ACT.Copy, scale=1.0 / HASHES).then_inc(attendedT_ready.sem, 1)
                    turned(it, 2, LN2B_S, LN2B_B)
                    feed_forward(it, 1)
                elif stage == 6:
                    turned(it, 3)
                    act.wait_ge(blk_q_in_psum.sem, blk_q_in_psum.at(it, 1))
                    act.activation(bqT[:, :], ps_wide[1][:, 0:SEQ], ACT.Relu, bias=bn_bias[:, 0:1]).then_inc(blk_q_ready.sem, 1)
                    for t in range(TILES):
                        act.wait_ge(blk_kv_in_psum.sem, blk_kv_in_psum.at(it, t + 1))
                        act.activation(bkv[:, t, :], ps_wide[0][:, t * 512:t * 512 + 2 * P], ACT.Relu).then_inc(blk_kv_ready.sem, 1)
                    act.wait_ge(blk_o_in_psum.sem, blk_o_in_psum.at(it, 1))
                    act.activation(boT[:, :], ps_pair[0][:, 0:SEQ], ACT.Relu).then_inc(blk_o_ready.sem, 1)
                    turned(it, 4)
                elif stage == 7:
                    for n in range(HEADS):
                        act.wait_ge(query_in_psum.sem, query_in_psum.at(it, n + 1))
                        if n >= 2:
                            act.wait_ge(halves_in_psum.sem, halves_in_psum.at(it, n - 1))
                        act.activation(query_T[:, n % 2, :], ps_wide[1][:, n % 2 * 512:n % 2 * 512 + SEQ], ACT.Identity,
                                       bias=vec[:, BQ + n:BQ + n + 1]).then_inc(query_ready.sem, 1)
                elif stage == 8:
                    act.wait_ge(shifted_ready.sem, shifted_ready.at(it, 1))
                    act.activation(exps[:, :, :].rearrange("p h k -> p (h k)"), shifted[:, :, :].rearrange("p h k -> p (h k)"),
                                   ACT.Exp).then_inc(exps_ready.sem, 1)

            def bend(g, it):
                act.wait_ge(inner_ready.sem, inner_ready.at(it, g + 1))
                act.activation(bent[:, :], inner[:, :], ACT.Tanh, scale=GELU_SCALE).then_inc(bent_ready.sem, 1)

            def scale_rows(g, it):
                act.wait_ge(value_ready.sem, value_ready.at(it, g + 1))
                for s in range(GROUP):
                    ins = act.activation(ring[:, g % RING, s, 1, :], ring[:, g % RING, s, 1, :], ACT.Copy,
                                         scale=value[:, g % RING, s:s + 1])
                ins.then_inc(scaled.sem, 1)

            act.wait_ge(loaded, 16 * LOADS)
            act.wait_ge(setup_scaled, 1)
            for stage in range(9):
                tower(stage, 0)
            with act.Fori(0, batches - 1) as i:
                for g in range(GROUPS):
                    if g:
                        scale_rows(g - 1, i)
                    tower(g, i + 1)
                    bend(g, i)
                scale_rows(GROUPS - 1, i)
                tower(8, i + 1)
            for g in range(GROUPS):
                bend(g, batches - 1)
                scale_rows(g, batches - 1)

        @block.vector
        def _(dve):
            def step(ins):
                dve.drain()
                return ins

            def inverse_root(y, x, xy):
                step(dve.tensor_scalar(y.bitcast(I32), x.bitcast(I32), -0.5, ROOT_GUESS, ALU.mult, ALU.add))
                for _ in range(3):
                    step(dve.tensor_tensor(xy, x, y, ALU.mult))
                    step(dve.scalar_tensor_tensor(xy, xy, -0.5, y, ALU.mult, ALU.mult))
                    step(dve.scalar_tensor_tensor(y, xy, 1.5, y, ALU.add, ALU.mult))

            dve.wait_ge(loaded, 16 * LOADS)
            n_ids = ids.shape[0]
            if n_ids < P:
                step(dve.memset(ids_f[:, :], 0.0))
            step(dve.tensor_copy(ids_f[0:n_ids, :], ids_rows[0:n_ids, :]))
            step(dve.tensor_scalar(ids_wrap[0:n_ids, :], ids_f[0:n_ids, :], 0.0, float(vocabulary), ALU.is_lt, ALU.mult))
            step(dve.tensor_tensor(ids_f[0:n_ids, :], ids_f[0:n_ids, :], ids_wrap[0:n_ids, :], ALU.add))
            dve.tensor_scalar(ids_f[0:n_ids, :], ids_f[0:n_ids, :], 0.0, float(vocabulary - 1), ALU.max, ALU.min).then_inc(ids_wrapped, 1)
            dve.memset(ones_row[:, :], 1.0)
            dve.memset(q_aug[:, :, :, :], 0.0)
            dve.memset(k_aug[:, :, :, :], 0.0)
            dve.memset(v_one[:, :, :, :], 1.0)
            dve.tensor_copy(prio[:, :], cst[:, C_PRIO:C_PRIO + ROTS])
            dve.tensor_copy(first_bias[:, :], vec[:, LN1A_B:LN1A_B + 1].to_broadcast([P, P]))
            bn = [vec[:, BN + 4 * n:BN + 4 * n + 4] for n in range(5)]
            step(dve.tensor_scalar(bn_bias[:, :], bn[4], LN_EPS, None, ALU.add))
            inverse_root(bn_scale[:, :], bn_bias[:, :], bn_tmp[:, :])
            step(dve.tensor_tensor(bn_scale[:, :], bn_scale[:, :], bn[1], ALU.mult))
            step(dve.tensor_tensor(bn_tmp[:, :], bn[0], bn[3], ALU.subtract))
            step(dve.tensor_tensor(bn_tmp[:, :], bn_tmp[:, :], bn_scale[:, :], ALU.mult))
            dve.tensor_tensor(bn_bias[:, :], bn_tmp[:, :], bn[2], ALU.add)
            dve.memset(k_aug[:, :, :, DH:DH + 1], 1.0)
            step(dve.tensor_tensor(wblk_scaled[:, :, :], wblk_rows[:, :, :], bn_scale[:, :].unsqueeze(2).to_broadcast([P, 4, P]), ALU.mult))
            dve.sem_inc(setup_scaled, 1)
            dve.wait_ge(setup_psum, 1)
            dve.tensor_copy(ids_col[:, :], ps_tr[:, 0:P])
            dve.wait_ge(setup_psum, 6)
            step(dve.tensor_tensor(pos_sb[:, :, :], pos_sb[:, :, :],
                                   ps_wide[0][:, 512:512 + P].unsqueeze(1).to_broadcast([P, TILES, P]), ALU.add))
            dve.sem_inc(setup_read, 1)

            def normalise(it, source, to):
                for t in range(TILES):
                    dve.bn_stats(stats[:, t, :], source[:, t, :])
                dve.drain()
                for t in range(TILES):
                    dve.bn_aggr(moments[:, t, :], stats[:, t, :])
                dve.drain()
                step(dve.tensor_scalar(variance[:, :], moments[:, :, 1], LN_EPS, None, ALU.add))
                inverse_root(rstd[:, :], variance[:, :], root_tmp[:, 0:TILES])
                for t in range(TILES):
                    ins = dve.tensor_scalar(to[:, t, :], source[:, t, :], moments[:, t, 0:1], rstd[:, t:t + 1], ALU.subtract, ALU.mult)
                ins.then_inc(xhat_ready.sem, 1)

            def psum_tokens(bank):
                return bank[:, 0:TILES * P].rearrange("p (t d) -> p t d", t=TILES)

            def tower(stage, it):
                if stage == 0:
                    dve.tensor_copy(ids_now[:, :], ids_col[:, bass.ds(it * TILES, TILES)]).then_inc(ids_ready.sem, 1)
                    dve.wait_ge(emb_here.sem, emb_here.at(it, 16 * TILES))
                    dve.tensor_tensor(y1[:, :, :], emb_rows[:, :, :], pos_sb[:, :, :], ALU.add).then_inc(y1_made.sem, 1)
                    dve.drain()
                    normalise(it, y1, xhat)
                    dve.wait_ge(ffn_in_psum.sem, ffn_in_psum.at(it, 1))
                    step(dve.tensor_tensor(y2[:, :, :], psum_tokens(ps_wide[1]), b2_all[:, 0:1, :].to_broadcast([P, TILES, P]), ALU.add))
                elif stage == 1:
                    normalise(it, y2, xhat)
                    dve.wait_ge(qkv_in_psum.sem, qkv_in_psum.at(it, 1))
                    qkv = ps_wide[1][:, :].rearrange("p (t w h d) -> p t w h d", t=2 * TILES, w=2, h=HEADS)
                    dve.tensor_copy(v_one[:, :, :, 0:DH], qkv[:, 0:TILES, 1, :, :])
                    step(dve.tensor_copy(q_aug[:, :, :, 0:DH], qkv[:, 0:TILES, 0, :, :]))
                    q = q_aug[:, :, :, 0:DH].rearrange("p t h d -> p (t h) d")
                    step(dve.tensor_tensor(q_sq[:, :, :], q, q, ALU.mult))
                    step(dve.tensor_reduce(norm2[:, :], q_sq[:, :, :], AX_X, ALU.add))
                    inverse_root(inv_norm[:, :], norm2[:, :], root_tmp[:, :])
                    step(dve.tensor_tensor(norm[:, :], norm2[:, :], inv_norm[:, :], ALU.mult))
                    step(dve.tensor_scalar(norm[:, :], norm[:, :], 1e-6, None, ALU.add))
                    step(dve.reciprocal(inv_norm[:, :], norm[:, :]))
                    step(dve.tensor_scalar(inv_norm[:, :], inv_norm[:, :], float(DH) ** -0.5, None, ALU.mult))
                    dve.scalar_tensor_tensor(q_aug[:, :, :, DH:DH + 1].rearrange("p t h d -> p (t h d)"), norm2[:, :], -1.0, inv_norm[:, :],
                                             ALU.mult, ALU.mult)
                    dve.tensor_tensor(k_aug[:, :, :, 0:DH].rearrange("p t h d -> p (t h) d"), q,
                                      inv_norm[:, :].unsqueeze(2).to_broadcast([P, TILES * HEADS, DH]), ALU.mult).then_inc(aug_ready.sem, 1)
                elif stage == 2:
                    for t in range(TILES):
                        dve.wait_ge(rot_in_psum.sem, rot_in_psum.at(it, t + 1))
                        for half in range(2):
                            o = slice(half * ORDERS // 2, (half + 1) * ORDERS // 2)
                            ins = dve.scalar_tensor_tensor(
                                rot_side[:, t, o, :], ps_wide[t][:, half * 512:half * 512 + 512].rearrange("p (o k) -> p o k", k=ROTS),
                                0.0, prio[:, :].unsqueeze(1).to_broadcast([P, ORDERS // 2, ROTS]), ALU.is_ge, ALU.add)
                        ins.then_inc(side_taken.sem, 1)
                    for t in range(TILES):
                        dve.wait_ge(abs_taken.sem, abs_taken.at(it, t + 1))
                        step(dve.tensor_reduce(rot_max[:, :], rot_abs[:, t, :, :], AX_X, ALU.max))
                        step(dve.tensor_tensor(rot_hit[:, :, :], rot_abs[:, t, :, :],
                                               rot_max[:, :].unsqueeze(2).to_broadcast([P, ORDERS, ROTS]), ALU.is_equal))
                        step(dve.tensor_tensor(rot_won[:, :, :].rearrange("p o k -> p (o k)"), rot_hit[:, :, :].rearrange("p o k -> p (o k)"),
                                               rot_side[:, t, :, :].rearrange("p o k -> p (o k)"), ALU.mult))
                        step(dve.tensor_reduce(bucket[:, :], rot_won[:, :, :], AX_X, ALU.max))
                        ins = dve.tensor_scalar(sort_key[:, t, :, :], bucket[:, :].unsqueeze(1).to_broadcast([P, 3, ORDERS]),
                                                float(-ROTS * SEQ), cst[:, C_POS + t:C_POS + t + 1], ALU.mult, ALU.add)
                    ins.then_inc(sort_key_ready.sem, 1)
                elif stage == 3:
                    dve.wait_ge(sort_keyT_in_psum.sem, sort_keyT_in_psum.at(it, 1))
                    dve.tensor_copy(keys_rows[:, :], ps_tr[0:3 * ORDERS, 0:SEQ])
                    step(dve.memset(probe[:, :], float(1 << (KEY_BITS - 1))))
                    for bit in range(KEY_BITS - 1, -1, -1):
                        step(dve.tensor_scalar(below[:, :], keys_rows[:, :], probe[:, 0:1], 0.0, ALU.is_lt, ALU.add, accum_out=count[:, :]))
                        step(dve.tensor_scalar(step_up[:, :], count[:, :], cst[0:3 * ORDERS, C_RANK:C_RANK + 1], float(1 << bit),
                                               ALU.is_le, ALU.mult))
                        down = float((1 << bit) - ((1 << bit) >> 1))
                        step(dve.scalar_tensor_tensor(probe[:, :], probe[:, :], -down, step_up[:, :], ALU.add, ALU.add))
                    dve.tensor_scalar(reached[:, :], keys_rows[:, :], probe[:, 0:1], None, ALU.is_ge).then_inc(reached_ready.sem, 1)
                elif stage == 4:
                    dve.wait_ge(chunk_in_psum.sem, chunk_in_psum.at(it, 1))
                    step(dve.tensor_tensor(own[:, :, :, :].rearrange("p t o c -> p (t o) c"),
                                           ps_tr[:, 0:TILES * ORDERS].unsqueeze(2).to_broadcast([P, TILES * ORDERS, CHUNKS]),
                                           cst[:, C_CHUNK:C_CHUNK + CHUNKS].unsqueeze(1).to_broadcast([P, TILES * ORDERS, CHUNKS]),
                                           ALU.is_equal))
                    dve.tensor_tensor(seen[:, :, :, 1:CHUNKS], own[:, :, :, 1:CHUNKS], own[:, :, :, 0:CHUNKS - 1], ALU.add)
                    step(dve.tensor_tensor(seen[:, :, :, 0:1], own[:, :, :, 0:1], own[:, :, :, CHUNKS - 1:CHUNKS], ALU.add))
                    for t in range(TILES):
                        dve.tensor_tensor(masked_v[:, t, :, :, :],
                                          v_one[:, t, :, :].unsqueeze(2).to_broadcast([P, HEADS, HASHES * CHUNKS, VC]),
                                          seen[:, t, :, :].rearrange("p (h r) c -> p h (r c)", h=HEADS).unsqueeze(3)
                                          .to_broadcast([P, HEADS, HASHES * CHUNKS, VC]), ALU.mult).then_inc(masked_ready.sem, 1)
                    for n in range(HEADS * TILES):
                        head, t = n // TILES, n % TILES
                        dve.wait_ge(pv_in_psum.sem, pv_in_psum.at(it, n + 1))
                        dve.tensor_tensor(picked[:, n % 2, :, :], wide_bank(n)[:, 0:MASKED].rearrange("p (c v) -> p c v", v=VC),
                                          own[:, t, HASHES * head:HASHES * (head + 1), :].rearrange("p r c -> p (r c)").unsqueeze(2)
                                          .to_broadcast([P, HASHES * CHUNKS, VC]), ALU.mult).then_inc(pv_taken.sem, 1)
                        dve.drain()
                        dve.tensor_reduce(hashed[:, t, head, :, :], picked[:, n % 2, :, :].rearrange("p (r c) v -> p r v c", r=HASHES),
                                          AX_X, ALU.add)
                    dve.drain()
                elif stage == 5:
                    every = hashed[:, :, :, :, :].rearrange("p t h r v -> p (t h r) v")
                    step(dve.reciprocal(inv_sum[:, :], every[:, :, DH]))
                    step(dve.tensor_tensor(hashed_n[:, :, :], every[:, :, 0:DH],
                                           inv_sum[:, :].unsqueeze(2).to_broadcast([P, TILES * ORDERS, DH]), ALU.mult))
                    dve.tensor_reduce(attended[:, :, :].rearrange("p t (h d) -> p (t h) d", h=HEADS),
                                      hashed_n[:, :, :].rearrange("p (n r) d -> p n d r", r=HASHES), AX_X, ALU.add
                                      ).then_inc(attended_ready.sem, 1)
                    dve.wait_ge(wo_in_psum.sem, wo_in_psum.at(it, 1))
                    step(dve.tensor_tensor(y1[:, :, :], psum_tokens(ps_wide[1]), y1[:, :, :], ALU.add))
                    normalise(it, y1, xhat)
                    step(dve.tensor_tensor(half_sum[:, :, :], y2[:, :, :], b2_all[:, 1:2, :].to_broadcast([P, TILES, P]), ALU.add))
                    step(dve.tensor_tensor(half_sum[:, :, :], half_sum[:, :, :], y1[:, :, :], ALU.add))
                    step(dve.tensor_scalar(half_sum[:, :, :], half_sum[:, :, :], 0.5, None, ALU.mult))
                    dve.wait_ge(ffn_in_psum.sem, ffn_in_psum.at(it, 2))
                    step(dve.scalar_tensor_tensor(h[:, :, :].rearrange("p t d -> p (t d)"), ps_wide[1][:, 0:TILES * P], 0.5,
                                                  half_sum[:, :, :].rearrange("p t d -> p (t d)"), ALU.mult, ALU.add))
                elif stage == 6:
                    normalise(it, h, xhat)
                    dve.wait_ge(kv_in_psum.sem, kv_in_psum.at(it, 1))
                    dve.tensor_tensor(kv_diag[:, :], ps_wide[1][:, 512:512 + P], cst[:, C_DIAG:C_DIAG + P], ALU.mult).then_inc(kv_diag_ready.sem, 1)
                    dve.wait_ge(blk_p_in_psum.sem, blk_p_in_psum.at(it, 1))
                    step(dve.scalar_tensor_tensor(h2[:, :, :].rearrange("p t d -> p (t d)"), ps_pair[1][:, 0:TILES * P], 0.0,
                                                  h[:, :, :].rearrange("p t d -> p (t d)"), ALU.max, ALU.add))
                    normalise(it, h2, z)
                elif stage == 7:
                    for n in range(HEADS):
                        dve.wait_ge(halves_in_psum.sem, halves_in_psum.at(it, n + 1))
                        dve.sem_inc(vector_passed, 1)
                        for t in range(TILES):
                            for half in range(2):
                                dve.max(half_s[:, t, n, half, :], halves_bank(n, half)[:, t * EXPERTS:(t + 1) * EXPERTS])
                        dve.drain()
                        for t in range(TILES):
                            for half in range(2):
                                ins = dve.max_index(half_i[:, t, n, half, :], half_s[:, t, n, half, :],
                                                    halves_bank(n, half)[:, t * EXPERTS:(t + 1) * EXPERTS])
                        ins.then_inc(halves_taken.sem, 1)
                    dve.drain()
                elif stage == 8:
                    step(dve.tensor_copy(half_f[:, :, :, :].rearrange("p n c k -> p (n c k)"),
                                         half_i[:, :, :, :, :].rearrange("p t n c k -> p (t n c k)")))
                    step(dve.tensor_scalar(half_f[:, :, 0, :], half_f[:, :, 0, :], float(EXPERTS), None, ALU.mult))
                    for pair, halves in ((pair_s, half_s[:, :, :, :, :].rearrange("p t n c k -> p (t n) c k")), (pair_i, half_f)):
                        a, b = halves[:, :, 0, :], halves[:, :, 1, :]
                        n = TILES * HEADS
                        dve.tensor_tensor(pair[:, :, 0:8], b[:, :, 0:8], a[:, :, 0:1].to_broadcast([P, n, 8]), ALU.add)
                        dve.tensor_tensor(pair[:, :, 8:12], b[:, :, 0:4], a[:, :, 1:2].to_broadcast([P, n, 4]), ALU.add)
                        dve.tensor_tensor(pair[:, :, 12:16].rearrange("p n (i j) -> p n i j", i=2),
                                          b[:, :, 0:2].unsqueeze(2).to_broadcast([P, n, 2, 2]),
                                          a[:, :, 2:4].unsqueeze(3).to_broadcast([P, n, 2, 2]), ALU.add)
                        dve.tensor_tensor(pair[:, :, 16:20], a[:, :, 4:8], b[:, :, 0:1].to_broadcast([P, n, 4]), ALU.add)
                    dve.drain()
                    for n in range(TILES * HEADS):
                        dve.max(best_s[:, n, :], pair_s[:, n, :])
                    dve.drain()
                    dve.tensor_tensor(shifted[:, :, :], best_s[:, :, :], best_s[:, :, 0:1].to_broadcast([P, TILES * HEADS, TOPK]),
                                      ALU.subtract).then_inc(shifted_ready.sem, 1)
                    for n in range(TILES * HEADS):
                        dve.max_index(best_p[:, n, :], best_s[:, n, :], pair_s[:, n, :])
                    dve.drain()
                    step(dve.tensor_copy(best_f[:, :, :].rearrange("p n k -> p (n k)"), best_p[:, :, :].rearrange("p n k -> p (n k)")))
                    step(dve.tensor_tensor(choice[:, :, :], best_f[:, :, :].rearrange("p n k -> p (n k)").unsqueeze(2).to_broadcast([P, TILES * ROWS, CAND]),
                                           cst[:, C_CAND:C_CAND + CAND].unsqueeze(1).to_broadcast([P, TILES * ROWS, CAND]), ALU.is_equal))
                    by_pair = choice[:, :, :].rearrange("p (n k) c -> p n k c", k=TOPK)
                    step(dve.tensor_tensor(by_pair, by_pair, pair_i[:, :, :].unsqueeze(2).to_broadcast([P, TILES * HEADS, TOPK, CAND]), ALU.mult))
                    step(dve.tensor_reduce(expert[:, :, :].rearrange("p t n -> p (t n)"), choice[:, :, :], AX_X, ALU.add))
                    dve.wait_ge(exps_ready.sem, exps_ready.at(it, 1))
                    step(dve.tensor_reduce(exp_sum[:, :], exps[:, :, :], AX_X, ALU.add))
                    step(dve.reciprocal(exp_sum[:, :], exp_sum[:, :]))
                    step(dve.tensor_tensor(gate[:, :, :], exps[:, :, :], exp_sum[:, :].unsqueeze(2).to_broadcast([P, TILES * HEADS, TOPK]), ALU.mult))
                    dve.tensor_copy(x_index[:, 0, :], expert[:, 0, :]).then_inc(index_ready[0].sem, 1)

            def hand_over(it):
                dve.drain()
                dve.tensor_copy(x_index[:, 1, :], expert[:, 1, :]).then_inc(index_ready[1].sem, 1)
                dve.tensor_copy(x_expert[:, :, :], z[:, :, :])
                dve.tensor_copy(x_resid[:, :, :], h2[:, :, :])
                dve.tensor_copy(x_gate[:, :, :].rearrange("p g s -> p (g s)"), gate[:, :, :].rearrange("p n k -> p (n k)"))
                dve.drain()

            def dots(g, it):
                t = g // (GROUPS // TILES)
                dve.wait_ge(gathered[g].sem, gathered[g].at(it, 16 * GROUP))
                step(dve.tensor_tensor(product[:, :, :], ring[:, g % RING, :, 0, :],
                                       x_expert[:, t:t + 1, :].to_broadcast([P, GROUP, P]), ALU.mult))
                step(dve.tensor_reduce(dot[:, :], product[:, :, :], AX_X, ALU.add))
                step(dve.tensor_tensor(dot2[:, :], dot[:, :], dot[:, :], ALU.mult))
                step(dve.tensor_scalar(cubed[:, :], dot2[:, :], GELU_CUBE, 1.0, ALU.mult, ALU.add))
                dve.tensor_tensor(inner[:, :], cubed[:, :], dot[:, :], ALU.mult).then_inc(inner_ready.sem, 1)

            def values(g, it):
                dve.wait_ge(bent_ready.sem, bent_ready.at(it, g + 1))
                step(dve.scalar_tensor_tensor(gelu2[:, :], bent[:, :], 1.0, dot[:, :], ALU.add, ALU.mult))
                dve.scalar_tensor_tensor(value[:, g % RING, :], gelu2[:, :], 0.5, x_gate[:, g, :], ALU.mult, ALU.mult).then_inc(value_ready.sem, 1)

            def finish(t, it):
                dve.wait_ge(mix_in_psum.sem, mix_in_psum.at(it, t + 1))
                step(dve.tensor_reduce(mix[:, :], ps_mix[:, :, :].rearrange("p n d -> p d n"), AX_X, ALU.add))
                dve.wait_ge(stored[t].sem, stored[t].at(it, 1))
                dve.tensor_tensor(out_rows[:, t, :], mix[:, :], x_resid[:, t, :], ALU.add).then_inc(out_ready.sem, 1)

            dve.wait_ge(setup_read, 5)
            for stage in range(9):
                tower(stage, 0)
            with dve.Fori(0, batches - 1) as i:
                hand_over(i)
                for g in range(GROUPS):
                    if g == GROUPS // TILES + 1:
                        finish(0, i)
                    if g:
                        values(g - 1, i)
                    tower(g, i + 1)
                    dots(g, i)
                values(GROUPS - 1, i)
                tower(8, i + 1)
                finish(1, i)
            hand_over(batches - 1)
            for g in range(GROUPS):
                if g == GROUPS // TILES:
                    finish(0, batches - 1)
                dots(g, batches - 1)
                values(g, batches - 1)
            finish(1, batches - 1)


def kernel(**inputs):
    import numpy as np
    import concourse.bacc as bacc
    from concourse import mybir as my
    from concourse.bass_utils import run_bass_kernel_spmd

    a = {k: np.asarray(v) for k, v in inputs.items()}
    t = {k[len("L0_tok_"):]: v for k, v in a.items() if k.startswith("L0_tok_")}
    b = {k[len("L0_attn_"):]: v for k, v in a.items() if k.startswith("L0_attn_")}
    f = {k[len("L0_ffn_"):]: v for k, v in a.items() if k.startswith("L0_ffn_")}
    sequences, length = a["x"].shape

    columns = [t["ln1_s"][1], t["ln1_b"][1], t["ln2_s"][0], t["ln2_b"][0], t["ln2_s"][1], t["ln2_b"][1], t["ln1_b"][0]]
    columns += list(t["b1"].reshape(2 * HID, P))
    columns += [b[f"{w}_{part}"] for part in ("b", "g", "beta", "mu", "var") for w in "qkvp"]
    columns += list(f["bq"].reshape(HEADS, P))

    const = np.zeros((P, NCONST), np.float32)
    const[:, C_ID:C_ID + P] = np.eye(P)
    const[:, C_DIAG:C_DIAG + P] = np.kron(np.eye(HEADS), np.full((DH, DH), 0.125))
    const[0:3 * ORDERS, C_SUM:C_SUM + ORDERS] = np.tile(np.eye(ORDERS), (3, 1))
    const[:, C_CHUNK:C_CHUNK + CHUNKS] = np.arange(CHUNKS)
    const[:, C_CAND:C_CAND + CAND] = np.arange(CAND)
    const[:, C_PRIO:C_PRIO + ROTS] = (ROTS - np.arange(ROTS)) / ROTS
    for tile in range(TILES):
        const[:, C_POS + tile] = 2 * ROTS * SEQ + tile * P + np.arange(P)
    const[0:3 * ORDERS, C_RANK] = 64 * (1 + np.arange(3 * ORDERS) // ORDERS)

    arrays = {
        "ids": a["x"].reshape(sequences * TILES, P),
        "emb": t["emb"],
        "pos": t["pos"],
        "vecs": np.stack(columns, axis=1),
        "consts": const,
        "b2": t["b2"], "wqk": t["Wqk"], "wv": t["Wv"], "wo": t["Wo"], "rots": t["rots"], "w1": t["W1"], "w2": t["W2"],
        "wblk": np.stack([b[f"{w}_w"] for w in "qkvp"]),
        "wqT": f["Wq"].T,
        "keysT": f["keys"].transpose(1, 3, 0, 2).reshape(P, HEADS * EXPERTS),
        "table": np.concatenate([f["w_down_embed"], f["w_up_embed"]], axis=1),
    }
    nc = bacc.Bacc("TRN2", target_bir_lowering=False, num_devices=1)
    arrays = {name: np.ascontiguousarray(v) for name, v in arrays.items()}
    args = [nc.dram_tensor(name, v.shape, my.dt.from_np(v.dtype), kind="ExternalInput").ap() for name, v in arrays.items()]
    out = nc.dram_tensor("out", (sequences * length, P), my.dt.float32, kind="ExternalOutput").ap()
    build(nc, *args, out)
    r = run_bass_kernel_spmd(nc, [arrays], core_ids=[0])
    return r.results[0]["out"].reshape(sequences, length, P)
```

```python
from contextlib import ExitStack

import concourse.bass as bass
from concourse import mybir

ALU = mybir.AluOpType
ACT = mybir.ActivationFunctionType
AX_X = mybir.AxisListType.X
F32 = mybir.dt.float32
BF16 = mybir.dt.bfloat16
I32 = mybir.dt.int32
U32 = mybir.dt.uint32

P = 128
TILES = 2
SEQ = P * TILES
HEADS = 8
DH = P // HEADS
AUG = 32
HASHES = 4
ORDERS = HEADS * HASHES
ROTS = 32
CHUNKS = SEQ // 64
HID = 4
VC = DH + 1
MASKED = HASHES * CHUNKS * VC
TOPK = 8
CAND = 20
ROWS = HEADS * TOPK
EXPERTS = 128
GROUP = 16
GROUPS = TILES * ROWS // GROUP
RING = 4
KEY_BITS = 14
LN_EPS = 1e-5
ROOT_GUESS = float(0x5F3759DF)
HALF_ROOT_GUESS = float(0x5F3759DF - (1 << 22) - (1 << 31))

LN1_S, LN1_B, LN2A_S, LN2A_B, LN2B_S, LN2B_B, LN1A_B = range(7)
B1 = 7
BN = B1 + 2 * HID
BQ = BN + 5 * 4
NVEC = BQ + HEADS
C_ID = 0
C_DIAG = C_ID + P
C_SUM = C_DIAG + P
C_CHUNK = C_SUM + ORDERS
C_CAND = C_CHUNK + CHUNKS
C_PRIO = C_CAND + CAND
C_POS = C_PRIO + ROTS
C_RANK = C_POS + TILES
NCONST = C_RANK + 1


class Signal:

    def __init__(self, nc, ctx, name, per):
        self.sem = ctx.enter_context(nc.semaphore(name))
        self.per = per

    def at(self, it, n):
        return it * self.per + n


def build(nc, ids, emb, pos, vecs, consts, b2, wqk, wv, wo, rots, w1, w2, wblk, wqT, keysT, table, out):
    batches = ids.shape[0] // TILES
    vocabulary = emb.shape[0]
    with ExitStack() as ctx:
        def sb(name, shape, dt=F32):
            return ctx.enter_context(nc.sbuf_tensor(name, shape, dt))

        def sem(name):
            return ctx.enter_context(nc.semaphore(name))

        def sig(name, per):
            return Signal(nc, ctx, name, per)

        cst = sb("cst", [P, NCONST])
        vec = sb("vec", [P, NVEC])
        ident = cst[:, C_ID:C_ID + P]
        ids_rows = sb("ids_rows", [P, P], I32)
        ids_col = sb("ids_col", [P, P], I32)
        pos_sb = sb("pos_sb", [P, TILES, P])
        b2_row = sb("b2_row", [1, 2 * P])
        b2_all = sb("b2_all", [P, 2, P])
        ones_row = sb("ones_row", [1, P])
        w_qkv = sb("w_qkv", [P, 2 * P])
        w_o1 = sb("w_o1", [P, P])
        w1_sb = sb("w1_sb", [P, 2, HID, P])
        w2_sb = sb("w2_sb", [P, 2, HID, P])
        rot_sb = sb("rot_sb", [P, 2, 4 * HASHES * ROTS])
        wblk_T = sb("wblk_T", [P, 4, P])
        bn_scale = sb("bn_scale", [P, 4])
        bn_tmp = sb("bn_tmp", [P, 4])
        bn_bias = sb("bn_bias", [P, 4])
        bias_row = sb("bias_row", [1, 3 * P])
        wq_sb = sb("wq_sb", [P, HEADS, P])
        key_sb = sb("key_sb", [P, HEADS, EXPERTS])
        prio = sb("prio", [P, ROTS], BF16)

        ids_now = sb("ids_now", [P, TILES], I32)
        emb_rows = sb("emb_rows", [P, TILES, P])
        y1 = sb("y1", [P, TILES, P])
        y2 = sb("y2", [P, TILES, P])
        half_sum = sb("half_sum", [P, TILES, P])
        stats = sb("stats", [P, TILES, 6])
        moments = sb("moments", [P, TILES, 2])
        variance = sb("variance", [P, TILES])
        rstd = sb("rstd", [P, TILES])
        root_tmp = sb("root_tmp", [P, TILES * HEADS])
        xhat = sb("xhat", [P, TILES, P])
        xT = sb("xT", [P, SEQ])
        hidT = sb("hidT", [P, HID, SEQ])
        q_aug = sb("q_aug", [P, TILES, HEADS, AUG])
        k_aug = sb("k_aug", [P, TILES, HEADS, AUG])
        v_one = sb("v_one", [P, TILES, HEADS, VC])
        q_sq = sb("q_sq", [P, TILES * HEADS, DH])
        norm2 = sb("norm2", [P, TILES * HEADS])
        norm = sb("norm", [P, TILES * HEADS])
        inv_norm = sb("inv_norm", [P, TILES * HEADS])
        qT = sb("qT", [P, 2, SEQ])
        kT = sb("kT", [P, 2, SEQ])
        rot_side = sb("rot_side", [P, TILES, ORDERS, ROTS], BF16)
        rot_abs = sb("rot_abs", [P, TILES, ORDERS, ROTS])
        rot_max = sb("rot_max", [P, ORDERS])
        rot_hit = sb("rot_hit", [P, ORDERS, ROTS], BF16)
        rot_won = sb("rot_won", [P, ORDERS, ROTS], BF16)
        bucket = sb("bucket", [P, ORDERS])
        sort_key = sb("sort_key", [P, TILES, 3, ORDERS])
        keys_rows = sb("keys_rows", [3 * ORDERS, SEQ])
        below = sb("below", [3 * ORDERS, SEQ])
        count = sb("count", [3 * ORDERS, 1])
        step_up = sb("step_up", [3 * ORDERS, 1])
        probe = sb("probe", [3 * ORDERS, 1])
        reached = sb("reached", [3 * ORDERS, SEQ])
        own = sb("own", [P, TILES, ORDERS, CHUNKS])
        seen = sb("seen", [P, TILES, ORDERS, CHUNKS])
        masked_v = sb("masked_v", [P, TILES, HEADS, HASHES * CHUNKS, VC])
        weights = sb("weights", [P, HEADS, TILES, SEQ])
        picked = sb("picked", [P, 2, HASHES * CHUNKS, VC])
        hashed = sb("hashed", [P, TILES, HEADS, HASHES, VC])
        inv_sum = sb("inv_sum", [P, TILES * ORDERS])
        hashed_n = sb("hashed_n", [P, TILES * ORDERS, DH])
        attended = sb("attended", [P, TILES, P])
        h = sb("h", [P, TILES, P])
        h2 = sb("h2", [P, TILES, P])
        bqT = sb("bqT", [P, SEQ])
        bkv = sb("bkv", [P, TILES, 2 * P])
        kv_diag = sb("kv_diag", [P, P])
        boT = sb("boT", [P, SEQ])
        z = sb("z", [P, TILES, P])
        query_T = sb("query_T", [P, 2, SEQ])
        half_s = sb("half_s", [P, TILES, HEADS, 2, TOPK])
        half_i = sb("half_i", [P, TILES, HEADS, 2, TOPK], U32)
        half_f = sb("half_f", [P, TILES * HEADS, 2, TOPK])
        pair_s = sb("pair_s", [P, TILES * HEADS, CAND])
        pair_i = sb("pair_i", [P, TILES * HEADS, CAND])
        best_s = sb("best_s", [P, TILES * HEADS, TOPK])
        best_p = sb("best_p", [P, TILES * HEADS, TOPK], U32)
        best_f = sb("best_f", [P, TILES * HEADS, TOPK])
        expert = sb("expert", [P, TILES, ROWS])
        shifted = sb("shifted", [P, TILES * HEADS, TOPK])
        exps = sb("exps", [P, TILES * HEADS, TOPK])
        exp_sum = sb("exp_sum", [P, TILES * HEADS])
        gate = sb("gate", [P, TILES * HEADS, TOPK])

        x_expert = sb("x_expert", [P, TILES, P])
        x_resid = sb("x_resid", [P, TILES, P])
        x_gate = sb("x_gate", [P, GROUPS, GROUP])
        x_index = sb("x_index", [P, TILES, ROWS], I32)
        ring = sb("ring", [P, RING, GROUP, 2, P])
        ids_f, ids_wrap, first_bias, first_value, w_v0, w_o0 = (ring[:, 0, n, 0, :] for n in range(6))
        wblk_rows, wblk_scaled = (ring[:, n, 0:2, :, :].rearrange("p a b d -> p (a b) d") for n in (1, 2))
        choice = masked_v[:, :, :, :, :].rearrange("p t h c v -> p (t h c v)")[:, 0:TILES * ROWS * CAND].rearrange("p (n c) -> p n c", c=CAND)
        dot = sb("dot", [P, GROUP])
        gelu = sb("gelu", [P, GROUP])
        value = sb("value", [P, RING, GROUP])
        mix = sb("mix", [P, P])
        out_rows = sb("out_rows", [P, TILES, P])

        ps_mix = ctx.enter_context(nc.psum_tensor("ps_mix", [P, 4, P], F32))
        ps_tr = ctx.enter_context(nc.psum_tensor("ps_tr", [P, 512], F32))
        ps_wide = [ctx.enter_context(nc.psum_tensor(f"ps_wide{n}", [P, 1024], F32)) for n in range(2)]
        ps_pair = [ctx.enter_context(nc.psum_tensor(f"ps_pair{n}", [P, 512], F32)) for n in range(2)]

        def wide_bank(n):
            return ps_wide[n // 2 % 2][:, 512 * (n % 2):512 * (n % 2) + 512]

        def halves_bank(n, half):
            return ps_pair[half] if n % 2 else ps_wide[0][:, 512 * half:512 * half + 512]

        loaded = sem("loaded")
        zeroed = sem("zeroed")
        rots_loaded = sem("rots_loaded")
        ids_wrapped = sem("ids_wrapped")
        setup_scaled = sem("setup_scaled")
        setup_psum = sem("setup_psum")
        setup_read = sem("setup_read")

        ids_ready = sig("ids_ready", 1)
        emb_here = sig("emb_here", 16 * TILES)
        y1_made = sig("y1_made", 1)
        xhat_ready = sig("xhat_ready", 5)
        xT_in_psum = sig("xT_in_psum", 5)
        xT_ready = sig("xT_ready", 5)
        hid_in_psum = sig("hid_in_psum", 4)
        hid_ready = sig("hid_ready", 4)
        ffn_in_psum = sig("ffn_in_psum", 2)
        qkv_in_psum = sig("qkv_in_psum", 1)
        aug_ready = sig("aug_ready", 1)
        augT_in_psum = sig("augT_in_psum", 2)
        qT_ready = sig("qT_ready", 1)
        kT_ready = sig("kT_ready", 1)
        rot_in_psum = sig("rot_in_psum", TILES)
        side_taken = sig("side_taken", TILES)
        abs_taken = sig("abs_taken", TILES)
        sort_key_ready = sig("sort_key_ready", 1)
        sort_keyT_in_psum = sig("sort_keyT_in_psum", 1)
        reached_ready = sig("reached_ready", 1)
        chunk_in_psum = sig("chunk_in_psum", 1)
        scores_in_psum = sig("scores_in_psum", HEADS)
        weights_ready = sig("weights_ready", HEADS)
        masked_ready = sig("masked_ready", TILES)
        pv_in_psum = sig("pv_in_psum", HEADS * TILES)
        pv_taken = sig("pv_taken", HEADS * TILES)
        attended_ready = sig("attended_ready", 1)
        attendedT_in_psum = sig("attendedT_in_psum", 1)
        attendedT_ready = sig("attendedT_ready", 1)
        wo_in_psum = sig("wo_in_psum", 1)
        blk_q_in_psum = sig("blk_q_in_psum", 1)
        blk_kv_in_psum = sig("blk_kv_in_psum", TILES)
        blk_q_ready = sig("blk_q_ready", 1)
        blk_kv_ready = sig("blk_kv_ready", TILES)
        kv_in_psum = sig("kv_in_psum", 1)
        kv_diag_ready = sig("kv_diag_ready", 1)
        blk_o_in_psum = sig("blk_o_in_psum", 1)
        blk_o_ready = sig("blk_o_ready", 1)
        blk_p_in_psum = sig("blk_p_in_psum", 1)
        query_in_psum = sig("query_in_psum", HEADS)
        query_ready = sig("query_ready", HEADS)
        halves_in_psum = sig("halves_in_psum", HEADS)
        halves_taken = sig("halves_taken", HEADS)
        shifted_ready = sig("shifted_ready", 1)
        exps_ready = sig("exps_ready", 1)

        index_ready = [sig(f"index_ready{t}", 1) for t in range(TILES)]
        gathered = [sig(f"gathered{g}", 16 * GROUP) for g in range(GROUPS)]
        slots_free = sig("slots_free", GROUPS)
        dots_ready = sig("dots_ready", GROUPS)
        gelu_ready = sig("gelu_ready", GROUPS)
        value_ready = sig("value_ready", GROUPS)
        scaled = sig("scaled", GROUPS)
        mix_in_psum = sig("mix_in_psum", TILES)
        out_ready = sig("out_ready", TILES)
        stored = [sig(f"stored{t}", 16) for t in range(TILES)]
        pool_passed = sem("pool_passed")
        vector_passed = sem("vector_passed")

        block = ctx.enter_context(nc.Block())

        LOADS = 0

        @block.sync
        def _(sp):
            nonlocal LOADS

            def load(to, of):
                nonlocal LOADS
                sp.dma_start(to, of).then_inc(loaded, 16)
                LOADS += 1

            load(ids_rows[0:ids.shape[0], :], ids)
            load(cst[:, :], consts)
            load(vec[:, :], vecs)
            load(pos_sb[:, :, :], pos[0, 0:SEQ, :].rearrange("(t p) d -> p t d", p=P))
            load(b2_row[:, :], b2.rearrange("(a l) d -> a (l d)", a=1))
            load(w_qkv[:, 0:P], wqk[1])
            load(w_qkv[:, P:2 * P], wv[1])
            load(w_v0[:, :], wv[0])
            load(w_o0[:, :], wo[0])
            load(w_o1[:, :], wo[1])
            load(w1_sb[:, :, :, :], w1.rearrange("l d (c f) -> d l c f", f=P))
            load(w2_sb[:, :, :, :], w2.rearrange("l (c f) d -> f l c d", f=P))
            load(wblk_rows[:, :, :], wblk.rearrange("w o i -> o w i"))
            load(wq_sb[:, :, :], wqT.rearrange("d (h n) -> d h n", h=HEADS))
            load(key_sb[:, :, :], keysT.rearrange("f (h e) -> f h e", h=HEADS))
            sp.wait_ge(zeroed, 1)
            for n in range(HEADS):
                g = n % 4
                sp.dma_start(rot_sb[AUG * g:AUG * g + DH, n // 4, P * g:P * g + P].rearrange("d (r k) -> d r k", r=HASHES),
                             rots[1, n].rearrange("r d k -> d r k")).then_inc(rots_loaded, 16)
            for t in range(TILES):
                sp.sem_inc(stored[t].sem, 1)

            def store(it):
                for t in range(TILES):
                    sp.wait_ge(out_ready.sem, out_ready.at(it, t + 1))
                    sp.dma_start(out[bass.ds(it * SEQ + t * P, P), :], out_rows[:, t, :]).then_inc(stored[t].sem, 16)

            with sp.Fori(0, batches - 1) as i:
                store(i)
            store(batches - 1)
            for t in range(TILES):
                sp.wait_ge(stored[t].sem, 16 * batches + 1)

        @block.gpsimd
        def _(pool):
            pool.memset(rot_sb[:, :, :], 0.0).then_inc(zeroed, 1)
            pool.sem_inc(slots_free.sem, RING)

            def gather_embeddings(it):
                pool.wait_ge(ids_ready.sem, ids_ready.at(it, 1))
                pool.sem_inc(pool_passed, 1)
                for t in range(TILES):
                    pool.indirect_dma_start(
                        out=emb_rows[:, t, :], out_offset=None, in_=emb,
                        in_offset=bass.IndirectOffsetOnAxis(ap=ids_now[:, t:t + 1], axis=0)).then_inc(emb_here.sem, 16)

            def gather_experts(it, groups):
                for g in groups:
                    t, first = g // (GROUPS // TILES), g % (GROUPS // TILES) * GROUP
                    pool.wait_ge(index_ready[t].sem, index_ready[t].at(it, 1))
                    pool.sem_inc(pool_passed, 1)
                    pool.wait_ge(slots_free.sem, slots_free.at(it, g + 1))
                    pool.sem_inc(pool_passed, 1)
                    for s in range(GROUP):
                        pool.indirect_dma_start(
                            out=ring[:, g % RING, s, :, :].rearrange("p a d -> p (a d)"), out_offset=None, in_=table,
                            in_offset=bass.IndirectOffsetOnAxis(ap=x_index[:, t, first + s:first + s + 1], axis=0)
                        ).then_inc(gathered[g].sem, 16)

            gather_embeddings(0)
            gather_embeddings(1)
            with pool.Fori(0, batches - 2) as i:
                gather_experts(i, range(0, 3))
                gather_embeddings(i + 2)
                gather_experts(i, range(3, GROUPS))
            gather_experts(batches - 2, range(GROUPS))
            gather_experts(batches - 1, range(GROUPS))

        @block.tensor
        def _(pe):
            pe.wait_ge(loaded, 16 * LOADS)
            pe.wait_ge(ids_wrapped, 1)
            pe.transpose(ps_tr[:, 0:P], ids_f[:, :], ident).then_inc(setup_psum, 1)
            pe.wait_ge(setup_scaled, 1)
            pe.matmul(ps_wide[0][:, 0:P], w_v0[:, :], first_bias[:, :], start=True, stop=True).then_inc(setup_psum, 1)
            pe.matmul(ps_wide[1][:, 0:2 * P], ones_row[:, :], b2_row[:, :], start=True, stop=True).then_inc(setup_psum, 1)
            for n in range(4):
                last = pe.transpose(ps_pair[0][:, n * P:(n + 1) * P], wblk_scaled[:, n, :], ident)
            last.then_inc(setup_psum, 1)
            for n in range(3):
                last = pe.transpose(ps_pair[1][0:1, n * P:(n + 1) * P], bn_bias[:, n + 1:n + 2], ident)
            last.then_inc(setup_psum, 1)
            pe.wait_ge(setup_read, 1)
            pe.matmul(ps_wide[0][:, 512:512 + P], first_value[:, :], w_o0[:, :], start=True, stop=True).then_inc(setup_psum, 1)

            def turn(it, n, source):
                pe.wait_ge(xhat_ready.sem, xhat_ready.at(it, n + 1))
                for t in range(TILES):
                    last = pe.transpose(ps_tr[:, t * P:(t + 1) * P], source[:, t, :], ident)
                last.then_inc(xT_in_psum.sem, 1)

            def feed_forward(it, layer, n):
                pe.wait_ge(xT_ready.sem, xT_ready.at(it, n + 1))
                for c in range(HID):
                    mm = pe.matmul(ps_wide[0][:, c * SEQ:(c + 1) * SEQ], w1_sb[:, layer, c, :], xT[:, :], start=True, stop=True)
                    if c % 2:
                        mm.then_inc(hid_in_psum.sem, 1)
                pe.wait_ge(hid_ready.sem, hid_ready.at(it, 2 * layer + 2))
                for t in range(TILES):
                    for c in range(HID):
                        mm = pe.matmul(ps_wide[1][:, t * P:(t + 1) * P], hidT[:, c, t * P:(t + 1) * P], w2_sb[:, layer, c, :],
                                       start=(c == 0), stop=(c == HID - 1))
                mm.then_inc(ffn_in_psum.sem, 1)

            def token_mix(it):
                turn(it, 0, xhat)
                feed_forward(it, 0, 0)

            def queries_keys(it):
                turn(it, 1, xhat)
                pe.wait_ge(xT_ready.sem, xT_ready.at(it, 2))
                for t in range(TILES):
                    mm = pe.matmul(ps_wide[1][:, t * 2 * P:(t + 1) * 2 * P], xT[:, t * P:(t + 1) * P], w_qkv[:, :],
                                   start=True, stop=True)
                mm.then_inc(qkv_in_psum.sem, 1)
                pe.wait_ge(aug_ready.sem, aug_ready.at(it, 1))
                for bank, source in ((ps_pair[0], q_aug), (ps_pair[1], k_aug)):
                    for half in range(2):
                        for t in range(TILES):
                            last = pe.transpose(bank[:, half * SEQ + t * P:half * SEQ + (t + 1) * P],
                                                source[:, t, 4 * half:4 * half + 4, :].rearrange("p h a -> p (h a)"), ident)
                    last.then_inc(augT_in_psum.sem, 1)
                pe.wait_ge(qT_ready.sem, qT_ready.at(it, 1))
                for t in range(TILES):
                    for half in range(2):
                        mm = pe.matmul(ps_wide[t][:, half * 512:half * 512 + 512], qT[:, half, t * P:(t + 1) * P],
                                       rot_sb[:, half, :], start=True, stop=True)
                    mm.then_inc(rot_in_psum.sem, 1)

            def scores(it, heads):
                pe.wait_ge(kT_ready.sem, kT_ready.at(it, 1))
                for n in heads:
                    if n >= 2:
                        pe.wait_ge(weights_ready.sem, weights_ready.at(it, n - 1))
                    rows = slice(AUG * (n % 4), AUG * (n % 4) + AUG)
                    for t in range(TILES):
                        mm = pe.matmul(ps_pair[n % 2][:, t * SEQ:(t + 1) * SEQ], kT[rows, n // 4, t * P:(t + 1) * P],
                                       qT[rows, n // 4, :], start=True, stop=True)
                    mm.then_inc(scores_in_psum.sem, 1)

            def turn_sort_keys(it):
                pe.wait_ge(sort_key_ready.sem, sort_key_ready.at(it, 1))
                for t in range(TILES):
                    last = pe.transpose(ps_tr[0:3 * ORDERS, t * P:(t + 1) * P],
                                        sort_key[:, t, :, :].rearrange("p c o -> p (c o)"), ident)
                last.then_inc(sort_keyT_in_psum.sem, 1)

            def chunks(it):
                pe.wait_ge(reached_ready.sem, reached_ready.at(it, 1))
                for t in range(TILES):
                    mm = pe.matmul(ps_tr[:, t * ORDERS:(t + 1) * ORDERS], reached[:, t * P:(t + 1) * P],
                                   cst[0:3 * ORDERS, C_SUM:C_SUM + ORDERS], start=True, stop=True)
                mm.then_inc(chunk_in_psum.sem, 1)

            def attend(it):
                pe.wait_ge(masked_ready.sem, masked_ready.at(it, TILES))
                pe.wait_ge(weights_ready.sem, weights_ready.at(it, HEADS))
                for n in range(HEADS * TILES):
                    head, t = n // TILES, n % TILES
                    if n >= 4:
                        pe.wait_ge(pv_taken.sem, pv_taken.at(it, n - 3))
                    for kt in range(TILES):
                        mm = pe.matmul(wide_bank(n)[:, 0:MASKED], weights[:, head, kt, t * P:(t + 1) * P],
                                       masked_v[:, kt, head, :, :].rearrange("p c v -> p (c v)"),
                                       start=(kt == 0), stop=(kt == TILES - 1))
                    mm.then_inc(pv_in_psum.sem, 1)

            def attention_out(it):
                pe.wait_ge(attended_ready.sem, attended_ready.at(it, 1))
                for t in range(TILES):
                    last = pe.transpose(ps_tr[:, t * P:(t + 1) * P], attended[:, t, :], ident)
                last.then_inc(attendedT_in_psum.sem, 1)
                pe.wait_ge(attendedT_ready.sem, attendedT_ready.at(it, 1))
                for t in range(TILES):
                    mm = pe.matmul(ps_wide[1][:, t * P:(t + 1) * P], xT[:, t * P:(t + 1) * P], w_o1[:, :], start=True, stop=True)
                mm.then_inc(wo_in_psum.sem, 1)

            def second_ffn(it):
                turn(it, 2, xhat)
                feed_forward(it, 1, 2)

            def linear_attention(it):
                turn(it, 3, xhat)
                pe.wait_ge(xT_ready.sem, xT_ready.at(it, 4))
                pe.matmul(ps_wide[1][:, 0:SEQ], wblk_T[:, 0, :], xT[:, :], start=True, stop=True).then_inc(blk_q_in_psum.sem, 1)
                for t in range(TILES):
                    bank = ps_wide[0][:, t * 512:t * 512 + 2 * P]
                    pe.matmul(bank, xT[:, t * P:(t + 1) * P], wblk_T[:, 1:3, :].rearrange("p w c -> p (w c)"), start=True, stop=False)
                    pe.matmul(bank, ones_row[:, :], bias_row[:, 0:2 * P], start=False, stop=True).then_inc(blk_kv_in_psum.sem, 1)
                pe.wait_ge(blk_kv_ready.sem, blk_kv_ready.at(it, TILES))
                for t in range(TILES):
                    mm = pe.matmul(ps_wide[1][:, 512:512 + P], bkv[:, t, 0:P], bkv[:, t, P:2 * P], start=(t == 0), stop=(t == TILES - 1))
                mm.then_inc(kv_in_psum.sem, 1)
                pe.wait_ge(kv_diag_ready.sem, kv_diag_ready.at(it, 1))
                pe.wait_ge(blk_q_ready.sem, blk_q_ready.at(it, 1))
                pe.matmul(ps_pair[0][:, 0:SEQ], kv_diag[:, :], bqT[:, :], start=True, stop=True).then_inc(blk_o_in_psum.sem, 1)
                pe.wait_ge(blk_o_ready.sem, blk_o_ready.at(it, 1))
                for t in range(TILES):
                    pe.matmul(ps_pair[1][:, t * P:(t + 1) * P], boT[:, t * P:(t + 1) * P], wblk_T[:, 3, :], start=True, stop=False)
                    mm = pe.matmul(ps_pair[1][:, t * P:(t + 1) * P], ones_row[:, :], bias_row[:, 2 * P:3 * P], start=False, stop=True)
                mm.then_inc(blk_p_in_psum.sem, 1)
                turn(it, 4, z)

            def halves(it):
                pe.wait_ge(xT_ready.sem, xT_ready.at(it, 5))

                def query(n):
                    if n >= 2:
                        pe.wait_ge(query_ready.sem, query_ready.at(it, n - 1))
                    pe.matmul(ps_wide[1][:, n % 2 * 512:n % 2 * 512 + SEQ], wq_sb[:, n, :], xT[:, :],
                              start=True, stop=True).then_inc(query_in_psum.sem, 1)

                query(0)
                query(1)
                for n in range(HEADS):
                    pe.wait_ge(query_ready.sem, query_ready.at(it, n + 1))
                    if n >= 2:
                        pe.wait_ge(halves_taken.sem, halves_taken.at(it, n - 1))
                    for t in range(TILES):
                        for half in range(2):
                            rows = slice(64 * half, 64 * half + 64)
                            mm = pe.matmul(halves_bank(n, half)[:, t * EXPERTS:(t + 1) * EXPERTS], query_T[rows, n % 2, t * P:(t + 1) * P],
                                           key_sb[rows, n, :], start=True, stop=True)
                    mm.then_inc(halves_in_psum.sem, 1)
                    if n + 2 < HEADS:
                        query(n + 2)

            def experts(g, it):
                t, first = g // (GROUPS // TILES), g % (GROUPS // TILES) == 0
                pe.wait_ge(scaled.sem, scaled.at(it, g + 1))
                for n in range(GROUP // 4):
                    mm = pe.matmul(ps_mix[:, :, :], ident, ring[:, g % RING, 4 * n:4 * n + 4, 1, :],
                                   start=(first and n == 0), stop=(g % (GROUPS // TILES) == GROUPS // TILES - 1 and n == GROUP // 4 - 1))
                mm.then_inc(slots_free.sem, 1)
                if g % (GROUPS // TILES) == GROUPS // TILES - 1:
                    pe.wait_ge(slots_free.sem, slots_free.at(it, g + 1) + RING)
                    pe.sem_inc(mix_in_psum.sem, 1)

            def head(it, tower=True):
                experts(0, it)
                if tower:
                    chunks(it + 1)
                experts(1, it)
                if tower:
                    attend(it + 1)
                    attention_out(it + 1)
                experts(2, it)
                if tower:
                    second_ffn(it + 1)
                experts(3, it)
                if tower:
                    linear_attention(it + 1)
                    halves(it + 1)
                for g in (4, 5, 6):
                    experts(g, it)

            def tail(it, tower=True, group7=True):
                if tower:
                    token_mix(it + 2)
                    queries_keys(it + 2)
                if group7:
                    experts(7, it)
                if tower:
                    scores(it + 2, range(0, HEADS // 2))
                    turn_sort_keys(it + 2)
                    scores(it + 2, range(HEADS // 2, HEADS))

            pe.wait_ge(setup_read, 5)
            pe.wait_ge(rots_loaded, 16 * HEADS)
            tail(-2, group7=False)
            chunks(0)
            attend(0)
            attention_out(0)
            second_ffn(0)
            linear_attention(0)
            halves(0)
            tail(-1, group7=False)
            with pe.Fori(0, batches - 2) as i:
                head(i)
                tail(i)
            head(batches - 2)
            tail(batches - 2, tower=False)
            head(batches - 1, tower=False)
            tail(batches - 1, tower=False)

        @block.scalar
        def _(act):
            act.wait_ge(setup_psum, 2)
            act.activation(first_value[:, :], ps_wide[0][:, 0:P], ACT.Copy).then_inc(setup_read, 1)
            act.wait_ge(setup_psum, 3)
            act.activation(b2_all[:, :, :].rearrange("p l d -> p (l d)"), ps_wide[1][:, 0:2 * P], ACT.Copy).then_inc(setup_read, 1)
            act.wait_ge(setup_psum, 4)
            act.activation(wblk_T[:, :, :].rearrange("p w c -> p (w c)"), ps_pair[0][:, :], ACT.Copy).then_inc(setup_read, 1)
            act.wait_ge(setup_psum, 5)
            act.activation(bias_row[:, :], ps_pair[1][0:1, 0:3 * P], ACT.Copy).then_inc(setup_read, 1)

            def turned(it, n, scale=None, bias=None):
                act.wait_ge(xT_in_psum.sem, xT_in_psum.at(it, n + 1))
                if scale is None:
                    ins = act.activation(xT[:, :], ps_tr[:, 0:SEQ], ACT.Copy)
                else:
                    ins = act.activation(xT[:, :], ps_tr[:, 0:SEQ], ACT.Identity, bias=vec[:, bias:bias + 1], scale=vec[:, scale:scale + 1])
                ins.then_inc(xT_ready.sem, 1)

            def feed_forward(it, layer):
                for c in range(HID):
                    if c % 2 == 0:
                        act.wait_ge(hid_in_psum.sem, hid_in_psum.at(it, 2 * layer + c // 2 + 1))
                    ins = act.activation(hidT[:, c, :], ps_wide[0][:, c * SEQ:(c + 1) * SEQ], ACT.Gelu_apprx_tanh,
                                         bias=vec[:, B1 + HID * layer + c:B1 + HID * layer + c + 1])
                    if c % 2:
                        ins.then_inc(hid_ready.sem, 1)

            def token_mix(it):
                turned(it, 0, LN2A_S, LN2A_B)
                feed_forward(it, 0)

            def normalised(it):
                turned(it, 1, LN1_S, LN1_B)

            def turned_heads(it):
                act.wait_ge(augT_in_psum.sem, augT_in_psum.at(it, 1))
                act.activation(qT[:, :, :].rearrange("p a s -> p (a s)"), ps_pair[0][:, :], ACT.Copy).then_inc(qT_ready.sem, 1)
                act.wait_ge(augT_in_psum.sem, augT_in_psum.at(it, 2))
                act.activation(kT[:, :, :].rearrange("p a s -> p (a s)"), ps_pair[1][:, :], ACT.Copy).then_inc(kT_ready.sem, 1)

            def magnitudes(it):
                for t in range(TILES):
                    act.wait_ge(side_taken.sem, side_taken.at(it, t + 1))
                    act.activation(rot_abs[:, t, :, :].rearrange("p o k -> p (o k)"), ps_wide[t][:, :], ACT.Abs).then_inc(abs_taken.sem, 1)

            def exponentials(it, heads):
                for n in heads:
                    act.wait_ge(scores_in_psum.sem, scores_in_psum.at(it, n + 1))
                    act.activation(weights[:, n, :, :].rearrange("p t s -> p (t s)"), ps_pair[n % 2][:, :], ACT.Exp).then_inc(weights_ready.sem, 1)

            def attention_out(it):
                act.wait_ge(attendedT_in_psum.sem, attendedT_in_psum.at(it, 1))
                act.activation(xT[:, :], ps_tr[:, 0:SEQ], ACT.Copy, scale=1.0 / HASHES).then_inc(attendedT_ready.sem, 1)

            def second_ffn(it):
                turned(it, 2, LN2B_S, LN2B_B)
                feed_forward(it, 1)

            def linear_attention(it):
                turned(it, 3)
                act.wait_ge(blk_q_in_psum.sem, blk_q_in_psum.at(it, 1))
                act.activation(bqT[:, :], ps_wide[1][:, 0:SEQ], ACT.Relu, bias=bn_bias[:, 0:1]).then_inc(blk_q_ready.sem, 1)
                for t in range(TILES):
                    act.wait_ge(blk_kv_in_psum.sem, blk_kv_in_psum.at(it, t + 1))
                    act.activation(bkv[:, t, :], ps_wide[0][:, t * 512:t * 512 + 2 * P], ACT.Relu).then_inc(blk_kv_ready.sem, 1)

            def linear_attention_out(it):
                act.wait_ge(blk_o_in_psum.sem, blk_o_in_psum.at(it, 1))
                act.activation(boT[:, :], ps_pair[0][:, 0:SEQ], ACT.Relu).then_inc(blk_o_ready.sem, 1)

            def queries(it, heads):
                for n in heads:
                    act.wait_ge(query_in_psum.sem, query_in_psum.at(it, n + 1))
                    if n >= 2:
                        act.wait_ge(halves_in_psum.sem, halves_in_psum.at(it, n - 1))
                    act.activation(query_T[:, n % 2, :], ps_wide[1][:, n % 2 * 512:n % 2 * 512 + SEQ], ACT.Identity,
                                   bias=vec[:, BQ + n:BQ + n + 1]).then_inc(query_ready.sem, 1)

            def softmax(it):
                act.wait_ge(shifted_ready.sem, shifted_ready.at(it, 1))
                act.activation(exps[:, :, :].rearrange("p h k -> p (h k)"), shifted[:, :, :].rearrange("p h k -> p (h k)"),
                               ACT.Exp).then_inc(exps_ready.sem, 1)

            def bend(g, it):
                act.wait_ge(dots_ready.sem, dots_ready.at(it, g + 1))
                act.activation(gelu[:, :], dot[:, :], ACT.Gelu_apprx_tanh).then_inc(gelu_ready.sem, 1)

            def scale_rows(g, it):
                act.wait_ge(value_ready.sem, value_ready.at(it, g + 1))
                for s in range(GROUP):
                    ins = act.activation(ring[:, g % RING, s, 1, :], ring[:, g % RING, s, 1, :], ACT.Copy,
                                         scale=value[:, g % RING, s:s + 1])
                ins.then_inc(scaled.sem, 1)

            def head(it, tower=True):
                if tower:
                    exponentials(it + 1, range(HEADS // 2, HEADS))
                bend(1, it)
                scale_rows(1, it)
                bend(2, it)
                scale_rows(2, it)
                if tower:
                    attention_out(it + 1)
                bend(3, it)
                scale_rows(3, it)
                if tower:
                    second_ffn(it + 1)
                bend(4, it)
                if tower:
                    linear_attention(it + 1)
                else:
                    scale_rows(4, it)
                bend(5, it)
                if tower:
                    linear_attention_out(it + 1)
                    scale_rows(4, it)
                    turned(it + 1, 4)
                    queries(it + 1, (0, 1))
                else:
                    scale_rows(5, it)
                bend(6, it)
                if tower:
                    queries(it + 1, range(2, HEADS))
                    scale_rows(5, it)
                scale_rows(6, it)
                if tower:
                    softmax(it + 1)

            def tail(it, tower=True, group7=True, group0=True):
                if tower:
                    token_mix(it + 2)
                if group7:
                    bend(7, it)
                if tower:
                    normalised(it + 2)
                if group7:
                    scale_rows(7, it)
                if tower:
                    turned_heads(it + 2)
                if group0:
                    bend(0, it + 1)
                if tower:
                    magnitudes(it + 2)
                    exponentials(it + 2, range(0, HEADS // 2))
                if group0:
                    scale_rows(0, it + 1)

            act.wait_ge(loaded, 16 * LOADS)
            act.wait_ge(setup_scaled, 1)
            tail(-2, group7=False, group0=False)
            exponentials(0, range(HEADS // 2, HEADS))
            attention_out(0)
            second_ffn(0)
            linear_attention(0)
            linear_attention_out(0)
            turned(0, 4)
            queries(0, range(HEADS))
            softmax(0)
            tail(-1, group7=False)
            with act.Fori(0, batches - 2) as i:
                head(i)
                tail(i)
            head(batches - 2)
            tail(batches - 2, tower=False)
            head(batches - 1, tower=False)
            tail(batches - 1, tower=False, group0=False)

        @block.vector
        def _(dve):
            def step(ins):
                dve.drain()
                return ins

            def inverse_root(y, x, xy):
                step(dve.tensor_scalar(y.bitcast(I32), x.bitcast(I32), -0.5, ROOT_GUESS, ALU.mult, ALU.add))
                for _ in range(3):
                    step(dve.tensor_tensor(xy, x, y, ALU.mult))
                    step(dve.scalar_tensor_tensor(xy, xy, -0.5, y, ALU.mult, ALU.mult))
                    step(dve.scalar_tensor_tensor(y, xy, 1.5, y, ALU.add, ALU.mult))

            dve.wait_ge(loaded, 16 * LOADS)
            n_ids = ids.shape[0]
            if n_ids < P:
                step(dve.memset(ids_f[:, :], 0.0))
            step(dve.tensor_copy(ids_f[0:n_ids, :], ids_rows[0:n_ids, :]))
            step(dve.tensor_scalar(ids_wrap[0:n_ids, :], ids_f[0:n_ids, :], 0.0, float(vocabulary), ALU.is_lt, ALU.mult))
            step(dve.tensor_tensor(ids_f[0:n_ids, :], ids_f[0:n_ids, :], ids_wrap[0:n_ids, :], ALU.add))
            dve.tensor_scalar(ids_f[0:n_ids, :], ids_f[0:n_ids, :], 0.0, float(vocabulary - 1), ALU.max, ALU.min).then_inc(ids_wrapped, 1)
            dve.memset(ones_row[:, :], 1.0)
            dve.memset(q_aug[:, :, :, :], 0.0)
            dve.memset(k_aug[:, :, :, :], 0.0)
            dve.memset(v_one[:, :, :, :], 1.0)
            dve.tensor_copy(prio[:, :], cst[:, C_PRIO:C_PRIO + ROTS])
            dve.tensor_copy(first_bias[:, :], vec[:, LN1A_B:LN1A_B + 1].to_broadcast([P, P]))
            bn = [vec[:, BN + 4 * n:BN + 4 * n + 4] for n in range(5)]
            step(dve.tensor_scalar(bn_bias[:, :], bn[4], LN_EPS, None, ALU.add))
            inverse_root(bn_scale[:, :], bn_bias[:, :], bn_tmp[:, :])
            step(dve.tensor_tensor(bn_scale[:, :], bn_scale[:, :], bn[1], ALU.mult))
            step(dve.tensor_tensor(bn_tmp[:, :], bn[0], bn[3], ALU.subtract))
            step(dve.tensor_tensor(bn_tmp[:, :], bn_tmp[:, :], bn_scale[:, :], ALU.mult))
            dve.tensor_tensor(bn_bias[:, :], bn_tmp[:, :], bn[2], ALU.add)
            dve.memset(k_aug[:, :, :, DH:DH + 1], 1.0)
            step(dve.tensor_tensor(wblk_scaled[:, :, :], wblk_rows[:, :, :], bn_scale[:, :].unsqueeze(2).to_broadcast([P, 4, P]), ALU.mult))
            dve.sem_inc(setup_scaled, 1)
            dve.wait_ge(setup_psum, 1)
            dve.tensor_copy(ids_col[:, :], ps_tr[:, 0:P])
            dve.wait_ge(setup_psum, 6)
            step(dve.tensor_tensor(pos_sb[:, :, :], pos_sb[:, :, :],
                                   ps_wide[0][:, 512:512 + P].unsqueeze(1).to_broadcast([P, TILES, P]), ALU.add))
            dve.sem_inc(setup_read, 1)

            def normalise(it, source, to):
                for t in range(TILES):
                    dve.bn_stats(stats[:, t, :], source[:, t, :])
                dve.drain()
                for t in range(TILES):
                    dve.bn_aggr(moments[:, t, :], stats[:, t, :])
                dve.drain()
                step(dve.tensor_scalar(variance[:, :], moments[:, :, 1], LN_EPS, 0.5, ALU.add, ALU.mult))
                step(dve.tensor_scalar(rstd[:, :].bitcast(I32), variance[:, :].bitcast(I32), -0.5, HALF_ROOT_GUESS, ALU.mult, ALU.add))
                for _ in range(3):
                    for t in range(TILES):
                        dve.tensor_scalar(root_tmp[:, t:t + 1], rstd[:, t:t + 1], rstd[:, t:t + 1], variance[:, t:t + 1], ALU.mult, ALU.mult)
                    dve.drain()
                    step(dve.scalar_tensor_tensor(rstd[:, :], root_tmp[:, 0:TILES], 1.5, rstd[:, :], ALU.subtract, ALU.mult))
                for t in range(TILES):
                    ins = dve.tensor_scalar(to[:, t, :], source[:, t, :], moments[:, t, 0:1], rstd[:, t:t + 1], ALU.subtract, ALU.mult)
                ins.then_inc(xhat_ready.sem, 1)

            def psum_tokens(bank):
                return bank[:, 0:TILES * P].rearrange("p (t d) -> p t d", t=TILES)

            def ids_ahead(it):
                dve.tensor_copy(ids_now[:, :], ids_col[:, bass.ds(it * TILES, TILES)]).then_inc(ids_ready.sem, 1)

            def embed(it):
                dve.wait_ge(emb_here.sem, emb_here.at(it, 16 * TILES))
                dve.tensor_tensor(y1[:, :, :], emb_rows[:, :, :], pos_sb[:, :, :], ALU.add).then_inc(y1_made.sem, 1)
                dve.drain()
                normalise(it, y1, xhat)

            def first_ffn(it):
                dve.wait_ge(ffn_in_psum.sem, ffn_in_psum.at(it, 1))
                step(dve.tensor_tensor(y2[:, :, :], psum_tokens(ps_wide[1]), b2_all[:, 0:1, :].to_broadcast([P, TILES, P]), ALU.add))
                normalise(it, y2, xhat)

            def heads(it):
                dve.wait_ge(qkv_in_psum.sem, qkv_in_psum.at(it, 1))
                qkv = ps_wide[1][:, :].rearrange("p (t w h d) -> p t w h d", t=2 * TILES, w=2, h=HEADS)
                dve.tensor_copy(v_one[:, :, :, 0:DH], qkv[:, 0:TILES, 1, :, :])
                step(dve.tensor_copy(q_aug[:, :, :, 0:DH], qkv[:, 0:TILES, 0, :, :]))
                q = q_aug[:, :, :, 0:DH].rearrange("p t h d -> p (t h) d")
                step(dve.tensor_tensor(q_sq[:, :, :], q, q, ALU.mult))
                step(dve.tensor_reduce(norm2[:, :], q_sq[:, :, :], AX_X, ALU.add))
                inverse_root(inv_norm[:, :], norm2[:, :], root_tmp[:, :])
                step(dve.tensor_tensor(norm[:, :], norm2[:, :], inv_norm[:, :], ALU.mult))
                step(dve.tensor_scalar(norm[:, :], norm[:, :], 1e-6, None, ALU.add))
                step(dve.reciprocal(inv_norm[:, :], norm[:, :]))
                step(dve.tensor_scalar(inv_norm[:, :], inv_norm[:, :], float(DH) ** -0.5, None, ALU.mult))
                dve.scalar_tensor_tensor(q_aug[:, :, :, DH:DH + 1].rearrange("p t h d -> p (t h d)"), norm2[:, :], -1.0, inv_norm[:, :],
                                         ALU.mult, ALU.mult)
                dve.tensor_tensor(k_aug[:, :, :, 0:DH].rearrange("p t h d -> p (t h) d"), q,
                                  inv_norm[:, :].unsqueeze(2).to_broadcast([P, TILES * HEADS, DH]), ALU.mult).then_inc(aug_ready.sem, 1)

            def sides(it):
                for t in range(TILES):
                    dve.wait_ge(rot_in_psum.sem, rot_in_psum.at(it, t + 1))
                    for half in range(2):
                        o = slice(half * ORDERS // 2, (half + 1) * ORDERS // 2)
                        ins = dve.scalar_tensor_tensor(
                            rot_side[:, t, o, :], ps_wide[t][:, half * 512:half * 512 + 512].rearrange("p (o k) -> p o k", k=ROTS),
                            0.0, prio[:, :].unsqueeze(1).to_broadcast([P, ORDERS // 2, ROTS]), ALU.is_ge, ALU.add)
                    ins.then_inc(side_taken.sem, 1)

            def buckets(it, tiles):
                for t in tiles:
                    dve.wait_ge(abs_taken.sem, abs_taken.at(it, t + 1))
                    step(dve.tensor_reduce(rot_max[:, :], rot_abs[:, t, :, :], AX_X, ALU.max))
                    step(dve.tensor_tensor(rot_hit[:, :, :], rot_abs[:, t, :, :],
                                           rot_max[:, :].unsqueeze(2).to_broadcast([P, ORDERS, ROTS]), ALU.is_equal))
                    step(dve.tensor_tensor(rot_won[:, :, :].rearrange("p o k -> p (o k)"), rot_hit[:, :, :].rearrange("p o k -> p (o k)"),
                                           rot_side[:, t, :, :].rearrange("p o k -> p (o k)"), ALU.mult))
                    step(dve.tensor_reduce(bucket[:, :], rot_won[:, :, :], AX_X, ALU.max))
                    ins = dve.tensor_scalar(sort_key[:, t, :, :], bucket[:, :].unsqueeze(1).to_broadcast([P, 3, ORDERS]),
                                            float(-ROTS * SEQ), cst[:, C_POS + t:C_POS + t + 1], ALU.mult, ALU.add)
                if tiles[-1] == TILES - 1:
                    ins.then_inc(sort_key_ready.sem, 1)

            def thresholds(it, bits):
                if bits[0] == KEY_BITS - 1:
                    dve.wait_ge(sort_keyT_in_psum.sem, sort_keyT_in_psum.at(it, 1))
                    dve.tensor_copy(keys_rows[:, :], ps_tr[0:3 * ORDERS, 0:SEQ])
                    step(dve.memset(probe[:, :], float(1 << (KEY_BITS - 1))))
                for bit in bits:
                    step(dve.tensor_scalar(below[:, :], keys_rows[:, :], probe[:, 0:1], 0.0, ALU.is_lt, ALU.add, accum_out=count[:, :]))
                    step(dve.tensor_scalar(step_up[:, :], count[:, :], cst[0:3 * ORDERS, C_RANK:C_RANK + 1], float(1 << bit),
                                           ALU.is_le, ALU.mult))
                    down = float((1 << bit) - ((1 << bit) >> 1))
                    step(dve.scalar_tensor_tensor(probe[:, :], probe[:, :], -down, step_up[:, :], ALU.add, ALU.add))
                if bits[-1] == 0:
                    dve.tensor_scalar(reached[:, :], keys_rows[:, :], probe[:, 0:1], None, ALU.is_ge).then_inc(reached_ready.sem, 1)

            def chunks(it):
                dve.wait_ge(chunk_in_psum.sem, chunk_in_psum.at(it, 1))
                step(dve.tensor_tensor(own[:, :, :, :].rearrange("p t o c -> p (t o) c"),
                                       ps_tr[:, 0:TILES * ORDERS].unsqueeze(2).to_broadcast([P, TILES * ORDERS, CHUNKS]),
                                       cst[:, C_CHUNK:C_CHUNK + CHUNKS].unsqueeze(1).to_broadcast([P, TILES * ORDERS, CHUNKS]),
                                       ALU.is_equal))
                dve.tensor_tensor(seen[:, :, :, 1:CHUNKS], own[:, :, :, 1:CHUNKS], own[:, :, :, 0:CHUNKS - 1], ALU.add)
                step(dve.tensor_tensor(seen[:, :, :, 0:1], own[:, :, :, 0:1], own[:, :, :, CHUNKS - 1:CHUNKS], ALU.add))
                for t in range(TILES):
                    dve.tensor_tensor(masked_v[:, t, :, :, :],
                                      v_one[:, t, :, :].unsqueeze(2).to_broadcast([P, HEADS, HASHES * CHUNKS, VC]),
                                      seen[:, t, :, :].rearrange("p (h r) c -> p h (r c)", h=HEADS).unsqueeze(3)
                                      .to_broadcast([P, HEADS, HASHES * CHUNKS, VC]), ALU.mult).then_inc(masked_ready.sem, 1)

            def pick(it):
                for n in range(HEADS * TILES):
                    head, t = n // TILES, n % TILES
                    dve.wait_ge(pv_in_psum.sem, pv_in_psum.at(it, n + 1))
                    dve.tensor_tensor(picked[:, n % 2, :, :], wide_bank(n)[:, 0:MASKED].rearrange("p (c v) -> p c v", v=VC),
                                      own[:, t, HASHES * head:HASHES * (head + 1), :].rearrange("p r c -> p (r c)").unsqueeze(2)
                                      .to_broadcast([P, HASHES * CHUNKS, VC]), ALU.mult).then_inc(pv_taken.sem, 1)
                    dve.drain()
                    dve.tensor_reduce(hashed[:, t, head, :, :], picked[:, n % 2, :, :].rearrange("p (r c) v -> p r v c", r=HASHES),
                                      AX_X, ALU.add)
                dve.drain()

            def attention_mean(it):
                every = hashed[:, :, :, :, :].rearrange("p t h r v -> p (t h r) v")
                step(dve.reciprocal(inv_sum[:, :], every[:, :, DH]))
                step(dve.tensor_tensor(hashed_n[:, :, :], every[:, :, 0:DH],
                                       inv_sum[:, :].unsqueeze(2).to_broadcast([P, TILES * ORDERS, DH]), ALU.mult))
                dve.tensor_reduce(attended[:, :, :].rearrange("p t (h d) -> p (t h) d", h=HEADS),
                                  hashed_n[:, :, :].rearrange("p (n r) d -> p n d r", r=HASHES), AX_X, ALU.add
                                  ).then_inc(attended_ready.sem, 1)

            def attention_out(it):
                dve.wait_ge(wo_in_psum.sem, wo_in_psum.at(it, 1))
                step(dve.tensor_tensor(y1[:, :, :], psum_tokens(ps_wide[1]), y1[:, :, :], ALU.add))

            def half_sums(it):
                step(dve.tensor_tensor(half_sum[:, :, :], y2[:, :, :], b2_all[:, 1:2, :].to_broadcast([P, TILES, P]), ALU.add))
                step(dve.tensor_tensor(half_sum[:, :, :], half_sum[:, :, :], y1[:, :, :], ALU.add))
                step(dve.tensor_scalar(half_sum[:, :, :], half_sum[:, :, :], 0.5, None, ALU.mult))

            def second_ffn(it):
                dve.wait_ge(ffn_in_psum.sem, ffn_in_psum.at(it, 2))
                step(dve.scalar_tensor_tensor(h[:, :, :].rearrange("p t d -> p (t d)"), ps_wide[1][:, 0:TILES * P], 0.5,
                                              half_sum[:, :, :].rearrange("p t d -> p (t d)"), ALU.mult, ALU.add))
                normalise(it, h, xhat)

            def linear_attention(it):
                dve.wait_ge(kv_in_psum.sem, kv_in_psum.at(it, 1))
                dve.tensor_tensor(kv_diag[:, :], ps_wide[1][:, 512:512 + P], cst[:, C_DIAG:C_DIAG + P], ALU.mult).then_inc(kv_diag_ready.sem, 1)

            def linear_attention_out(it):
                dve.wait_ge(blk_p_in_psum.sem, blk_p_in_psum.at(it, 1))
                step(dve.scalar_tensor_tensor(h2[:, :, :].rearrange("p t d -> p (t d)"), ps_pair[1][:, 0:TILES * P], 0.0,
                                              h[:, :, :].rearrange("p t d -> p (t d)"), ALU.max, ALU.add))
                normalise(it, h2, z)

            def top_halves(it):
                for n in range(HEADS):
                    dve.wait_ge(halves_in_psum.sem, halves_in_psum.at(it, n + 1))
                    dve.sem_inc(vector_passed, 1)
                    for t in range(TILES):
                        for half in range(2):
                            dve.max(half_s[:, t, n, half, :], halves_bank(n, half)[:, t * EXPERTS:(t + 1) * EXPERTS])
                    dve.drain()
                    for t in range(TILES):
                        for half in range(2):
                            ins = dve.max_index(half_i[:, t, n, half, :], half_s[:, t, n, half, :],
                                                halves_bank(n, half)[:, t * EXPERTS:(t + 1) * EXPERTS])
                    ins.then_inc(halves_taken.sem, 1)
                dve.drain()

            def choose(it):
                step(dve.tensor_copy(half_f[:, :, :, :].rearrange("p n c k -> p (n c k)"),
                                     half_i[:, :, :, :, :].rearrange("p t n c k -> p (t n c k)")))
                step(dve.tensor_scalar(half_f[:, :, 0, :], half_f[:, :, 0, :], float(EXPERTS), None, ALU.mult))
                for pair, halves in ((pair_s, half_s[:, :, :, :, :].rearrange("p t n c k -> p (t n) c k")), (pair_i, half_f)):
                    a, b = halves[:, :, 0, :], halves[:, :, 1, :]
                    n = TILES * HEADS
                    dve.tensor_tensor(pair[:, :, 0:8], b[:, :, 0:8], a[:, :, 0:1].to_broadcast([P, n, 8]), ALU.add)
                    dve.tensor_tensor(pair[:, :, 8:12], b[:, :, 0:4], a[:, :, 1:2].to_broadcast([P, n, 4]), ALU.add)
                    dve.tensor_tensor(pair[:, :, 12:16].rearrange("p n (i j) -> p n i j", i=2),
                                      b[:, :, 0:2].unsqueeze(2).to_broadcast([P, n, 2, 2]),
                                      a[:, :, 2:4].unsqueeze(3).to_broadcast([P, n, 2, 2]), ALU.add)
                    dve.tensor_tensor(pair[:, :, 16:20], a[:, :, 4:8], b[:, :, 0:1].to_broadcast([P, n, 4]), ALU.add)
                dve.drain()
                for n in range(TILES * HEADS):
                    dve.max(best_s[:, n, :], pair_s[:, n, :])
                dve.drain()
                dve.tensor_tensor(shifted[:, :, :], best_s[:, :, :], best_s[:, :, 0:1].to_broadcast([P, TILES * HEADS, TOPK]),
                                  ALU.subtract).then_inc(shifted_ready.sem, 1)
                for n in range(TILES * HEADS):
                    dve.max_index(best_p[:, n, :], best_s[:, n, :], pair_s[:, n, :])
                dve.drain()
                step(dve.tensor_copy(best_f[:, :, :].rearrange("p n k -> p (n k)"), best_p[:, :, :].rearrange("p n k -> p (n k)")))
                step(dve.tensor_tensor(choice[:, :, :], best_f[:, :, :].rearrange("p n k -> p (n k)").unsqueeze(2).to_broadcast([P, TILES * ROWS, CAND]),
                                       cst[:, C_CAND:C_CAND + CAND].unsqueeze(1).to_broadcast([P, TILES * ROWS, CAND]), ALU.is_equal))
                by_pair = choice[:, :, :].rearrange("p (n k) c -> p n k c", k=TOPK)
                step(dve.tensor_tensor(by_pair, by_pair, pair_i[:, :, :].unsqueeze(2).to_broadcast([P, TILES * HEADS, TOPK, CAND]), ALU.mult))
                step(dve.tensor_reduce(expert[:, :, :].rearrange("p t n -> p (t n)"), choice[:, :, :], AX_X, ALU.add))
                dve.wait_ge(exps_ready.sem, exps_ready.at(it, 1))
                step(dve.tensor_reduce(exp_sum[:, :], exps[:, :, :], AX_X, ALU.add))
                step(dve.reciprocal(exp_sum[:, :], exp_sum[:, :]))
                step(dve.tensor_tensor(gate[:, :, :], exps[:, :, :], exp_sum[:, :].unsqueeze(2).to_broadcast([P, TILES * HEADS, TOPK]), ALU.mult))
            def hand_over(t, it):
                dve.drain()
                dve.tensor_copy(x_index[:, t, :], expert[:, t, :]).then_inc(index_ready[t].sem, 1)
                dve.tensor_copy(x_expert[:, t, :], z[:, t, :])
                dve.tensor_copy(x_gate[:, GROUPS // TILES * t:GROUPS // TILES * (t + 1), :].rearrange("p g s -> p (g s)"),
                                gate[:, HEADS * t:HEADS * (t + 1), :].rearrange("p n k -> p (n k)"))

            def hand_over_residual(t):
                step(dve.tensor_copy(x_resid[:, t, :], h2[:, t, :]))

            def dots(g, it):
                t = g // (GROUPS // TILES)
                dve.wait_ge(gathered[g].sem, gathered[g].at(it, 16 * GROUP))
                for s in range(GROUP):
                    row = ring[:, g % RING, s, 0, :]
                    ins = dve.scalar_tensor_tensor(row, row, 1.0, x_expert[:, t, :], ALU.mult, ALU.mult, accum_out=dot[:, s:s + 1])
                ins.then_inc(dots_ready.sem, 1)

            def values(g, it):
                dve.wait_ge(gelu_ready.sem, gelu_ready.at(it, g + 1))
                dve.tensor_tensor(value[:, g % RING, :], gelu[:, :], x_gate[:, g, :], ALU.mult).then_inc(value_ready.sem, 1)

            def finish(t, it):
                dve.wait_ge(mix_in_psum.sem, mix_in_psum.at(it, t + 1))
                step(dve.tensor_reduce(mix[:, :], ps_mix[:, :, :].rearrange("p n d -> p d n"), AX_X, ALU.add))
                dve.wait_ge(stored[t].sem, stored[t].at(it, 1))
                step(dve.tensor_tensor(out_rows[:, t, :], mix[:, :], x_resid[:, t, :], ALU.add))
                dve.sem_inc(out_ready.sem, 1)

            EARLY = 4

            def head(it, tower=True, ids_left=True):
                if ids_left:
                    ids_ahead(it + 2)
                dots(1, it)
                if tower:
                    thresholds(it + 1, range(KEY_BITS - 1, EARLY - 1, -1))
                values(1, it)
                if tower:
                    thresholds(it + 1, range(EARLY - 1, -1, -1))
                dots(2, it)
                if tower:
                    chunks(it + 1)
                values(2, it)
                if tower:
                    pick(it + 1)
                    attention_mean(it + 1)
                dots(3, it)
                if tower:
                    attention_out(it + 1)
                values(3, it)
                if tower:
                    normalise(it + 1, y1, xhat)
                    half_sums(it + 1)
                dots(4, it)
                if tower:
                    second_ffn(it + 1)
                finish(0, it)
                values(4, it)
                dots(5, it)
                if tower:
                    linear_attention(it + 1)
                values(5, it)
                if tower:
                    linear_attention_out(it + 1)
                dots(6, it)
                if tower:
                    top_halves(it + 1)
                values(6, it)
                if tower:
                    choose(it + 1)

            def tail(it, tower=True, group7=True, group0=True):
                if group0:
                    hand_over(0, it + 1)
                    hand_over_residual(0)
                if tower:
                    embed(it + 2)
                if group7:
                    dots(7, it)
                if tower:
                    first_ffn(it + 2)
                if group7:
                    values(7, it)
                if tower:
                    heads(it + 2)
                if group0:
                    hand_over(1, it + 1)
                    dve.drain()
                    dots(0, it + 1)
                if tower:
                    sides(it + 2)
                    buckets(it + 2, (0,))
                if group7:
                    finish(1, it)
                if group0:
                    hand_over_residual(1)
                    values(0, it + 1)
                if tower:
                    buckets(it + 2, (1,))

            dve.wait_ge(setup_read, 5)
            ids_ahead(0)
            tail(-2, group7=False, group0=False)
            ids_ahead(1)
            thresholds(0, range(KEY_BITS - 1, -1, -1))
            chunks(0)
            pick(0)
            attention_mean(0)
            attention_out(0)
            normalise(0, y1, xhat)
            half_sums(0)
            second_ffn(0)
            linear_attention(0)
            linear_attention_out(0)
            top_halves(0)
            choose(0)
            tail(-1, group7=False)
            with dve.Fori(0, batches - 2) as i:
                head(i)
                tail(i)
            head(batches - 2, ids_left=False)
            tail(batches - 2, tower=False)
            head(batches - 1, tower=False, ids_left=False)
            tail(batches - 1, tower=False, group0=False)


def kernel(**inputs):
    import numpy as np
    import concourse.bacc as bacc
    from concourse import mybir as my
    from concourse.bass_utils import run_bass_kernel_spmd

    a = {k: np.asarray(v) for k, v in inputs.items()}
    t = {k[len("L0_tok_"):]: v for k, v in a.items() if k.startswith("L0_tok_")}
    b = {k[len("L0_attn_"):]: v for k, v in a.items() if k.startswith("L0_attn_")}
    f = {k[len("L0_ffn_"):]: v for k, v in a.items() if k.startswith("L0_ffn_")}
    sequences, length = a["x"].shape

    columns = [t["ln1_s"][1], t["ln1_b"][1], t["ln2_s"][0], t["ln2_b"][0], t["ln2_s"][1], t["ln2_b"][1], t["ln1_b"][0]]
    columns += list(t["b1"].reshape(2 * HID, P))
    columns += [b[f"{w}_{part}"] for part in ("b", "g", "beta", "mu", "var") for w in "qkvp"]
    columns += list(f["bq"].reshape(HEADS, P))

    const = np.zeros((P, NCONST), np.float32)
    const[:, C_ID:C_ID + P] = np.eye(P)
    const[:, C_DIAG:C_DIAG + P] = np.kron(np.eye(HEADS), np.full((DH, DH), 0.125))
    const[0:3 * ORDERS, C_SUM:C_SUM + ORDERS] = np.tile(np.eye(ORDERS), (3, 1))
    const[:, C_CHUNK:C_CHUNK + CHUNKS] = np.arange(CHUNKS)
    const[:, C_CAND:C_CAND + CAND] = np.arange(CAND)
    const[:, C_PRIO:C_PRIO + ROTS] = (ROTS - np.arange(ROTS)) / ROTS
    for tile in range(TILES):
        const[:, C_POS + tile] = 2 * ROTS * SEQ + tile * P + np.arange(P)
    const[0:3 * ORDERS, C_RANK] = 64 * (1 + np.arange(3 * ORDERS) // ORDERS)

    arrays = {
        "ids": a["x"].reshape(sequences * TILES, P),
        "emb": t["emb"],
        "pos": t["pos"],
        "vecs": np.stack(columns, axis=1),
        "consts": const,
        "b2": t["b2"], "wqk": t["Wqk"], "wv": t["Wv"], "wo": t["Wo"], "rots": t["rots"], "w1": t["W1"], "w2": t["W2"],
        "wblk": np.stack([b[f"{w}_w"] for w in "qkvp"]),
        "wqT": f["Wq"].T,
        "keysT": f["keys"].transpose(1, 3, 0, 2).reshape(P, HEADS * EXPERTS),
        "table": np.concatenate([f["w_down_embed"], f["w_up_embed"]], axis=1),
    }
    nc = bacc.Bacc("TRN2", target_bir_lowering=False, num_devices=1)
    arrays = {name: np.ascontiguousarray(v) for name, v in arrays.items()}
    args = [nc.dram_tensor(name, v.shape, my.dt.from_np(v.dtype), kind="ExternalInput").ap() for name, v in arrays.items()]
    out = nc.dram_tensor("out", (sequences * length, P), my.dt.float32, kind="ExternalOutput").ap()
    build(nc, *args, out)
    r = run_bass_kernel_spmd(nc, [arrays], core_ids=[0])
    return r.results[0]["out"].reshape(sequences, length, P)
```

```python
from contextlib import ExitStack

import concourse.bass as bass
from concourse import mybir

ALU = mybir.AluOpType
ACT = mybir.ActivationFunctionType
AX_X = mybir.AxisListType.X
F32 = mybir.dt.float32
BF16 = mybir.dt.bfloat16
I32 = mybir.dt.int32
U32 = mybir.dt.uint32

P = 128
TILES = 2
SEQ = P * TILES
HEADS = 8
DH = P // HEADS
AUG = 32
HASHES = 4
ORDERS = HEADS * HASHES
ROTS = 32
CHUNKS = SEQ // 64
HID = 4
VC = DH + 1
MASKED = HASHES * CHUNKS * VC
TOPK = 8
CAND = 20
ROWS = HEADS * TOPK
EXPERTS = 128
GROUP = 16
GROUPS = TILES * ROWS // GROUP
RING = 4
EARLY_HEADS = 2
KEY_BITS = 14
LN_EPS = 1e-5
ROOT_GUESS = float(0x5F3759DF)
ROOT_A = -0.9034816386646751
ROOT_B = 1.7067791804276105
ROOT_C = -4.241986606244085
ROOT_D = 5.26532839907137
ROOT_GAIN = 3.64868728337055

LN1_S, LN1_B, LN2A_S, LN2A_B, LN2B_S, LN2B_B, LN1A_B = range(7)
B1 = 7
BN = B1 + 2 * HID
BQ = BN + 5 * 4
NVEC = BQ + HEADS
C_ID = 0
C_DIAG = C_ID + P
C_SUM = C_DIAG + P
C_CHUNK = C_SUM + ORDERS
C_CAND = C_CHUNK + CHUNKS
C_PRIO = C_CAND + CAND
C_POS = C_PRIO + ROTS
C_RANK = C_POS + TILES
C_PART = C_RANK + 1
NCONST = C_PART + 2


class Signal:

    def __init__(self, nc, ctx, name, per):
        self.sem = ctx.enter_context(nc.semaphore(name))
        self.per = per

    def at(self, it, n):
        return it * self.per + n


def build(nc, ids, emb, pos, vecs, consts, b2, wqk, wv, wo, rots, w1, w2, wblk, wq, keysT, table, out):
    batches = ids.shape[0] // TILES
    vocabulary = emb.shape[0]
    with ExitStack() as ctx:
        def sb(name, shape, dt=F32):
            return ctx.enter_context(nc.sbuf_tensor(name, shape, dt))

        def sem(name):
            return ctx.enter_context(nc.semaphore(name))

        def sig(name, per):
            return Signal(nc, ctx, name, per)

        cst = sb("cst", [P, NCONST])
        vec = sb("vec", [P, NVEC])
        ident = cst[:, C_ID:C_ID + P]
        ids_rows = sb("ids_rows", [P, P], I32)
        ids_col = sb("ids_col", [P, P], I32)
        pos_sb = sb("pos_sb", [P, TILES, P])
        b2_row = sb("b2_row", [1, 2 * P])
        b2_all = sb("b2_all", [P, 2, P])
        ones_row = sb("ones_row", [1, P])
        w_qkv = sb("w_qkv", [P, 2 * P])
        w_o1 = sb("w_o1", [P, P])
        w1_sb = sb("w1_sb", [P, 2, HID, P])
        w2_sb = sb("w2_sb", [P, 2, HID, P])
        rot_sb = sb("rot_sb", [P, 2, 4 * HASHES * ROTS])
        wblk_T = sb("wblk_T", [P, 4, P])
        bn_scale = sb("bn_scale", [P, 4])
        bn_tmp = sb("bn_tmp", [P, 4])
        bn_bias = sb("bn_bias", [P, 4])
        bias_row = sb("bias_row", [1, 3 * P])
        key_x = sb("key_x", [P, HEADS, 2, EXPERTS])
        key_bias = sb("key_bias", [3, HEADS, 2, EXPERTS], BF16)
        ones_bf = sb("ones_bf", [3, P], BF16)
        bq3 = sb("bq3", [P, HEADS, 3])
        cand = sb("cand", [P, CAND, ROWS], BF16)
        prio = sb("prio", [P, ROTS], BF16)

        ids_now = sb("ids_now", [P, TILES], I32)
        emb_rows = sb("emb_rows", [P, TILES, P])
        y1 = sb("y1", [P, TILES, P])
        y2 = sb("y2", [P, TILES, P])
        half_sum = sb("half_sum", [P, TILES, P])
        stats = sb("stats", [P, TILES, 6])
        moments = sb("moments", [P, TILES, 2])
        variance = sb("variance", [P, TILES])
        rstd = sb("rstd", [P, TILES])
        root_tmp = sb("root_tmp", [P, 2, TILES * HEADS])
        xhat = sb("xhat", [P, TILES, P])
        xT = sb("xT", [P, SEQ])
        hidT = sb("hidT", [P, HID, SEQ])
        q_aug = sb("q_aug", [P, TILES, HEADS, AUG])
        k_aug = sb("k_aug", [P, TILES, HEADS, AUG])
        v_one = sb("v_one", [P, TILES, HEADS, VC])
        q_sq = sb("q_sq", [P, TILES * HEADS, DH])
        norm2 = sb("norm2", [P, TILES * HEADS])
        norm = sb("norm", [P, TILES * HEADS])
        inv_norm = sb("inv_norm", [P, TILES * HEADS])
        qT = sb("qT", [P, 2, SEQ])
        kT = sb("kT", [P, 2, SEQ])
        rot_side = sb("rot_side", [P, TILES, ORDERS, ROTS], BF16)
        rot_abs = sb("rot_abs", [P, TILES, ORDERS, ROTS])
        rot_max = sb("rot_max", [P, ORDERS])
        rot_hit = sb("rot_hit", [P, ORDERS, ROTS], BF16)
        rot_won = sb("rot_won", [P, ORDERS, ROTS], BF16)
        bucket = sb("bucket", [P, ORDERS])
        sort_key = sb("sort_key", [P, TILES, 3, ORDERS])
        below = sb("below", [3 * ORDERS, SEQ])
        count = sb("count", [3 * ORDERS, 1])
        lower = sb("lower", [3 * ORDERS, 1])
        probe = sb("probe", [3 * ORDERS, 1])
        reached = sb("reached", [3 * ORDERS, SEQ])
        own = sb("own", [P, TILES, ORDERS, CHUNKS])
        seen = sb("seen", [P, TILES, ORDERS, CHUNKS])
        masked_v = sb("masked_v", [P, TILES, HEADS, HASHES * CHUNKS, VC])
        weights = sb("weights", [P, HEADS, TILES, SEQ])
        picked = sb("picked", [P, 2, TILES, HASHES * CHUNKS, VC])
        hashed = sb("hashed", [P, HEADS, TILES, HASHES, VC])
        inv_sum = sb("inv_sum", [P, TILES * ORDERS])
        hashed_n = picked[:, :, :, :, :].rearrange("p a t c v -> p (a t c v)")[:, 0:TILES * ORDERS * DH].rearrange("p (n d) -> p n d", d=DH)
        attended = sb("attended", [P, TILES, P])
        h = sb("h", [P, TILES, P])
        h2 = sb("h2", [P, TILES, P])
        bqT = sb("bqT", [P, SEQ])
        bkv = sb("bkv", [P, TILES, 2 * P])
        kv_diag = sb("kv_diag", [P, P])
        boT = sb("boT", [P, SEQ])
        z = sb("z", [P, TILES, P])
        half_s = sb("half_s", [P, TILES, HEADS, 2, TOPK])
        half_i = sb("half_i", [P, TILES, HEADS, 2, TOPK], U32)
        half_f = sb("half_f", [P, TILES * HEADS, 2, TOPK])
        pair_s = sb("pair_s", [P, TILES * HEADS, CAND])
        pair_i = sb("pair_i", [P, TILES * HEADS, CAND])
        best_s = sb("best_s", [P, TILES * HEADS, TOPK])
        best_p = sb("best_p", [P, TILES * HEADS, TOPK], U32)
        expert = sb("expert", [P, ROWS])
        best_bf = sb("best_bf", [P, TILES * ROWS], BF16)
        shifted = sb("shifted", [P, TILES * HEADS, TOPK])
        exps = sb("exps", [P, TILES * HEADS, TOPK])
        exp_sum = sb("exp_sum", [P, TILES * HEADS])

        x_expert = sb("x_expert", [P, TILES, P])
        x_resid = sb("x_resid", [P, TILES, P])
        x_gate = sb("x_gate", [P, GROUPS, GROUP])
        x_index = sb("x_index", [P, TILES, ROWS], I32)
        ring = sb("ring", [P, RING, GROUP, 2, P])
        ids_f, ids_wrap, first_bias, first_value, w_v0, w_o0 = (ring[:, 0, n, 0, :] for n in range(6))
        wq_rows, key_rows = (ring[:, 3, 4 * n:4 * n + 4, :, :].rearrange("p a b d -> p (a b) d") for n in range(2))
        key_bias_f = ring[0:3, 3, 8:16, :, :].rearrange("p h c e -> p h c e")
        wblk_rows, wblk_scaled = (ring[:, n, 0:2, :, :].rearrange("p a b d -> p (a b) d") for n in (1, 2))
        masked_flat = masked_v[:, :, :, :, :].rearrange("p t h c v -> p (t h c v)")
        choice = masked_flat[:, 0:ROWS * CAND].rearrange("p (c n) -> p c n", c=CAND)
        is_choice = masked_flat[:, ROWS * CAND:ROWS * CAND * 3 // 2].bitcast(BF16).rearrange("p (c n) -> p c n", c=CAND)
        dot = sb("dot", [P, 2, GROUP])
        gelu = sb("gelu", [P, 2, GROUP])
        value = sb("value", [P, RING, GROUP])
        mix = sb("mix", [P, P])
        out_rows = sb("out_rows", [P, TILES, P])

        ps_mix = ctx.enter_context(nc.psum_tensor("ps_mix", [P, 4, P], F32))
        ps_tr = ctx.enter_context(nc.psum_tensor("ps_tr", [P, 512], F32))
        ps_wide = [ctx.enter_context(nc.psum_tensor(f"ps_wide{n}", [P, 1024], F32)) for n in range(2)]
        ps_pair = [ctx.enter_context(nc.psum_tensor(f"ps_pair{n}", [P, 512], F32)) for n in range(2)]

        def pv_bank(head, t):
            return ps_wide[head % 2][:, 512 * t:512 * t + 512]

        def halves_bank(n):
            return (ps_wide[0][:, 0:512], ps_wide[0][:, 512:1024], ps_pair[0], ps_pair[1])[n % 4]

        loaded = sem("loaded")
        tensor_loaded = sem("tensor_loaded")
        zeroed = sem("zeroed")
        rots_loaded = sem("rots_loaded")
        ids_wrapped = sem("ids_wrapped")
        setup_scaled = sem("setup_scaled")
        setup_psum = sem("setup_psum")
        setup_read = sem("setup_read")
        setup_keys = sem("setup_keys")
        key_bias_ready = sem("key_bias_ready")

        ids_ready = sig("ids_ready", 1)
        emb_here = sig("emb_here", 16 * TILES)
        y1_made = sig("y1_made", 1)
        xhat_ready = sig("xhat_ready", 5)
        xT_in_psum = sig("xT_in_psum", 5)
        xT_ready = sig("xT_ready", 5)
        hid_in_psum = sig("hid_in_psum", 4)
        hid_ready = sig("hid_ready", 4)
        ffn_in_psum = sig("ffn_in_psum", 2)
        qkv_in_psum = sig("qkv_in_psum", 1)
        aug_ready = sig("aug_ready", 1)
        augT_in_psum = sig("augT_in_psum", 2)
        qT_ready = sig("qT_ready", 1)
        kT_ready = sig("kT_ready", 1)
        rot_in_psum = sig("rot_in_psum", TILES)
        side_taken = sig("side_taken", TILES)
        abs_taken = sig("abs_taken", TILES)
        sort_key_ready = sig("sort_key_ready", 1)
        sort_keyT_in_psum = sig("sort_keyT_in_psum", 1)
        reached_ready = sig("reached_ready", 1)
        chunk_in_psum = sig("chunk_in_psum", 1)
        scores_in_psum = sig("scores_in_psum", HEADS)
        weights_ready = sig("weights_ready", HEADS)
        masked_ready = sig("masked_ready", 2)
        pv_in_psum = sig("pv_in_psum", HEADS)
        pv_taken = sig("pv_taken", HEADS)
        attended_ready = sig("attended_ready", 1)
        attendedT_in_psum = sig("attendedT_in_psum", 1)
        attendedT_ready = sig("attendedT_ready", 1)
        wo_in_psum = sig("wo_in_psum", 1)
        blk_q_in_psum = sig("blk_q_in_psum", 1)
        blk_kv_in_psum = sig("blk_kv_in_psum", TILES)
        blk_q_ready = sig("blk_q_ready", 1)
        blk_kv_ready = sig("blk_kv_ready", TILES)
        kv_in_psum = sig("kv_in_psum", 1)
        kv_diag_ready = sig("kv_diag_ready", 1)
        blk_o_in_psum = sig("blk_o_in_psum", 1)
        blk_o_ready = sig("blk_o_ready", 1)
        blk_p_in_psum = sig("blk_p_in_psum", 1)
        halves_in_psum = sig("halves_in_psum", HEADS)
        halves_taken = sig("halves_taken", HEADS // 2)
        shifted_ready = sig("shifted_ready", 1)
        exps_ready = sig("exps_ready", 1)

        index_ready = [sig(f"index_ready{t}", 1) for t in range(TILES)]
        gathered = [[sig(f"gathered{g}_{half}", 16 * GROUP // 2) for half in range(2)] for g in range(GROUPS)]
        slots_free = sig("slots_free", GROUPS)
        dots_ready = sig("dots_ready", GROUPS)
        gelu_ready = sig("gelu_ready", GROUPS)
        value_ready = sig("value_ready", GROUPS)
        scaled = sig("scaled", GROUPS)
        mix_in_psum = sig("mix_in_psum", TILES)
        out_ready = sig("out_ready", TILES)
        stored = [sig(f"stored{t}", 16) for t in range(TILES)]
        pool_passed = sem("pool_passed")
        vector_passed = sem("vector_passed")

        block = ctx.enter_context(nc.Block())

        LOADS = 0

        @block.sync
        def _(sp):
            nonlocal LOADS

            def load(to, of):
                nonlocal LOADS
                sp.dma_start(to, of).then_inc(loaded, 16)
                LOADS += 1

            load(ids_rows[0:ids.shape[0], :], ids)
            load(cst[:, :], consts)
            load(vec[:, :], vecs)
            load(pos_sb[:, :, :], pos[0, 0:SEQ, :].rearrange("(t p) d -> p t d", p=P))
            load(b2_row[:, :], b2.rearrange("(a l) d -> a (l d)", a=1))
            load(w_qkv[:, 0:P], wqk[1])
            load(w_qkv[:, P:2 * P], wv[1])
            load(w_v0[:, :], wv[0])
            load(w_o0[:, :], wo[0])
            load(w_o1[:, :], wo[1])
            load(wblk_rows[:, :, :], wblk.rearrange("w o i -> o w i"))
            sp.wait_ge(zeroed, 1)
            for n in range(HEADS):
                g = n % 4
                sp.dma_start(rot_sb[AUG * g:AUG * g + DH, n // 4, P * g:P * g + P].rearrange("d (r k) -> d r k", r=HASHES),
                             rots[1, n].rearrange("r d k -> d r k")).then_inc(rots_loaded, 16)
            for t in range(TILES):
                sp.sem_inc(stored[t].sem, 1)

            def store(it):
                for t in range(TILES):
                    sp.wait_ge(out_ready.sem, out_ready.at(it, t + 1))
                    sp.dma_start(out[bass.ds(it * SEQ + t * P, P), :], out_rows[:, t, :]).then_inc(stored[t].sem, 16)

            with sp.Fori(0, batches - 1) as i:
                store(i)
            store(batches - 1)
            for t in range(TILES):
                sp.wait_ge(stored[t].sem, 16 * batches + 1)

        @block.gpsimd
        def _(pool):
            pool.memset(rot_sb[:, :, :], 0.0).then_inc(zeroed, 1)
            pool.dma_start(w1_sb[:, :, :, :], w1.rearrange("l d (c f) -> d l c f", f=P)).then_inc(tensor_loaded, 16)
            pool.dma_start(w2_sb[:, :, :, :], w2.rearrange("l (c f) d -> f l c d", f=P)).then_inc(tensor_loaded, 16)
            pool.dma_start(wq_rows, wq.rearrange("(h n) d -> n h d", h=HEADS)).then_inc(tensor_loaded, 16)
            pool.dma_start(key_rows, keysT.rearrange("f (h e) -> f h e", h=HEADS)).then_inc(tensor_loaded, 16)
            pool.sem_inc(slots_free.sem, RING)

            def gather_embeddings(it):
                pool.wait_ge(ids_ready.sem, ids_ready.at(it, 1))
                pool.sem_inc(pool_passed, 1)
                for t in range(TILES):
                    pool.indirect_dma_start(
                        out=emb_rows[:, t, :], out_offset=None, in_=emb,
                        in_offset=bass.IndirectOffsetOnAxis(ap=ids_now[:, t:t + 1], axis=0)).then_inc(emb_here.sem, 16)

            def gather_experts(it, groups):
                for g in groups:
                    t, first = g // (GROUPS // TILES), g % (GROUPS // TILES) * GROUP
                    pool.wait_ge(index_ready[t].sem, index_ready[t].at(it, 1))
                    pool.sem_inc(pool_passed, 1)
                    pool.wait_ge(slots_free.sem, slots_free.at(it, g + 1))
                    pool.sem_inc(pool_passed, 1)
                    for s in range(GROUP):
                        pool.indirect_dma_start(
                            out=ring[:, g % RING, s, :, :].rearrange("p a d -> p (a d)"), out_offset=None, in_=table,
                            in_offset=bass.IndirectOffsetOnAxis(ap=x_index[:, t, first + s:first + s + 1], axis=0)
                        ).then_inc(gathered[g][2 * s // GROUP].sem, 16)

            gather_embeddings(0)
            gather_embeddings(1)
            with pool.Fori(0, batches - 2) as i:
                gather_experts(i, range(0, 3))
                gather_embeddings(i + 2)
                gather_experts(i, range(3, GROUPS))
            gather_experts(batches - 2, range(GROUPS))
            gather_experts(batches - 1, range(GROUPS))

        @block.tensor
        def _(pe):
            pe.wait_ge(loaded, 16 * LOADS)
            pe.wait_ge(ids_wrapped, 1)
            pe.transpose(ps_tr[:, 0:P], ids_f[:, :], ident).then_inc(setup_psum, 1)
            pe.wait_ge(setup_scaled, 1)
            pe.matmul(ps_wide[0][:, 0:P], w_v0[:, :], first_bias[:, :], start=True, stop=True).then_inc(setup_psum, 1)
            pe.matmul(ps_wide[1][:, 0:2 * P], ones_row[:, :], b2_row[:, :], start=True, stop=True).then_inc(setup_psum, 1)
            for n in range(4):
                last = pe.transpose(ps_pair[0][:, n * P:(n + 1) * P], wblk_scaled[:, n, :], ident)
            last.then_inc(setup_psum, 1)
            for n in range(3):
                last = pe.transpose(ps_pair[1][0:1, n * P:(n + 1) * P], bn_bias[:, n + 1:n + 2], ident)
            last.then_inc(setup_psum, 1)
            pe.wait_ge(setup_read, 1)
            pe.matmul(ps_wide[0][:, 512:512 + P], first_value[:, :], w_o0[:, :], start=True, stop=True).then_inc(setup_psum, 1)

            pe.wait_ge(tensor_loaded, 4 * 16)
            for four in range(2):
                pe.wait_ge(setup_read, 5 + 2 * four)
                for half in range(2):
                    rows = slice(64 * half, 64 * half + 64)
                    for n in range(4):
                        mm = pe.matmul(ps_pair[half][:, n * EXPERTS:(n + 1) * EXPERTS], wq_rows[rows, 4 * four + n, :],
                                       key_rows[rows, 4 * four + n, :], start=True, stop=True)
                    mm.then_inc(setup_keys, 1)
            for half in range(2):
                rows = slice(64 * half, 64 * half + 64)
                for n in range(HEADS):
                    mm = pe.matmul(ps_wide[half][0:3, n * EXPERTS:(n + 1) * EXPERTS], bq3[rows, n, :], key_rows[rows, n, :],
                                   start=True, stop=True)
                mm.then_inc(setup_keys, 1)

            def turn(it, n, source):
                pe.wait_ge(xhat_ready.sem, xhat_ready.at(it, n + 1))
                for t in range(TILES):
                    last = pe.transpose(ps_tr[:, t * P:(t + 1) * P], source[:, t, :], ident)
                last.then_inc(xT_in_psum.sem, 1)

            def feed_forward(it, layer, n):
                pe.wait_ge(xT_ready.sem, xT_ready.at(it, n + 1))
                for c in range(HID):
                    mm = pe.matmul(ps_wide[0][:, c * SEQ:(c + 1) * SEQ], w1_sb[:, layer, c, :], xT[:, :], start=True, stop=True)
                    if c % 2:
                        mm.then_inc(hid_in_psum.sem, 1)
                for c in range(HID):
                    if c % 2 == 0:
                        pe.wait_ge(hid_ready.sem, hid_ready.at(it, 2 * layer + c // 2 + 1))
                    for t in range(TILES):
                        mm = pe.matmul(ps_wide[1][:, t * 512:t * 512 + P], hidT[:, c, t * P:(t + 1) * P], w2_sb[:, layer, c, :],
                                       start=(c == 0), stop=(c == HID - 1))
                mm.then_inc(ffn_in_psum.sem, 1)

            def token_mix(it):
                turn(it, 0, xhat)
                feed_forward(it, 0, 0)

            def queries_keys(it):
                turn(it, 1, xhat)
                pe.wait_ge(xT_ready.sem, xT_ready.at(it, 2))
                for t in range(TILES):
                    mm = pe.matmul(ps_wide[1][:, t * 2 * P:(t + 1) * 2 * P], xT[:, t * P:(t + 1) * P], w_qkv[:, :],
                                   start=True, stop=True)
                mm.then_inc(qkv_in_psum.sem, 1)
                pe.wait_ge(aug_ready.sem, aug_ready.at(it, 1))
                for bank, source in ((ps_pair[0], q_aug), (ps_pair[1], k_aug)):
                    for half in range(2):
                        for t in range(TILES):
                            last = pe.transpose(bank[:, half * SEQ + t * P:half * SEQ + (t + 1) * P],
                                                source[:, t, 4 * half:4 * half + 4, :].rearrange("p h a -> p (h a)"), ident)
                    last.then_inc(augT_in_psum.sem, 1)
                pe.wait_ge(qT_ready.sem, qT_ready.at(it, 1))
                for t in range(TILES):
                    for half in range(2):
                        mm = pe.matmul(ps_wide[t][:, half * 512:half * 512 + 512], qT[:, half, t * P:(t + 1) * P],
                                       rot_sb[:, half, :], start=True, stop=True)
                    mm.then_inc(rot_in_psum.sem, 1)

            def scores(it, heads):
                pe.wait_ge(kT_ready.sem, kT_ready.at(it, 1))
                for n in heads:
                    if n >= 2:
                        pe.wait_ge(weights_ready.sem, weights_ready.at(it, n - 1))
                    rows = slice(AUG * (n % 4), AUG * (n % 4) + AUG)
                    for t in range(TILES):
                        mm = pe.matmul(ps_pair[n % 2][:, t * SEQ:(t + 1) * SEQ], kT[rows, n // 4, t * P:(t + 1) * P],
                                       qT[rows, n // 4, :], start=True, stop=True)
                    mm.then_inc(scores_in_psum.sem, 1)

            def turn_sort_keys(it):
                pe.wait_ge(sort_key_ready.sem, sort_key_ready.at(it, 1))
                for t in range(TILES):
                    last = pe.transpose(ps_tr[0:3 * ORDERS, t * P:(t + 1) * P],
                                        sort_key[:, t, :, :].rearrange("p c o -> p (c o)"), ident)
                last.then_inc(sort_keyT_in_psum.sem, 1)

            def chunks(it):
                pe.wait_ge(reached_ready.sem, reached_ready.at(it, 1))
                for t in range(TILES):
                    mm = pe.matmul(ps_tr[:, t * ORDERS:(t + 1) * ORDERS], reached[:, t * P:(t + 1) * P],
                                   cst[0:3 * ORDERS, C_SUM:C_SUM + ORDERS], start=True, stop=True)
                mm.then_inc(chunk_in_psum.sem, 1)

            def attend(it):
                pe.wait_ge(weights_ready.sem, weights_ready.at(it, HEADS))
                for head in range(HEADS):
                    if head % 4 == 0:
                        pe.wait_ge(masked_ready.sem, masked_ready.at(it, head // 4 + 1))
                    if head >= 2:
                        pe.wait_ge(pv_taken.sem, pv_taken.at(it, head - 1))
                    for t in range(TILES):
                        for kt in range(TILES):
                            mm = pe.matmul(pv_bank(head, t)[:, 0:MASKED], weights[:, head, kt, t * P:(t + 1) * P],
                                           masked_v[:, kt, head, :, :].rearrange("p c v -> p (c v)"),
                                           start=(kt == 0), stop=(kt == TILES - 1))
                    mm.then_inc(pv_in_psum.sem, 1)

            def attention_out(it):
                pe.wait_ge(attended_ready.sem, attended_ready.at(it, 1))
                for t in range(TILES):
                    last = pe.transpose(ps_tr[:, t * P:(t + 1) * P], attended[:, t, :], ident)
                last.then_inc(attendedT_in_psum.sem, 1)
                pe.wait_ge(attendedT_ready.sem, attendedT_ready.at(it, 1))
                for t in range(TILES):
                    mm = pe.matmul(ps_wide[1][:, t * P:(t + 1) * P], xT[:, t * P:(t + 1) * P], w_o1[:, :], start=True, stop=True)
                mm.then_inc(wo_in_psum.sem, 1)

            def second_ffn(it):
                turn(it, 2, xhat)
                feed_forward(it, 1, 2)

            def halves_bias(n):
                pe.matmul(halves_bank(n).rearrange("p (t x) -> p t x", t=TILES), ones_bf[:, :],
                          key_bias[:, n, :, :].rearrange("p c e -> p (c e)").unsqueeze(1).to_broadcast([3, TILES, 2 * EXPERTS]),
                          start=True, stop=False)

            def kv_bank(t):
                return ps_wide[0][:, t * 512:t * 512 + 2 * P]

            def linear_attention_biases(it):
                for t in range(TILES):
                    pe.matmul(kv_bank(t), ones_row[:, :], bias_row[:, 0:2 * P], start=True, stop=False)
                pe.matmul(ps_pair[1][:, 0:TILES * P].rearrange("p (t d) -> p t d", t=TILES), ones_row[:, :],
                          bias_row[:, 2 * P:3 * P].unsqueeze(1).to_broadcast([1, TILES, P]), start=True, stop=False)

            def linear_attention(it):
                linear_attention_biases(it)
                turn(it, 3, xhat)
                pe.wait_ge(xT_ready.sem, xT_ready.at(it, 4))
                for t in range(TILES):
                    pe.matmul(kv_bank(t), xT[:, t * P:(t + 1) * P], wblk_T[:, 1:3, :].rearrange("p w c -> p (w c)"),
                              start=False, stop=True).then_inc(blk_kv_in_psum.sem, 1)
                pe.matmul(ps_wide[1][:, 0:SEQ], wblk_T[:, 0, :], xT[:, :], start=True, stop=True).then_inc(blk_q_in_psum.sem, 1)
                pe.wait_ge(blk_kv_ready.sem, blk_kv_ready.at(it, TILES))
                for t in range(TILES):
                    mm = pe.matmul(ps_wide[1][:, 512:512 + P], bkv[:, t, 0:P], bkv[:, t, P:2 * P], start=(t == 0), stop=(t == TILES - 1))
                mm.then_inc(kv_in_psum.sem, 1)
                halves_bias(0)
                halves_bias(1)
                pe.wait_ge(kv_diag_ready.sem, kv_diag_ready.at(it, 1))
                pe.wait_ge(blk_q_ready.sem, blk_q_ready.at(it, 1))
                pe.matmul(ps_pair[0][:, 0:SEQ], kv_diag[:, :], bqT[:, :], start=True, stop=True).then_inc(blk_o_in_psum.sem, 1)
                pe.wait_ge(blk_o_ready.sem, blk_o_ready.at(it, 1))
                for t in range(TILES):
                    mm = pe.matmul(ps_pair[1][:, t * P:(t + 1) * P], boT[:, t * P:(t + 1) * P], wblk_T[:, 3, :], start=False, stop=(t == TILES - 1))
                mm.then_inc(blk_p_in_psum.sem, 1)

            def halves(it):
                halves_bias(2)
                halves_bias(3)
                pe.wait_ge(xT_ready.sem, xT_ready.at(it, 5))
                for n in range(HEADS):
                    if n >= 4:
                        pe.wait_ge(halves_taken.sem, halves_taken.at(it, n // 2 - 1))
                        halves_bias(n)
                    for t in range(TILES):
                        mm = pe.matmul(halves_bank(n)[:, t * 2 * EXPERTS:(t + 1) * 2 * EXPERTS], xT[:, t * P:(t + 1) * P],
                                       key_x[:, n, :, :].rearrange("p c e -> p (c e)"), start=False, stop=(t == TILES - 1))
                    mm.then_inc(halves_in_psum.sem, 1)

            def experts(g, it):
                t, first = g // (GROUPS // TILES), g % (GROUPS // TILES) == 0
                pe.wait_ge(scaled.sem, scaled.at(it, g + 1))
                for n in range(GROUP // 4):
                    mm = pe.matmul(ps_mix[:, :, :], ident, ring[:, g % RING, 4 * n:4 * n + 4, 1, :],
                                   start=(first and n == 0), stop=(g % (GROUPS // TILES) == GROUPS // TILES - 1 and n == GROUP // 4 - 1))
                mm.then_inc(slots_free.sem, 1)
                if g % (GROUPS // TILES) == GROUPS // TILES - 1:
                    pe.wait_ge(slots_free.sem, slots_free.at(it, g + 1) + RING)
                    pe.sem_inc(mix_in_psum.sem, 1)

            def head(it, tower=True):
                experts(0, it)
                if tower:
                    chunks(it + 1)
                experts(1, it)
                if tower:
                    attend(it + 1)
                    attention_out(it + 1)
                experts(2, it)
                if tower:
                    second_ffn(it + 1)
                if tower:
                    linear_attention(it + 1)
                experts(3, it)
                if tower:
                    turn(it + 1, 4, z)
                    halves(it + 1)
                experts(4, it)
                experts(5, it)

            def tail(it, tower=True, groups=True):
                if tower:
                    token_mix(it + 2)
                    queries_keys(it + 2)
                if groups:
                    experts(6, it)
                if tower:
                    scores(it + 2, range(0, EARLY_HEADS))
                if groups:
                    experts(7, it)
                if tower:
                    turn_sort_keys(it + 2)
                    scores(it + 2, range(EARLY_HEADS, HEADS))

            pe.wait_ge(setup_read, 9)
            pe.wait_ge(key_bias_ready, 1)
            pe.wait_ge(rots_loaded, 16 * HEADS)
            tail(-2, groups=False)
            chunks(0)
            attend(0)
            attention_out(0)
            second_ffn(0)
            linear_attention(0)
            turn(0, 4, z)
            halves(0)
            tail(-1, groups=False)
            with pe.Fori(0, batches - 2) as i:
                head(i)
                tail(i)
            head(batches - 2)
            tail(batches - 2, tower=False)
            head(batches - 1, tower=False)
            tail(batches - 1, tower=False)

        @block.scalar
        def _(act):
            act.wait_ge(setup_psum, 2)
            act.activation(first_value[:, :], ps_wide[0][:, 0:P], ACT.Copy).then_inc(setup_read, 1)
            act.wait_ge(setup_psum, 3)
            act.activation(b2_all[:, :, :].rearrange("p l d -> p (l d)"), ps_wide[1][:, 0:2 * P], ACT.Copy).then_inc(setup_read, 1)
            act.wait_ge(setup_psum, 4)
            act.activation(wblk_T[:, :, :].rearrange("p w c -> p (w c)"), ps_pair[0][:, :], ACT.Copy).then_inc(setup_read, 1)
            act.wait_ge(setup_psum, 5)
            act.activation(bias_row[:, :], ps_pair[1][0:1, 0:3 * P], ACT.Copy).then_inc(setup_read, 1)
            for four in range(2):
                for half in range(2):
                    act.wait_ge(setup_keys, 2 * four + half + 1)
                    act.activation(key_x[:, 4 * four:4 * four + 4, half, :], ps_pair[half][:, :].rearrange("p (n e) -> p n e", e=EXPERTS),
                                   ACT.Copy).then_inc(setup_read, 1)

            def turned(it, n, scale=None, bias=None):
                act.wait_ge(xT_in_psum.sem, xT_in_psum.at(it, n + 1))
                if scale is None:
                    ins = act.activation(xT[:, :], ps_tr[:, 0:SEQ], ACT.Copy)
                else:
                    ins = act.activation(xT[:, :], ps_tr[:, 0:SEQ], ACT.Identity, bias=vec[:, bias:bias + 1], scale=vec[:, scale:scale + 1])
                ins.then_inc(xT_ready.sem, 1)

            def feed_forward(it, layer):
                for c in range(HID):
                    if c % 2 == 0:
                        act.wait_ge(hid_in_psum.sem, hid_in_psum.at(it, 2 * layer + c // 2 + 1))
                    ins = act.activation(hidT[:, c, :], ps_wide[0][:, c * SEQ:(c + 1) * SEQ], ACT.Gelu_apprx_tanh,
                                         bias=vec[:, B1 + HID * layer + c:B1 + HID * layer + c + 1])
                    if c % 2:
                        ins.then_inc(hid_ready.sem, 1)

            def token_mix(it):
                turned(it, 0, LN2A_S, LN2A_B)
                feed_forward(it, 0)

            def normalised(it):
                turned(it, 1, LN1_S, LN1_B)

            def turned_heads(it):
                act.wait_ge(augT_in_psum.sem, augT_in_psum.at(it, 1))
                act.activation(qT[:, :, :].rearrange("p a s -> p (a s)"), ps_pair[0][:, :], ACT.Copy).then_inc(qT_ready.sem, 1)
                act.wait_ge(augT_in_psum.sem, augT_in_psum.at(it, 2))
                act.activation(kT[:, :, :].rearrange("p a s -> p (a s)"), ps_pair[1][:, :], ACT.Copy).then_inc(kT_ready.sem, 1)

            def magnitudes(it):
                for t in range(TILES):
                    act.wait_ge(side_taken.sem, side_taken.at(it, t + 1))
                    act.activation(rot_abs[:, t, :, :].rearrange("p o k -> p (o k)"), ps_wide[t][:, :], ACT.Abs).then_inc(abs_taken.sem, 1)

            def exponentials(it, heads):
                for n in heads:
                    act.wait_ge(scores_in_psum.sem, scores_in_psum.at(it, n + 1))
                    act.activation(weights[:, n, :, :].rearrange("p t s -> p (t s)"), ps_pair[n % 2][:, :], ACT.Exp).then_inc(weights_ready.sem, 1)

            def attention_out(it):
                act.wait_ge(attendedT_in_psum.sem, attendedT_in_psum.at(it, 1))
                act.activation(xT[:, :], ps_tr[:, 0:SEQ], ACT.Copy, scale=1.0 / HASHES).then_inc(attendedT_ready.sem, 1)

            def second_ffn(it):
                turned(it, 2, LN2B_S, LN2B_B)
                feed_forward(it, 1)

            def linear_attention(it):
                turned(it, 3)
                for t in range(TILES):
                    act.wait_ge(blk_kv_in_psum.sem, blk_kv_in_psum.at(it, t + 1))
                    act.activation(bkv[:, t, :], ps_wide[0][:, t * 512:t * 512 + 2 * P], ACT.Relu).then_inc(blk_kv_ready.sem, 1)
                act.wait_ge(blk_q_in_psum.sem, blk_q_in_psum.at(it, 1))
                act.activation(bqT[:, :], ps_wide[1][:, 0:SEQ], ACT.Relu, bias=bn_bias[:, 0:1]).then_inc(blk_q_ready.sem, 1)

            def linear_attention_out(it):
                act.wait_ge(blk_o_in_psum.sem, blk_o_in_psum.at(it, 1))
                act.activation(boT[:, :], ps_pair[0][:, 0:SEQ], ACT.Relu).then_inc(blk_o_ready.sem, 1)

            def softmax(it):
                act.wait_ge(shifted_ready.sem, shifted_ready.at(it, 1))
                act.activation(exps[:, :, :].rearrange("p h k -> p (h k)"), shifted[:, :, :].rearrange("p h k -> p (h k)"),
                               ACT.Exp).then_inc(exps_ready.sem, 1)

            def bend(g, it):
                act.wait_ge(dots_ready.sem, dots_ready.at(it, g + 1))
                act.activation(gelu[:, g % 2, :], dot[:, g % 2, :], ACT.Gelu_apprx_tanh).then_inc(gelu_ready.sem, 1)

            def scale_rows(g, it, rows=range(GROUP)):
                act.wait_ge(value_ready.sem, value_ready.at(it, g + 1))
                for s in rows:
                    ins = act.activation(ring[:, g % RING, s, 1, :], ring[:, g % RING, s, 1, :], ACT.Copy,
                                         scale=value[:, g % RING, s:s + 1])
                if rows[-1] == GROUP - 1:
                    ins.then_inc(scaled.sem, 1)

            def head(it, tower=True):
                if tower:
                    exponentials(it + 1, range(EARLY_HEADS, HEADS))
                scale_rows(0, it)
                bend(1, it)
                scale_rows(1, it)
                bend(2, it)
                scale_rows(2, it)
                if tower:
                    attention_out(it + 1)
                bend(3, it)
                scale_rows(3, it, range(0, 10))
                if tower:
                    second_ffn(it + 1)
                scale_rows(3, it, range(10, GROUP))
                if tower:
                    linear_attention(it + 1)
                bend(4, it)
                if tower:
                    linear_attention_out(it + 1)
                    turned(it + 1, 4)
                bend(5, it)
                scale_rows(4, it)
                scale_rows(5, it)
                if tower:
                    softmax(it + 1)

            def tail(it, tower=True, groups=True, next_one=True):
                if tower:
                    token_mix(it + 2)
                if groups:
                    bend(6, it)
                if tower:
                    normalised(it + 2)
                if groups:
                    scale_rows(6, it)
                if tower:
                    turned_heads(it + 2)
                if groups:
                    bend(7, it)
                if tower:
                    magnitudes(it + 2)
                if groups:
                    scale_rows(7, it)
                if next_one:
                    bend(0, it + 1)
                if tower:
                    exponentials(it + 2, range(0, EARLY_HEADS))

            act.wait_ge(loaded, 16 * LOADS)
            act.wait_ge(setup_scaled, 1)
            tail(-2, groups=False, next_one=False)
            exponentials(0, range(EARLY_HEADS, HEADS))
            attention_out(0)
            second_ffn(0)
            linear_attention(0)
            linear_attention_out(0)
            turned(0, 4)
            softmax(0)
            tail(-1, groups=False)
            with act.Fori(0, batches - 2) as i:
                head(i)
                tail(i)
            head(batches - 2)
            tail(batches - 2, tower=False)
            head(batches - 1, tower=False)
            tail(batches - 1, tower=False, next_one=False)

        @block.vector
        def _(dve):
            def step(ins):
                dve.drain()
                return ins

            def inverse_root(y, w, u, v):
                step(dve.tensor_scalar(y.bitcast(I32), w.bitcast(I32), -0.5, ROOT_GUESS, ALU.mult, ALU.add))
                step(dve.tensor_tensor(u, w, y, ALU.mult))
                step(dve.tensor_tensor(u, u, y, ALU.mult))
                dve.scalar_tensor_tensor(v, u, ROOT_C, u, ALU.add, ALU.mult)
                step(dve.scalar_tensor_tensor(u, u, ROOT_A, u, ALU.add, ALU.mult))
                step(dve.scalar_tensor_tensor(y, v, ROOT_D, y, ALU.add, ALU.mult))
                step(dve.scalar_tensor_tensor(y, u, ROOT_B, y, ALU.add, ALU.mult))

            dve.wait_ge(loaded, 16 * LOADS)
            n_ids = ids.shape[0]
            if n_ids < P:
                step(dve.memset(ids_f[:, :], 0.0))
            step(dve.tensor_copy(ids_f[0:n_ids, :], ids_rows[0:n_ids, :]))
            step(dve.tensor_scalar(ids_wrap[0:n_ids, :], ids_f[0:n_ids, :], 0.0, float(vocabulary), ALU.is_lt, ALU.mult))
            step(dve.tensor_tensor(ids_f[0:n_ids, :], ids_f[0:n_ids, :], ids_wrap[0:n_ids, :], ALU.add))
            dve.tensor_scalar(ids_f[0:n_ids, :], ids_f[0:n_ids, :], 0.0, float(vocabulary - 1), ALU.max, ALU.min).then_inc(ids_wrapped, 1)
            dve.memset(ones_row[:, :], 1.0)
            dve.memset(ones_bf[:, :], 1.0)
            dve.tensor_copy(cand[:, :, :], cst[:, C_CAND:C_CAND + CAND].unsqueeze(2).to_broadcast([P, CAND, ROWS]))
            dve.tensor_copy(bq3[:, :, :], vec[:, BQ:BQ + HEADS].unsqueeze(2).to_broadcast([P, HEADS, 3]))
            dve.memset(q_aug[:, :, :, :], 0.0)
            dve.memset(k_aug[:, :, :, :], 0.0)
            dve.memset(v_one[:, :, :, :], 1.0)
            dve.tensor_copy(prio[:, :], cst[:, C_PRIO:C_PRIO + ROTS])
            dve.tensor_copy(first_bias[:, :], vec[:, LN1A_B:LN1A_B + 1].to_broadcast([P, P]))
            bn = [vec[:, BN + 4 * n:BN + 4 * n + 4] for n in range(5)]
            step(dve.tensor_scalar(bn_bias[:, :], bn[4], LN_EPS, ROOT_GAIN ** 2, ALU.add, ALU.mult))
            inverse_root(bn_scale[:, :], bn_bias[:, :], bn_tmp[:, :], root_tmp[:, 0, 0:4])
            step(dve.tensor_tensor(bn_scale[:, :], bn_scale[:, :], bn[1], ALU.mult))
            step(dve.tensor_tensor(bn_tmp[:, :], bn[0], bn[3], ALU.subtract))
            step(dve.tensor_tensor(bn_tmp[:, :], bn_tmp[:, :], bn_scale[:, :], ALU.mult))
            dve.tensor_tensor(bn_bias[:, :], bn_tmp[:, :], bn[2], ALU.add)
            dve.memset(k_aug[:, :, :, DH:DH + 1], 1.0)
            step(dve.tensor_tensor(wblk_scaled[:, :, :], wblk_rows[:, :, :], bn_scale[:, :].unsqueeze(2).to_broadcast([P, 4, P]), ALU.mult))
            dve.sem_inc(setup_scaled, 1)
            dve.wait_ge(setup_psum, 1)
            dve.tensor_copy(ids_col[:, :], ps_tr[:, 0:P])
            dve.wait_ge(setup_psum, 6)
            step(dve.tensor_tensor(pos_sb[:, :, :], pos_sb[:, :, :],
                                   ps_wide[0][:, 512:512 + P].unsqueeze(1).to_broadcast([P, TILES, P]), ALU.add))
            dve.sem_inc(setup_read, 1)
            dve.wait_ge(setup_keys, 6)
            for half in range(2):
                dve.tensor_copy(key_bias_f[:, :, half, :], ps_wide[half][0:3, :].rearrange("p (n e) -> p n e", e=EXPERTS))
            dve.drain()
            for part in range(2):
                step(dve.tensor_copy(key_bias[:, :, :, :], key_bias_f))
                step(dve.scalar_tensor_tensor(key_bias_f, key_bias[:, :, :, :], cst[0:3, C_PART + part:C_PART + part + 1], key_bias_f,
                                              ALU.mult, ALU.add))
            dve.tensor_copy(key_bias[:, :, :, :], key_bias_f).then_inc(key_bias_ready, 1)

            def normalise(it, source, to):
                for t in range(TILES):
                    dve.bn_stats(stats[:, t, :], source[:, t, :])
                dve.drain()
                for t in range(TILES):
                    dve.bn_aggr(moments[:, t, :], stats[:, t, :])
                dve.drain()
                step(dve.tensor_scalar(variance[:, :], moments[:, :, 1], LN_EPS, ROOT_GAIN ** 2, ALU.add, ALU.mult))
                inverse_root(rstd[:, :], variance[:, :], root_tmp[:, 0, 0:TILES], root_tmp[:, 1, 0:TILES])
                for t in range(TILES):
                    ins = dve.tensor_scalar(to[:, t, :], source[:, t, :], moments[:, t, 0:1], rstd[:, t:t + 1], ALU.subtract, ALU.mult)
                ins.then_inc(xhat_ready.sem, 1)

            ffn_tokens = ps_wide[1][:, :].rearrange("p (t x) -> p t x", t=TILES)[:, :, 0:P]

            def psum_tokens(bank):
                return bank[:, 0:TILES * P].rearrange("p (t d) -> p t d", t=TILES)

            def ids_ahead(it):
                dve.tensor_copy(ids_now[:, :], ids_col[:, bass.ds(it * TILES, TILES)]).then_inc(ids_ready.sem, 1)

            def embed(it):
                dve.wait_ge(emb_here.sem, emb_here.at(it, 16 * TILES))
                dve.tensor_tensor(y1[:, :, :], emb_rows[:, :, :], pos_sb[:, :, :], ALU.add).then_inc(y1_made.sem, 1)
                dve.drain()
                normalise(it, y1, xhat)

            def first_ffn(it):
                dve.wait_ge(ffn_in_psum.sem, ffn_in_psum.at(it, 1))
                step(dve.tensor_tensor(y2[:, :, :], ffn_tokens, b2_all[:, 0:1, :].to_broadcast([P, TILES, P]), ALU.add))
                normalise(it, y2, xhat)

            def heads(it):
                dve.wait_ge(qkv_in_psum.sem, qkv_in_psum.at(it, 1))
                qkv = ps_wide[1][:, :].rearrange("p (t w h d) -> p t w h d", t=2 * TILES, w=2, h=HEADS)
                dve.tensor_copy(v_one[:, :, :, 0:DH], qkv[:, 0:TILES, 1, :, :])
                step(dve.tensor_copy(q_aug[:, :, :, 0:DH], qkv[:, 0:TILES, 0, :, :]))
                q = q_aug[:, :, :, 0:DH].rearrange("p t h d -> p (t h) d")
                step(dve.tensor_tensor(q_sq[:, :, :], q, q, ALU.mult))
                step(dve.tensor_reduce(norm2[:, :], q_sq[:, :, :], AX_X, ALU.add))
                inverse_root(inv_norm[:, :], norm2[:, :], root_tmp[:, 0, :], root_tmp[:, 1, :])
                step(dve.scalar_tensor_tensor(norm[:, :], norm2[:, :], 1 / ROOT_GAIN, inv_norm[:, :], ALU.mult, ALU.mult))
                step(dve.tensor_scalar(norm[:, :], norm[:, :], 1e-6, float(DH) ** 0.5, ALU.add, ALU.mult))
                step(dve.reciprocal(inv_norm[:, :], norm[:, :]))
                dve.scalar_tensor_tensor(q_aug[:, :, :, DH:DH + 1].rearrange("p t h d -> p (t h d)"), norm2[:, :], -1.0, inv_norm[:, :],
                                         ALU.mult, ALU.mult)
                dve.tensor_tensor(k_aug[:, :, :, 0:DH].rearrange("p t h d -> p (t h) d"), q,
                                  inv_norm[:, :].unsqueeze(2).to_broadcast([P, TILES * HEADS, DH]), ALU.mult).then_inc(aug_ready.sem, 1)

            def sides(it):
                for t in range(TILES):
                    dve.wait_ge(rot_in_psum.sem, rot_in_psum.at(it, t + 1))
                    for half in range(2):
                        o = slice(half * ORDERS // 2, (half + 1) * ORDERS // 2)
                        ins = dve.scalar_tensor_tensor(
                            rot_side[:, t, o, :], ps_wide[t][:, half * 512:half * 512 + 512].rearrange("p (o k) -> p o k", k=ROTS),
                            0.0, prio[:, :].unsqueeze(1).to_broadcast([P, ORDERS // 2, ROTS]), ALU.is_ge, ALU.add)
                    ins.then_inc(side_taken.sem, 1)

            def buckets(it, tiles):
                for t in tiles:
                    dve.wait_ge(abs_taken.sem, abs_taken.at(it, t + 1))
                    step(dve.tensor_reduce(rot_max[:, :], rot_abs[:, t, :, :], AX_X, ALU.max))
                    step(dve.tensor_tensor(rot_hit[:, :, :], rot_abs[:, t, :, :],
                                           rot_max[:, :].unsqueeze(2).to_broadcast([P, ORDERS, ROTS]), ALU.is_equal))
                    step(dve.tensor_tensor(rot_won[:, :, :].rearrange("p o k -> p (o k)"), rot_hit[:, :, :].rearrange("p o k -> p (o k)"),
                                           rot_side[:, t, :, :].rearrange("p o k -> p (o k)"), ALU.mult))
                    step(dve.tensor_reduce(bucket[:, :], rot_won[:, :, :], AX_X, ALU.max))
                    ins = dve.tensor_scalar(sort_key[:, t, :, :], bucket[:, :].unsqueeze(1).to_broadcast([P, 3, ORDERS]),
                                            float(-ROTS * SEQ), cst[:, C_POS + t:C_POS + t + 1], ALU.mult, ALU.add)
                if tiles[-1] == TILES - 1:
                    ins.then_inc(sort_key_ready.sem, 1)

            def thresholds(it, bits):
                keys = ps_tr[0:3 * ORDERS, 0:SEQ]
                if bits[0] == KEY_BITS - 1:
                    step(dve.memset(probe[:, :], 0.5))
                    dve.wait_ge(sort_keyT_in_psum.sem, sort_keyT_in_psum.at(it, 1))
                for bit in bits:
                    dve.scalar_tensor_tensor(below[:, :], keys, 0.5 / (1 << bit), probe[:, 0:1].to_broadcast([3 * ORDERS, SEQ]),
                                             ALU.mult, ALU.is_lt, accum_out=count[:, :])
                    step(dve.tensor_scalar(lower[:, :], probe[:, :], 2.0, -0.5 if bit else -1.0, ALU.mult, ALU.add))
                    step(dve.scalar_tensor_tensor(probe[:, :], count[:, :], cst[0:3 * ORDERS, C_RANK:C_RANK + 1], lower[:, :], ALU.is_le, ALU.add))
                if bits[-1] == 0:
                    dve.tensor_scalar(reached[:, :], keys, probe[:, 0:1], None, ALU.is_ge).then_inc(reached_ready.sem, 1)

            def chunks(it):
                dve.wait_ge(chunk_in_psum.sem, chunk_in_psum.at(it, 1))
                step(dve.tensor_tensor(own[:, :, :, :].rearrange("p t o c -> p (t o) c"),
                                       ps_tr[:, 0:TILES * ORDERS].unsqueeze(2).to_broadcast([P, TILES * ORDERS, CHUNKS]),
                                       cst[:, C_CHUNK:C_CHUNK + CHUNKS].unsqueeze(1).to_broadcast([P, TILES * ORDERS, CHUNKS]),
                                       ALU.is_equal))
                dve.tensor_tensor(seen[:, :, :, 1:CHUNKS], own[:, :, :, 1:CHUNKS], own[:, :, :, 0:CHUNKS - 1], ALU.add)
                step(dve.tensor_tensor(seen[:, :, :, 0:1], own[:, :, :, 0:1], own[:, :, :, CHUNKS - 1:CHUNKS], ALU.add))
                for four in range(2):
                    n = slice(4 * four, 4 * four + 4)
                    for t in range(TILES):
                        ins = dve.tensor_tensor(masked_v[:, t, n, :, :],
                                                v_one[:, t, n, :].unsqueeze(2).to_broadcast([P, 4, HASHES * CHUNKS, VC]),
                                                seen[:, t, HASHES * 4 * four:HASHES * 4 * (four + 1), :].rearrange("p (h r) c -> p h (r c)", h=4)
                                                .unsqueeze(3).to_broadcast([P, 4, HASHES * CHUNKS, VC]), ALU.mult)
                    ins.then_inc(masked_ready.sem, 1)

            def pick(it, head):
                dve.wait_ge(pv_in_psum.sem, pv_in_psum.at(it, head + 1))
                for t in range(TILES):
                    ins = dve.tensor_tensor(picked[:, head % 2, t, :, :], pv_bank(head, t)[:, 0:MASKED].rearrange("p (c v) -> p c v", v=VC),
                                            own[:, t, HASHES * head:HASHES * (head + 1), :].rearrange("p r c -> p (r c)").unsqueeze(2)
                                            .to_broadcast([P, HASHES * CHUNKS, VC]), ALU.mult)
                step(ins.then_inc(pv_taken.sem, 1))
                dve.tensor_reduce(hashed[:, head, :, :, :].rearrange("p t r v -> p (t r) v"),
                                  picked[:, head % 2, :, :, :].rearrange("p t (r c) v -> p (t r) v c", r=HASHES), AX_X, ALU.add)

            def attention_mean(it):
                every = hashed[:, :, :, :, :].rearrange("p h t r v -> p (h t r) v")
                step(dve.reciprocal(inv_sum[:, :], every[:, :, DH]))
                step(dve.tensor_tensor(hashed_n[:, :, :], every[:, :, 0:DH],
                                       inv_sum[:, :].unsqueeze(2).to_broadcast([P, TILES * ORDERS, DH]), ALU.mult))
                for t in range(TILES):
                    ins = dve.tensor_reduce(attended[:, t, :].rearrange("p (h d) -> p h d", h=HEADS),
                                            hashed_n[:, :, :].rearrange("p (h t r) d -> p h t d r", t=TILES, r=HASHES)[:, :, t, :, :],
                                            AX_X, ALU.add)
                ins.then_inc(attended_ready.sem, 1)

            def attention_out(it):
                dve.wait_ge(wo_in_psum.sem, wo_in_psum.at(it, 1))
                step(dve.tensor_tensor(y1[:, :, :], psum_tokens(ps_wide[1]), y1[:, :, :], ALU.add))

            def half_sums(it):
                step(dve.tensor_tensor(half_sum[:, :, :], y2[:, :, :], b2_all[:, 1:2, :].to_broadcast([P, TILES, P]), ALU.add))
                step(dve.tensor_tensor(half_sum[:, :, :], half_sum[:, :, :], y1[:, :, :], ALU.add))
                step(dve.tensor_scalar(half_sum[:, :, :], half_sum[:, :, :], 0.5, None, ALU.mult))

            def second_ffn(it):
                dve.wait_ge(ffn_in_psum.sem, ffn_in_psum.at(it, 2))
                step(dve.scalar_tensor_tensor(h[:, :, :], ffn_tokens, 0.5, half_sum[:, :, :], ALU.mult, ALU.add))

            def linear_attention(it):
                dve.wait_ge(kv_in_psum.sem, kv_in_psum.at(it, 1))
                dve.tensor_tensor(kv_diag[:, :], ps_wide[1][:, 512:512 + P], cst[:, C_DIAG:C_DIAG + P], ALU.mult).then_inc(kv_diag_ready.sem, 1)

            def linear_attention_out(it):
                dve.wait_ge(blk_p_in_psum.sem, blk_p_in_psum.at(it, 1))
                step(dve.scalar_tensor_tensor(h2[:, :, :].rearrange("p t d -> p (t d)"), ps_pair[1][:, 0:TILES * P], 0.0,
                                              h[:, :, :].rearrange("p t d -> p (t d)"), ALU.max, ALU.add))
                normalise(it, h2, z)

            def top_halves(it, pair):
                views = [halves_bank(n)[:, :].rearrange("p (t c e) -> p t c e", t=TILES, c=2) for n in (2 * pair, 2 * pair + 1)]
                for n, view in zip((2 * pair, 2 * pair + 1), views):
                    dve.wait_ge(halves_in_psum.sem, halves_in_psum.at(it, n + 1))
                    dve.sem_inc(vector_passed, 1)
                    for t in range(TILES):
                        for half in range(2):
                            dve.max(half_s[:, t, n, half, :], view[:, t, half, :])
                dve.drain()
                for n, view in zip((2 * pair, 2 * pair + 1), views):
                    for t in range(TILES):
                        for half in range(2):
                            ins = dve.max_index(half_i[:, t, n, half, :], half_s[:, t, n, half, :], view[:, t, half, :])
                ins.then_inc(halves_taken.sem, 1)

            def choose(it):
                dve.drain()
                step(dve.tensor_copy(half_f[:, :, :, :].rearrange("p n c k -> p (n c k)"),
                                     half_i[:, :, :, :, :].rearrange("p t n c k -> p (t n c k)")))
                step(dve.tensor_scalar(half_f[:, :, 0, :], half_f[:, :, 0, :], float(EXPERTS), None, ALU.mult))
                for pair, halves in ((pair_s, half_s[:, :, :, :, :].rearrange("p t n c k -> p (t n) c k")), (pair_i, half_f)):
                    a, b = halves[:, :, 0, :], halves[:, :, 1, :]
                    n = TILES * HEADS
                    dve.tensor_tensor(pair[:, :, 0:8], b[:, :, 0:8], a[:, :, 0:1].to_broadcast([P, n, 8]), ALU.add)
                    dve.tensor_tensor(pair[:, :, 8:12], b[:, :, 0:4], a[:, :, 1:2].to_broadcast([P, n, 4]), ALU.add)
                    dve.tensor_tensor(pair[:, :, 12:16].rearrange("p n (i j) -> p n i j", i=2),
                                      b[:, :, 0:2].unsqueeze(2).to_broadcast([P, n, 2, 2]),
                                      a[:, :, 2:4].unsqueeze(3).to_broadcast([P, n, 2, 2]), ALU.add)
                    dve.tensor_tensor(pair[:, :, 16:20], a[:, :, 4:8], b[:, :, 0:1].to_broadcast([P, n, 4]), ALU.add)
                dve.drain()
                for n in range(TILES * HEADS):
                    dve.max(best_s[:, n, :], pair_s[:, n, :])
                dve.drain()
                dve.tensor_tensor(shifted[:, :, :], best_s[:, :, :], best_s[:, :, 0:1].to_broadcast([P, TILES * HEADS, TOPK]),
                                  ALU.subtract).then_inc(shifted_ready.sem, 1)
                for n in range(TILES * HEADS):
                    dve.max_index(best_p[:, n, :], best_s[:, n, :], pair_s[:, n, :])
                dve.drain()
                step(dve.tensor_copy(best_bf[:, :], best_p[:, :, :].rearrange("p n k -> p (n k)")))

            def mark(t):
                n = slice(HEADS * t, HEADS * (t + 1))
                step(dve.tensor_tensor(is_choice, best_bf[:, ROWS * t:ROWS * (t + 1)].unsqueeze(1).to_broadcast([P, CAND, ROWS]),
                                       cand[:, :, :], ALU.is_equal))
                step(dve.tensor_tensor(choice.rearrange("p c (n k) -> p c n k", k=TOPK), is_choice.rearrange("p c (n k) -> p c n k", k=TOPK),
                                       pair_i[:, n, :].rearrange("p n c -> p c n").unsqueeze(3).to_broadcast([P, CAND, HEADS, TOPK]), ALU.mult))

            def sum_numbers():
                step(dve.tensor_reduce(expert[:, :], choice.rearrange("p c n -> p n c"), AX_X, ALU.add))

            def hand_over_numbers(t):
                dve.tensor_copy(x_index[:, t, :], expert[:, :]).then_inc(index_ready[t].sem, 1)

            def gate_sums(it):
                dve.wait_ge(exps_ready.sem, exps_ready.at(it, 1))
                step(dve.tensor_reduce(exp_sum[:, :], exps[:, :, :], AX_X, ALU.add))
                step(dve.reciprocal(exp_sum[:, :], exp_sum[:, :]))

            def gates(t):
                n = slice(HEADS * t, HEADS * (t + 1))
                step(dve.tensor_tensor(x_gate[:, GROUPS // TILES * t:GROUPS // TILES * (t + 1), :].rearrange("p g (n k) -> p (g n) k", k=TOPK),
                                       exps[:, n, :], exp_sum[:, n].unsqueeze(2).to_broadcast([P, HEADS, TOPK]), ALU.mult))

            def hand_over(t):
                dve.tensor_copy(x_expert[:, t, :], z[:, t, :])

            def hand_over_residual(t):
                return dve.tensor_copy(x_resid[:, t, :], h2[:, t, :])

            def dots(g, it, rows=range(GROUP)):
                t = g // (GROUPS // TILES)
                for s in rows:
                    if s % (GROUP // 2) == 0:
                        half = gathered[g][2 * s // GROUP]
                        dve.wait_ge(half.sem, half.at(it, 16 * GROUP // 2))
                    row = ring[:, g % RING, s, 0, :]
                    ins = dve.scalar_tensor_tensor(row, row, 1.0, x_expert[:, t, :], ALU.mult, ALU.mult, accum_out=dot[:, g % 2, s:s + 1])
                if rows[-1] == GROUP - 1:
                    ins.then_inc(dots_ready.sem, 1)

            def values(g, it):
                dve.wait_ge(gelu_ready.sem, gelu_ready.at(it, g + 1))
                dve.tensor_tensor(value[:, g % RING, :], gelu[:, g % 2, :], x_gate[:, g, :], ALU.mult).then_inc(value_ready.sem, 1)

            def finish(t, it):
                dve.wait_ge(mix_in_psum.sem, mix_in_psum.at(it, t + 1))
                step(dve.tensor_reduce(mix[:, :], ps_mix[:, :, :].rearrange("p n d -> p d n"), AX_X, ALU.add))
                dve.wait_ge(stored[t].sem, stored[t].at(it, 1))
                step(dve.tensor_tensor(out_rows[:, t, :], mix[:, :], x_resid[:, t, :], ALU.add))
                dve.sem_inc(out_ready.sem, 1)

            BITS_1, BITS_2, BITS_3 = range(13, 9, -1), range(9, 2, -1), range(2, -1, -1)

            first, second = range(0, GROUP // 2), range(GROUP // 2, GROUP)

            def head(it, tower=True, ids_left=True):
                if ids_left:
                    ids_ahead(it + 2)
                if tower:
                    thresholds(it + 1, BITS_2)
                values(1, it)
                if tower:
                    thresholds(it + 1, BITS_3)
                dots(2, it, first)
                if tower:
                    chunks(it + 1)
                for n in range(HEADS):
                    if tower:
                        pick(it + 1, n)
                    if n < 4:
                        dots(2, it, second[2 * n:2 * n + 2])
                    elif n == 4:
                        values(2, it)
                if tower:
                    dve.drain()
                    attention_mean(it + 1)
                dots(3, it)
                if tower:
                    attention_out(it + 1)
                values(3, it)
                if tower:
                    normalise(it + 1, y1, xhat)
                    half_sums(it + 1)
                dots(4, it)
                if tower:
                    second_ffn(it + 1)
                    normalise(it + 1, h, xhat)
                dots(5, it, range(0, 10))
                if tower:
                    linear_attention(it + 1)
                dots(5, it, range(10, GROUP))
                if tower:
                    linear_attention_out(it + 1)
                finish(0, it)
                values(4, it)
                for pair in range(HEADS // 2):
                    if tower:
                        top_halves(it + 1, pair)
                    dots(6, it, first[2 * pair:2 * pair + 2])
                    if pair == 0:
                        values(5, it)
                if tower:
                    choose(it + 1)
                    mark(0)
                    sum_numbers()
                    hand_over_numbers(0)

            def tail(it, tower=True, groups=True, next_one=True):
                if tower:
                    embed(it + 2)
                if groups:
                    dots(6, it, second)
                    dots(7, it, first)
                if next_one:
                    mark(1)
                    gate_sums(it + 1)
                if tower:
                    first_ffn(it + 2)
                if groups:
                    values(6, it)
                if next_one:
                    sum_numbers()
                    hand_over(0)
                    hand_over_residual(0)
                    gates(0)
                if tower:
                    heads(it + 2)
                if groups:
                    dots(7, it, second)
                if next_one:
                    hand_over_numbers(1)
                    dots(0, it + 1)
                if groups:
                    values(7, it)
                if tower:
                    sides(it + 2)
                if next_one:
                    dve.drain()
                    hand_over(1)
                    gates(1)
                if tower:
                    buckets(it + 2, range(TILES))
                if next_one:
                    dots(1, it + 1)
                if tower:
                    thresholds(it + 2, BITS_1)
                if groups:
                    finish(1, it)
                if next_one:
                    hand_over_residual(1)
                    values(0, it + 1)

            dve.wait_ge(setup_read, 9)
            ids_ahead(0)
            tail(-2, groups=False, next_one=False)
            ids_ahead(1)
            thresholds(0, BITS_2)
            thresholds(0, BITS_3)
            chunks(0)
            for n in range(HEADS):
                pick(0, n)
            dve.drain()
            attention_mean(0)
            attention_out(0)
            normalise(0, y1, xhat)
            half_sums(0)
            second_ffn(0)
            normalise(0, h, xhat)
            linear_attention(0)
            linear_attention_out(0)
            for pair in range(HEADS // 2):
                top_halves(0, pair)
            choose(0)
            mark(0)
            sum_numbers()
            hand_over_numbers(0)
            tail(-1, groups=False)
            with dve.Fori(0, batches - 2) as i:
                head(i)
                tail(i)
            head(batches - 2, ids_left=False)
            tail(batches - 2, tower=False)
            head(batches - 1, tower=False, ids_left=False)
            tail(batches - 1, tower=False, next_one=False)


def kernel(**inputs):
    import numpy as np
    import concourse.bacc as bacc
    from concourse import mybir as my
    from concourse.bass_utils import run_bass_kernel_spmd

    a = {k: np.asarray(v) for k, v in inputs.items()}
    t = {k[len("L0_tok_"):]: v for k, v in a.items() if k.startswith("L0_tok_")}
    b = {k[len("L0_attn_"):]: v for k, v in a.items() if k.startswith("L0_attn_")}
    f = {k[len("L0_ffn_"):]: v for k, v in a.items() if k.startswith("L0_ffn_")}
    sequences, length = a["x"].shape

    columns = [t["ln1_s"][1], t["ln1_b"][1], t["ln2_s"][0], t["ln2_b"][0], t["ln2_s"][1], t["ln2_b"][1], t["ln1_b"][0]]
    columns += list(t["b1"].reshape(2 * HID, P))
    columns += [b[f"{w}_{part}"] for part in ("b", "g", "beta", "mu", "var") for w in "qkvp"]
    columns += list(f["bq"].reshape(HEADS, P))

    const = np.zeros((P, NCONST), np.float32)
    const[:, C_ID:C_ID + P] = np.eye(P)
    const[:, C_DIAG:C_DIAG + P] = np.kron(np.eye(HEADS), np.full((DH, DH), 0.125))
    const[0:3 * ORDERS, C_SUM:C_SUM + ORDERS] = np.tile(np.eye(ORDERS), (3, 1))
    const[:, C_CHUNK:C_CHUNK + CHUNKS] = np.arange(CHUNKS)
    const[:, C_CAND:C_CAND + CAND] = np.arange(CAND)
    const[:, C_PRIO:C_PRIO + ROTS] = (ROTS - np.arange(ROTS)) / ROTS
    for tile in range(TILES):
        const[:, C_POS + tile] = 2 * ROTS * SEQ + tile * P + np.arange(P)
    const[0:3 * ORDERS, C_RANK] = 64 * (1 + np.arange(3 * ORDERS) // ORDERS)
    const[1:3, C_PART] = -1
    const[2, C_PART + 1] = -1

    arrays = {
        "ids": a["x"].reshape(sequences * TILES, P),
        "emb": t["emb"],
        "pos": t["pos"],
        "vecs": np.stack(columns, axis=1),
        "consts": const,
        "b2": t["b2"], "wqk": t["Wqk"], "wv": t["Wv"], "wo": t["Wo"], "rots": t["rots"], "w1": t["W1"], "w2": t["W2"],
        "wblk": np.stack([b[f"{w}_w"] for w in "qkvp"]),
        "wq": f["Wq"],
        "keysT": f["keys"].transpose(1, 3, 0, 2).reshape(P, HEADS * EXPERTS),
        "table": np.concatenate([f["w_down_embed"], f["w_up_embed"]], axis=1),
    }
    nc = bacc.Bacc("TRN2", target_bir_lowering=False, num_devices=1)
    arrays = {name: np.ascontiguousarray(v) for name, v in arrays.items()}
    args = [nc.dram_tensor(name, v.shape, my.dt.from_np(v.dtype), kind="ExternalInput").ap() for name, v in arrays.items()]
    out = nc.dram_tensor("out", (sequences * length, P), my.dt.float32, kind="ExternalOutput").ap()
    build(nc, *args, out)
    r = run_bass_kernel_spmd(nc, [arrays], core_ids=[0])
    return r.results[0]["out"].reshape(sequences, length, P)
```
